# Optimizing a Trainium2 kernel written in Bass

```python
import numpy as np
import jax
import jax.numpy as jnp

def _softmax(x, axis=-1):
    return jax.nn.softmax(x, axis=axis)

def _gelu(x):
    return jax.nn.gelu(x, approximate=True)

def _silu(x):
    return jax.nn.silu(x)

def _sigmoid(x):
    return jax.nn.sigmoid(x)

def _layernorm(x, axis=-1, eps=1e-05):
    m = jnp.mean(x, axis=axis, keepdims=True)
    v = jnp.var(x, axis=axis, keepdims=True)
    return (x - m) / jnp.sqrt(v + eps)

def _scatter_add(tgt, idx, src, axis=0):
    return tgt.at[idx].add(src)

def _segment_sum(src, seg, n):
    return jax.ops.segment_sum(src, seg, n)
kernel_name = 'mk_hybrid_d1_jaxref_r4_6a0e86'

def setup_inputs(seed: int=0):
    np.random.seed(seed)
    _w = jnp.asarray

    def _L0_attn_a_setup():
        import jax, jax.numpy as jnp
        import numpy as np
        B, T, C = (2, 512, 256)
        NHEADS = 16
        HEAD_DIM = C // NHEADS
        THETA = 10000.0
        SCALE_BASE = 512.0
        GN_EPS = 1e-05

        def _rotate_half(x):
            x1 = x[..., 0::2]
            x2 = x[..., 1::2]
            return jnp.stack([-x2, x1], axis=-1).reshape(x.shape)

        def _rope_xpos(q, k, T):
            d = q.shape[-1]
            half = jnp.arange(0, d, 2, dtype=jnp.float32)
            inv_freq = 1.0 / THETA ** (half / d)
            t = jnp.arange(T, dtype=jnp.float32)
            freqs = t[:, None] * inv_freq[None, :]
            freqs = jnp.repeat(freqs, 2, axis=-1)
            scale_vec = (half + 0.4 * d) / (1.4 * d)
            power = (t - T // 2) / SCALE_BASE
            scale = scale_vec[None, :] ** power[:, None]
            scale = jnp.repeat(scale, 2, axis=-1)
            cos, sin = (jnp.cos(freqs), jnp.sin(freqs))
            q = q * (cos * scale) + _rotate_half(q) * (sin * scale)
            k = k * (cos / scale) + _rotate_half(k) * (sin / scale)
            return (q, k)

        def _decay_mask(T):
            gamma = 1.0 - 2.0 ** (-5.0 - jnp.arange(NHEADS, dtype=jnp.float32))
            idx = jnp.arange(T)
            diff = idx[:, None] - idx[None, :]
            causal = diff >= 0
            expn = jnp.where(causal, diff, 0).astype(jnp.float32)
            return jnp.where(causal[None], gamma[:, None, None] ** expn[None], 0.0)
        key = jax.random.key(seed)
        ks = jax.random.split(key, 4)
        s = 0.02
        return {'x': jax.random.normal(ks[0], (B, T, C), jnp.float32), 'w_qkv': jax.random.normal(ks[1], (3 * C, C), jnp.float32) * s, 'w_gated': jax.random.normal(ks[2], (C, C), jnp.float32) * s, 'w_proj': jax.random.normal(ks[3], (C, C), jnp.float32) * s, 'gn_weight': jnp.ones((C,), jnp.float32), 'gn_bias': jnp.zeros((C,), jnp.float32)}
    _L0_attn_a_in = _L0_attn_a_setup()

    def _L0_attn_b_setup():
        import jax, jax.numpy as jnp
        import numpy as np
        B, T, C, H = (2, 256, 256, 16)
        K = C // H
        A = 32
        D = 64
        EPS = 1e-05

        def _rwkv6_forward(x, time_maa_x, time_maa_wkvrg, tm_w1, tm_w2, time_decay, td_w1, td_w2, time_faaaa, Wr, Wk, Wv, Wg, Wo, ln_w, ln_b):
            Bb, Tt, Cc = x.shape
            sx = jnp.concatenate([jnp.zeros_like(x[:, :1]), x[:, :-1]], axis=1) - x
            xxx = x + sx * time_maa_x
            m = jnp.tanh(xxx @ tm_w1).reshape(Bb, Tt, 5, A)
            delta = jnp.einsum('btfa,fac->btfc', m, tm_w2)
            mix = time_maa_wkvrg[None, None] + delta
            xw, xk, xv, xr, xg = [x + sx * mix[:, :, i] for i in range(5)]
            r = xr @ Wr
            k = xk @ Wk
            v = xv @ Wv
            g = jax.nn.silu(xg @ Wg)
            ww = time_decay + jnp.tanh(xw @ td_w1) @ td_w2
            w = jnp.exp(-jnp.exp(ww))
            tm = lambda z: z.reshape(Bb, Tt, H, K).transpose(1, 0, 2, 3)
            r_, k_, v_, w_ = (tm(r), tm(k), tm(v), tm(w))
            u = time_faaaa

            def step(state, rkvw):
                r_t, k_t, v_t, w_t = rkvw
                a = k_t[..., :, None] * v_t[..., None, :]
                y = jnp.einsum('bhk,bhkv->bhv', r_t, state + u[None, :, :, None] * a)
                new_state = w_t[..., :, None] * state + a
                return (new_state, y)
            state0 = jnp.zeros((Bb, H, K, K), x.dtype)
            _, ys = jax.lax.scan(step, state0, (r_, k_, v_, w_))
            y = ys.transpose(1, 0, 2, 3)
            mu = y.mean(-1, keepdims=True)
            var = ((y - mu) ** 2).mean(-1, keepdims=True)
            yn = (y - mu) * jax.lax.rsqrt(var + EPS)
            yn = yn * ln_w.reshape(H, K) + ln_b.reshape(H, K)
            return yn.reshape(Bb, Tt, Cc) * g @ Wo
        key = jax.random.key(seed)
        ks = jax.random.split(key, 17)
        n = lambda k, s, sc=0.02: jax.random.normal(k, s, jnp.float32) * sc
        u01 = lambda k, s: jax.random.uniform(k, s, jnp.float32)
        return {'x': jax.random.normal(ks[0], (B, T, C), jnp.float32), 'time_maa_x': u01(ks[1], (C,)), 'time_maa_wkvrg': u01(ks[2], (5, C)), 'tm_w1': n(ks[3], (C, 5 * A)), 'tm_w2': n(ks[4], (5, A, C)), 'time_decay': n(ks[5], (C,), 1.0) - 4.0, 'td_w1': n(ks[6], (C, D)), 'td_w2': n(ks[7], (D, C)), 'time_faaaa': n(ks[8], (H, K), 0.5), 'Wr': n(ks[9], (C, C)), 'Wk': n(ks[10], (C, C)), 'Wv': n(ks[11], (C, C)), 'Wg': n(ks[12], (C, C)), 'Wo': n(ks[13], (C, C)), 'ln_w': jnp.ones((C,), jnp.float32), 'ln_b': jnp.zeros((C,), jnp.float32)}
    _L0_attn_b_in = _L0_attn_b_setup()

    def _L0_ffn_setup():
        import jax, jax.numpy as jnp
        import numpy as np
        E = 8
        K = 2
        DIM = 256
        DFF = 512

        def _moe(x, Wg, bg, w1, w2):
            B, S, D = x.shape
            t = x.reshape(-1, D)
            logits = t @ Wg.T + bg
            probs = jax.nn.softmax(logits, axis=-1)
            topw, topi = jax.lax.top_k(probs, K)
            topw = topw / jnp.sum(topw, axis=-1, keepdims=True)
            combine = jnp.sum(jax.nn.one_hot(topi, E, dtype=t.dtype) * topw[..., None], axis=1)

            def body(acc, packed):
                w1e, w2e, ce = packed
                h = t @ w1e.T
                gate, up = jnp.split(h, 2, axis=-1)
                a = jax.nn.silu(gate) * up
                o = a @ w2e.T
                return (acc + ce[:, None] * o, None)
            out, _ = jax.lax.scan(body, jnp.zeros_like(t), (w1, w2, combine.T))
            return out.reshape(B, S, D)
        key = jax.random.key(seed)
        ks = jax.random.split(key, 5)
        B, S = (4, 512)
        x = jax.random.normal(ks[0], (B, S, DIM), dtype=jnp.float32)
        Wg = jax.random.normal(ks[1], (E, DIM), dtype=jnp.float32) * 0.02
        bg = jax.random.normal(ks[2], (E,), dtype=jnp.float32) * 0.02
        w1 = jax.random.normal(ks[3], (E, DFF, DIM), dtype=jnp.float32) * 0.02
        w2 = jax.random.normal(ks[4], (E, DIM, DFF // 2), dtype=jnp.float32) * 0.02
        return {'x': x, 'Wg': Wg, 'bg': bg, 'w1': w1, 'w2': w2}
    _L0_ffn_in = _L0_ffn_setup()
    _d = {'L0_attn_a_x': _L0_attn_a_in['x'], 'L0_attn_a_w_qkv': _L0_attn_a_in['w_qkv'], 'L0_attn_a_w_gated': _L0_attn_a_in['w_gated'], 'L0_attn_a_w_proj': _L0_attn_a_in['w_proj'], 'L0_attn_a_gn_weight': _L0_attn_a_in['gn_weight'], 'L0_attn_a_gn_bias': _L0_attn_a_in['gn_bias'], 'L0_attn_b_time_maa_x': _L0_attn_b_in['time_maa_x'], 'L0_attn_b_time_maa_wkvrg': _L0_attn_b_in['time_maa_wkvrg'], 'L0_attn_b_tm_w1': _L0_attn_b_in['tm_w1'], 'L0_attn_b_tm_w2': _L0_attn_b_in['tm_w2'], 'L0_attn_b_time_decay': _L0_attn_b_in['time_decay'], 'L0_attn_b_td_w1': _L0_attn_b_in['td_w1'], 'L0_attn_b_td_w2': _L0_attn_b_in['td_w2'], 'L0_attn_b_time_faaaa': _L0_attn_b_in['time_faaaa'], 'L0_attn_b_Wr': _L0_attn_b_in['Wr'], 'L0_attn_b_Wk': _L0_attn_b_in['Wk'], 'L0_attn_b_Wv': _L0_attn_b_in['Wv'], 'L0_attn_b_Wg': _L0_attn_b_in['Wg'], 'L0_attn_b_Wo': _L0_attn_b_in['Wo'], 'L0_attn_b_ln_w': _L0_attn_b_in['ln_w'], 'L0_attn_b_ln_b': _L0_attn_b_in['ln_b'], 'L0_ffn_Wg': _L0_ffn_in['Wg'], 'L0_ffn_bg': _L0_ffn_in['bg'], 'L0_ffn_w1': _L0_ffn_in['w1'], 'L0_ffn_w2': _L0_ffn_in['w2']}
    _x0 = _d['L0_attn_a_x']
    _d['L0_attn_a_x'] = jax.random.normal(jax.random.fold_in(jax.random.key(seed), 1), (4, 1024, 256), dtype=_x0.dtype)
    del _x0
    return _d

def reference(L0_attn_a_x, L0_attn_a_w_qkv, L0_attn_a_w_gated, L0_attn_a_w_proj, L0_attn_a_gn_weight, L0_attn_a_gn_bias, L0_attn_b_time_maa_x, L0_attn_b_time_maa_wkvrg, L0_attn_b_tm_w1, L0_attn_b_tm_w2, L0_attn_b_time_decay, L0_attn_b_td_w1, L0_attn_b_td_w2, L0_attn_b_time_faaaa, L0_attn_b_Wr, L0_attn_b_Wk, L0_attn_b_Wv, L0_attn_b_Wg, L0_attn_b_Wo, L0_attn_b_ln_w, L0_attn_b_ln_b, L0_ffn_Wg, L0_ffn_bg, L0_ffn_w1, L0_ffn_w2):

    def _L0_attn_a_ref(x, w_qkv, w_gated, w_proj, gn_weight, gn_bias):
        import jax, jax.numpy as jnp
        import numpy as np
        B, T, C = (2, 512, 256)
        NHEADS = 16
        HEAD_DIM = C // NHEADS
        THETA = 10000.0
        SCALE_BASE = 512.0
        GN_EPS = 1e-05

        def _rotate_half(x):
            x1 = x[..., 0::2]
            x2 = x[..., 1::2]
            return jnp.stack([-x2, x1], axis=-1).reshape(x.shape)

        def _rope_xpos(q, k, T):
            d = q.shape[-1]
            half = jnp.arange(0, d, 2, dtype=jnp.float32)
            inv_freq = 1.0 / THETA ** (half / d)
            t = jnp.arange(T, dtype=jnp.float32)
            freqs = t[:, None] * inv_freq[None, :]
            freqs = jnp.repeat(freqs, 2, axis=-1)
            scale_vec = (half + 0.4 * d) / (1.4 * d)
            power = (t - T // 2) / SCALE_BASE
            scale = scale_vec[None, :] ** power[:, None]
            scale = jnp.repeat(scale, 2, axis=-1)
            cos, sin = (jnp.cos(freqs), jnp.sin(freqs))
            q = q * (cos * scale) + _rotate_half(q) * (sin * scale)
            k = k * (cos / scale) + _rotate_half(k) * (sin / scale)
            return (q, k)

        def _decay_mask(T):
            gamma = 1.0 - 2.0 ** (-5.0 - jnp.arange(NHEADS, dtype=jnp.float32))
            idx = jnp.arange(T)
            diff = idx[:, None] - idx[None, :]
            causal = diff >= 0
            expn = jnp.where(causal, diff, 0).astype(jnp.float32)
            return jnp.where(causal[None], gamma[:, None, None] ** expn[None], 0.0)
        Bx, Tx, Cx = x.shape
        qkv = x @ w_qkv.T
        q, k, v = jnp.split(qkv, 3, axis=-1)

        def to_heads(u):
            return u.reshape(Bx, Tx, NHEADS, HEAD_DIM).transpose(0, 2, 1, 3)
        q, k, v = (to_heads(q), to_heads(k), to_heads(v))
        q, k = _rope_xpos(q, k, Tx)
        mask = _decay_mask(Tx)
        scores = jnp.einsum('bhtd,bhsd->bhts', q, k) * HEAD_DIM ** (-0.5)
        scores = scores * mask[None]
        y = jnp.einsum('bhts,bhsd->bhtd', scores, v)
        y = y.transpose(0, 2, 1, 3).reshape(Bx, Tx, Cx)
        yt = y.transpose(0, 2, 1).reshape(Bx, NHEADS, HEAD_DIM, Tx)
        mean = yt.mean(axis=(2, 3), keepdims=True)
        var = yt.var(axis=(2, 3), keepdims=True)
        yn = (yt - mean) / jnp.sqrt(var + GN_EPS)
        yn = yn.reshape(Bx, Cx, Tx)
        yn = yn * gn_weight[None, :, None] + gn_bias[None, :, None]
        yn = yn.transpose(0, 2, 1)
        out = jax.nn.silu(x @ w_gated.T) * yn
        return out @ w_proj.T

    def _L0_attn_b_ref(x, time_maa_x, time_maa_wkvrg, tm_w1, tm_w2, time_decay, td_w1, td_w2, time_faaaa, Wr, Wk, Wv, Wg, Wo, ln_w, ln_b):
        import jax, jax.numpy as jnp
        import numpy as np
        B, T, C, H = (2, 256, 256, 16)
        K = C // H
        A = 32
        D = 64
        EPS = 1e-05

        def _rwkv6_forward(x, time_maa_x, time_maa_wkvrg, tm_w1, tm_w2, time_decay, td_w1, td_w2, time_faaaa, Wr, Wk, Wv, Wg, Wo, ln_w, ln_b):
            Bb, Tt, Cc = x.shape
            sx = jnp.concatenate([jnp.zeros_like(x[:, :1]), x[:, :-1]], axis=1) - x
            xxx = x + sx * time_maa_x
            m = jnp.tanh(xxx @ tm_w1).reshape(Bb, Tt, 5, A)
            delta = jnp.einsum('btfa,fac->btfc', m, tm_w2)
            mix = time_maa_wkvrg[None, None] + delta
            xw, xk, xv, xr, xg = [x + sx * mix[:, :, i] for i in range(5)]
            r = xr @ Wr
            k = xk @ Wk
            v = xv @ Wv
            g = jax.nn.silu(xg @ Wg)
            ww = time_decay + jnp.tanh(xw @ td_w1) @ td_w2
            w = jnp.exp(-jnp.exp(ww))
            tm = lambda z: z.reshape(Bb, Tt, H, K).transpose(1, 0, 2, 3)
            r_, k_, v_, w_ = (tm(r), tm(k), tm(v), tm(w))
            u = time_faaaa

            def step(state, rkvw):
                r_t, k_t, v_t, w_t = rkvw
                a = k_t[..., :, None] * v_t[..., None, :]
                y = jnp.einsum('bhk,bhkv->bhv', r_t, state + u[None, :, :, None] * a)
                new_state = w_t[..., :, None] * state + a
                return (new_state, y)
            state0 = jnp.zeros((Bb, H, K, K), x.dtype)
            _, ys = jax.lax.scan(step, state0, (r_, k_, v_, w_))
            y = ys.transpose(1, 0, 2, 3)
            mu = y.mean(-1, keepdims=True)
            var = ((y - mu) ** 2).mean(-1, keepdims=True)
            yn = (y - mu) * jax.lax.rsqrt(var + EPS)
            yn = yn * ln_w.reshape(H, K) + ln_b.reshape(H, K)
            return yn.reshape(Bb, Tt, Cc) * g @ Wo
        return _rwkv6_forward(x, time_maa_x, time_maa_wkvrg, tm_w1, tm_w2, time_decay, td_w1, td_w2, time_faaaa, Wr, Wk, Wv, Wg, Wo, ln_w, ln_b)

    def _L0_ffn_ref(x, Wg, bg, w1, w2):
        import jax, jax.numpy as jnp
        import numpy as np
        E = 8
        K = 2
        DIM = 256
        DFF = 512

        def _moe(x, Wg, bg, w1, w2):
            B, S, D = x.shape
            t = x.reshape(-1, D)
            logits = t @ Wg.T + bg
            probs = jax.nn.softmax(logits, axis=-1)
            topw, topi = jax.lax.top_k(probs, K)
            topw = topw / jnp.sum(topw, axis=-1, keepdims=True)
            combine = jnp.sum(jax.nn.one_hot(topi, E, dtype=t.dtype) * topw[..., None], axis=1)

            def body(acc, packed):
                w1e, w2e, ce = packed
                h = t @ w1e.T
                gate, up = jnp.split(h, 2, axis=-1)
                a = jax.nn.silu(gate) * up
                o = a @ w2e.T
                return (acc + ce[:, None] * o, None)
            out, _ = jax.lax.scan(body, jnp.zeros_like(t), (w1, w2, combine.T))
            return out.reshape(B, S, D)
        return _moe(x, Wg, bg, w1, w2)
    x = L0_attn_a_x
    x = x + _L0_attn_a_ref(_layernorm(x, axis=-1), L0_attn_a_w_qkv, L0_attn_a_w_gated, L0_attn_a_w_proj, L0_attn_a_gn_weight, L0_attn_a_gn_bias)
    x = x + _L0_ffn_ref(_layernorm(x, axis=-1), L0_ffn_Wg, L0_ffn_bg, L0_ffn_w1, L0_ffn_w2)
    x = x + _L0_attn_b_ref(_layernorm(x, axis=-1), L0_attn_b_time_maa_x, L0_attn_b_time_maa_wkvrg, L0_attn_b_tm_w1, L0_attn_b_tm_w2, L0_attn_b_time_decay, L0_attn_b_td_w1, L0_attn_b_td_w2, L0_attn_b_time_faaaa, L0_attn_b_Wr, L0_attn_b_Wk, L0_attn_b_Wv, L0_attn_b_Wg, L0_attn_b_Wo, L0_attn_b_ln_w, L0_attn_b_ln_b)
    x = x + _L0_ffn_ref(_layernorm(x, axis=-1), L0_ffn_Wg, L0_ffn_bg, L0_ffn_w1, L0_ffn_w2)
    return x

_drawn_inputs = setup_inputs


def setup_inputs(seed=0):
    import zlib

    import numpy as np

    out = dict(_drawn_inputs(seed))
    spreads = {'L0_attn_a_gn_weight': (1.0, 0.6),
     'L0_attn_a_gn_bias': (0.0, 0.8),
     'L0_attn_b_ln_w': (1.0, 0.6),
     'L0_attn_b_ln_b': (0.0, 0.8)}
    factors = {'L0_attn_b_time_maa_x': 8.0,
     'L0_attn_b_tm_w1': 8.0,
     'L0_attn_b_tm_w2': 8.0,
     'L0_attn_b_td_w1': 28.823,
     'L0_attn_b_td_w2': 26.366,
     'L0_attn_b_time_faaaa': 8.0,
     'L0_ffn_Wg': 2.716,
     'L0_ffn_bg': 64.0}
    for name, (base, spread) in spreads.items():
        noise = np.random.default_rng([zlib.crc32(name.encode()), seed]).standard_normal(out[name].shape)
        drawn = base * np.exp(spread * noise) if base else spread * noise
        out[name] = jnp.asarray(drawn.astype(out[name].dtype))
    for name, factor in factors.items():
        out[name] = (out[name] * factor).astype(out[name].dtype)
    return out
```

```python
from contextlib import ExitStack

import concourse.bass as bass
from concourse import mybir

ALU = mybir.AluOpType
ACT = mybir.ActivationFunctionType
F32 = mybir.dt.float32
BF16 = mybir.dt.bfloat16
AX = mybir.AxisListType.X

P = 128
C = 256
KT = C // P
B, T = 4, 1024
TILES = B * T // P
TPB = T // P
NH, HD = 16, 16
HPT = P // HD
EPS = 1e-5
BANK = 512


def moments(dve, stats, scratch, mean, vare, step, first, n):
    even, odd = stats[:, :, 0:3], stats[:, :, 3:6]
    total, apart, squares = scratch[:, 0, :], scratch[:, 1, :], scratch[:, 2, :]
    dve.tensor_tensor(total, even[:, :, 1], odd[:, :, 1], ALU.add).then_inc(step, 1)
    dve.tensor_tensor(apart, even[:, :, 1], odd[:, :, 1], ALU.subtract).then_inc(step, 1)
    dve.tensor_tensor(squares, even[:, :, 2], odd[:, :, 2], ALU.add).then_inc(step, 1)
    dve.wait_ge(step, first + 1)
    dve.tensor_scalar(mean, total, 0.5, None, ALU.mult).then_inc(step, 1)
    dve.wait_ge(step, first + 2)
    dve.tensor_tensor(apart, apart, apart, ALU.mult).then_inc(step, 1)
    dve.wait_ge(step, first + 3)
    dve.tensor_scalar(squares, squares, 1.0 / n, EPS, ALU.mult, ALU.add).then_inc(step, 1)
    dve.wait_ge(step, first + 6)
    dve.scalar_tensor_tensor(vare, apart, 0.25, squares, ALU.mult, ALU.add).then_inc(step, 1)


MOMENT_STEPS = 7


def retention(nc, d, x, x_loaded):
    with ExitStack() as ctx:
        def sb(name, shape, dt=F32):
            return ctx.enter_context(nc.sbuf_tensor("ret_" + name, shape, dt))

        def ps(name, shape):
            return ctx.enter_context(nc.psum_tensor("ret_" + name, shape, F32))

        def sem(name):
            return ctx.enter_context(nc.semaphore("ret_" + name))

        w_qk = sb("w_qk", [P, KT, 2 * C])
        w_v = sb("w_v", [P, KT, C])
        w_gate = sb("w_gate", [P, KT, C])
        w_proj = sb("w_proj", [P, KT, C])
        rope_cos = sb("rope_cos", [P, TPB, 2 * C])
        rope_sin = sb("rope_sin", [P, TPB, 2 * C])
        ident = sb("ident", [P, P])
        causal = sb("causal", [P, P])
        head_of = sb("head_of", [P, HPT])
        same_head = sb("same_head", [P, P])
        head_mean = sb("head_mean", [P, P])
        gn_w = sb("gn_w", [P, KT])
        gn_b = sb("gn_b", [P, KT])
        expo = sb("expo", [P, TPB])
        stats = sb("stats", [P, TPB, 6])
        scratch = sb("scratch", [P, 3, TPB])
        mean = sb("mean", [P, TPB])
        vare = sb("vare", [P, TPB])
        rstd = sb("rstd", [P, TPB])
        xn = sb("xn", [P, TPB, C])
        xnt = sb("xnt", [P, KT, T])
        roped = sb("roped", [P, 2, 2 * C])
        rope_t1 = sb("rope_t1", [P, 2 * C])
        rope_t2 = sb("rope_t2", [P, 2 * C])
        v = sb("v", [P, 2, C])
        v_heads = sb("v_heads", [P, 2, NH, P])
        qkt = sb("qkt", [P, 2, 4, P])
        q_heads = sb("q_heads", [P, NH, P])
        probs = sb("probs", [P, NH, P])
        state = sb("state", [P, KT, P])
        state_add = sb("state_add", [P, KT, P])
        yt = sb("yt", [P, KT, T])
        silu_g = sb("silu_g", [P, KT, T])
        ynorm = sb("ynorm", [P, KT, T])
        gn_stats = sb("gn_stats", [P, KT, 2, 6])
        gn_sum = sb("gn_sum", [P, KT])
        gn_dev = sb("gn_dev", [P, KT, 4])
        gn_dev_sum = sb("gn_dev_sum", [P, KT])
        gn_squares = sb("gn_squares", [P, KT])
        gn_var = sb("gn_var", [P, KT])
        gn_mean = sb("gn_mean", [P, KT])
        gn_vare = sb("gn_vare", [P, KT])
        gn_rstd = sb("gn_rstd", [P, KT])
        gn_scale = sb("gn_scale", [P, KT])
        gn_shift = sb("gn_shift", [P, KT])

        score = ps("score", [P, 4, BANK])
        ps_qk = ps("ps_qk", [P, BANK])
        ps_xv = ps("ps_xv", [P, BANK])
        ps_xt, ps_v = ps_xv[:, 0:C], ps_xv[:, C:2 * C]
        ps_qkt = ps("ps_qkt", [P, BANK])
        ps_ys = ps("ps_ys", [P, BANK])
        out_banks = [ps_qkt, ps_xv]
        ps_y, ps_state = ps_ys[:, 0:C], ps_ys[:, C:2 * C]

        consts_loaded = sem("consts_loaded")
        zeroed = sem("zeroed")
        ln_stats = sem("ln_stats")
        ln_moments = sem("ln_moments")
        ln_rstd = sem("ln_rstd")
        xn_ready = sem("xn_ready")
        xt_in_psum = sem("xt_in_psum")
        xnt_ready = sem("xnt_ready")
        qk_in_psum = sem("qk_in_psum")
        v_in_psum = sem("v_in_psum")
        v_ready = sem("v_ready")
        rope_parts = sem("rope_parts")
        rope_done = sem("rope_done")
        qkt_in_psum = sem("qkt_in_psum")
        qkt_ready = sem("qkt_ready")
        q_heads_ready = sem("q_heads_ready")
        score_in_psum = sem("score_in_psum")
        probs_ready = sem("probs_ready")
        y_in_psum = sem("y_in_psum")
        yt_ready = sem("yt_ready")
        state_masked = sem("state_masked")
        state_ready = sem("state_ready")
        gate_in_psum = sem("gate_in_psum")
        gate_ready = sem("gate_ready")
        gn_half_stats = sem("gn_half_stats")
        gn_step = sem("gn_step")
        gn_sums = sem("gn_sums")
        gn_root = sem("gn_root")
        ynorm_ready = sem("ynorm_ready")
        out_in_psum = sem("out_in_psum")
        x_added = sem("x_added")

        consts = [(w_qk, "a_w_qk"), (w_v, "a_w_v"), (w_gate, "a_w_gate"), (w_proj, "a_w_proj"),
                  (rope_cos, "rope_cos"), (rope_sin, "rope_sin"), (ident, "ident"), (causal, "causal"),
                  (head_of, "head_of"), (same_head, "same_head"), (head_mean, "head_mean"),
                  (gn_w, "a_gn_w"), (gn_b, "a_gn_b")]
        HALF = T // 2
        GN_STEPS = 12

        starts_at_one = [xnt_ready, v_ready, rope_parts, qkt_ready, q_heads_ready, gate_ready, yt_ready, state_masked, state_ready]
        with nc.Block() as block:
            @block.sync
            def _(sp):
                for s in starts_at_one:
                    sp.sem_inc(s, 1)

        with nc.Block() as block:

            @block.sync
            def _(sp):
                for tile, name in consts:
                    sp.dma_start(tile[:], d[name]).then_inc(consts_loaded, 16)
                for b in range(B):
                    sp.wait_ge(x_loaded, b * 16)
                    sp.dma_start(x[:, b * TPB:(b + 1) * TPB, :], d["x"][:, b * TPB:(b + 1) * TPB, :]) \
                        .then_inc(x_loaded, 16)
                sp.wait_ge(x_loaded, 16 * B)
                sp.wait_ge(consts_loaded, 16 * len(consts))

            @block.gpsimd
            def _(pool):
                pool.memset(expo[:], -0.5).then_inc(zeroed, 1)
                pool.memset(v_heads[:], 0.0).then_inc(zeroed, 1)
                pool.wait_ge(zeroed, 2)
                with pool.Fori(0, B) as b:
                    pool.wait_ge(ln_moments, (b + 1) * MOMENT_STEPS)
                    pool.tensor_tensor(rstd[:], vare[:], expo[:], ALU.pow).then_inc(ln_rstd, 1)
                    for c in range(TPB):
                        pool.wait_ge(rope_parts, 1 + (b * TPB + (c + 1)) * 3)
                        if c >= 2:
                            pool.wait_ge(y_in_psum, b * TPB + (c - 1))
                        pool.tensor_tensor(roped[:, c % 2, :], rope_t1[:], rope_t2[:], ALU.add) \
                            .then_inc(rope_done, 1)
                        if c >= 3:
                            pool.wait_ge(state_masked, 1 + b * (TPB - 1) + (c - 1))
                            pool.tensor_tensor(state[:], state[:], state_add[:], ALU.add).then_inc(state_ready, 1)
                    pool.wait_ge(state_masked, 1 + (b + 1) * (TPB - 1))
                    pool.tensor_tensor(state[:], state[:], state_add[:], ALU.add).then_inc(state_ready, 1)
                    pool.wait_ge(gn_step, b * GN_STEPS + 9)
                    pool.tensor_tensor(gn_rstd[:], gn_vare[:], expo[:, 0:KT], ALU.pow).then_inc(gn_root, 1)

            @block.scalar
            def _(act):
                def x_transposed(b, c):
                    act.wait_ge(xt_in_psum, b * TPB + (c + 1))
                    act.activation(xnt[:, :, c * P:(c + 1) * P], ps_xt.rearrange("p (k t) -> p k t", k=KT),
                                   ACT.Copy).then_inc(xnt_ready, 1)

                def y_out(b, c):
                    act.wait_ge(y_in_psum, b * TPB + (c + 1))
                    act.activation(yt[:, :, c * P:(c + 1) * P], ps_y.rearrange("p (k t) -> p k t", k=KT),
                                   ACT.Copy).then_inc(yt_ready, 1)

                def v_out(b, c):
                    act.wait_ge(v_in_psum, b * TPB + (c + 1))
                    act.activation(v[:, c % 2, :], ps_v, ACT.Copy).then_inc(v_ready, 1)
                    for k in range(KT):
                        blocks = v_heads[:, c % 2, k * HPT:(k + 1) * HPT, :]
                        diagonal = bass.AP(blocks.tensor, blocks.offset,
                                           [blocks.ap[0], [P + HD, HPT], [1, HD]])
                        act.activation(diagonal, ps_v[:, k * P:(k + 1) * P].rearrange("p (h e) -> p h e", e=HD),
                                       ACT.Copy).then_inc(v_ready, 1)

                def qk_out(b, c):
                    act.wait_ge(qkt_in_psum, b * TPB + (c + 1))
                    act.activation(qkt[:, c % 2, :, :], ps_qkt[:].rearrange("p (j t) -> p j t", j=4),
                                   ACT.Copy).then_inc(qkt_ready, 1)

                act.wait_ge(zeroed, 2)
                with act.Fori(0, B) as b:
                    for t in range(TPB + 2):
                        if t < TPB:
                            x_transposed(b, t)
                        if t >= 2:
                            y_out(b, t - 2)
                        if t < TPB:
                            v_out(b, t)
                            qk_out(b, t)
                    act.wait_ge(gate_in_psum, b + 1)
                    act.activation(silu_g[:], score[:].rearrange("p (k n) t -> p k (n t)", k=KT),
                                   ACT.Silu).then_inc(gate_ready, 1)

            @block.tensor
            def _(pe):
                def transpose_x(b, c):
                    pe.wait_ge(xn_ready, b * TPB + (c + 1))
                    pe.wait_ge(xnt_ready, 1 + b * TPB + c)
                    pe.wait_ge(v_ready, 1 + (b * TPB + c) * 3)
                    for k in range(KT):
                        mm = pe.transpose(ps_xt[:, k * P:(k + 1) * P], xn[:, c, k * P:(k + 1) * P], ident[:])
                    mm.then_inc(xt_in_psum, 1)

                def project(b, c):
                    pe.wait_ge(xnt_ready, 1 + b * TPB + (c + 1))
                    pe.wait_ge(rope_parts, 1 + (b * TPB + c) * 3)
                    for k in range(KT):
                        mm = pe.matmul(ps_qk[:], xnt[:, k, c * P:(c + 1) * P], w_qk[:, k, :],
                                       start=(k == 0), stop=(k == KT - 1))
                    mm.then_inc(qk_in_psum, 1)
                    for k in range(KT):
                        mm = pe.matmul(ps_v, xnt[:, k, c * P:(c + 1) * P], w_v[:, k, :],
                                       start=(k == 0), stop=(k == KT - 1))
                    mm.then_inc(v_in_psum, 1)

                def transpose_qk(b, c):
                    pe.wait_ge(rope_done, b * TPB + (c + 1))
                    pe.wait_ge(qkt_ready, 1 + b * TPB + c)
                    pe.wait_ge(q_heads_ready, 1 + (b * TPB + c) * 2)
                    for j in range(4):
                        mm = pe.transpose(ps_qkt[:, j * P:(j + 1) * P], roped[:, c % 2, j * P:(j + 1) * P], ident[:])
                    mm.then_inc(qkt_in_psum, 1)

                def scores(b, c):
                    pe.wait_ge(qkt_ready, 1 + b * TPB + (c + 1))
                    for k in range(KT):
                        pe.wait_ge(q_heads_ready, 1 + (b * TPB + c) * 2 + (k + 1))
                        for n in range(2):
                            bank = 2 * k + n
                            if c == 0:
                                pe.wait_ge(gate_ready, 1 + b)
                            else:
                                pe.wait_ge(probs_ready, (b * TPB + (c - 1)) * 4 + (bank + 1))
                            pe.matmul(score[:, bank, :], qkt[:, c % 2, 2 + k, :],
                                      q_heads[:, 4 * bank:4 * bank + 4, :], start=True, stop=True) \
                                .then_inc(score_in_psum, 1)

                def outputs(b, c):
                    pe.wait_ge(yt_ready, 1 + b * TPB + c)
                    pe.wait_ge(state_masked, 1 + b * (TPB - 1) + c)
                    pe.wait_ge(v_ready, 1 + (b * TPB + (c + 1)) * 3)
                    if c >= 2:
                        pe.wait_ge(state_ready, 1 + b * (TPB - 2) + (c - 1))
                    for k in range(KT):
                        y_half = ps_y[:, k * P:(k + 1) * P]
                        if c >= 1:
                            pe.matmul(y_half, state[:, k, :], qkt[:, c % 2, k, :], start=True, stop=False)
                        for h in range(HPT):
                            head = k * HPT + h
                            if h % 4 == 0:
                                pe.wait_ge(probs_ready, (b * TPB + c) * 4 + (head // 4 + 1))
                            mm = pe.matmul(y_half, v_heads[:, c % 2, head, :], probs[:, head, :],
                                      start=(h == 0 and c == 0), stop=(h == HPT - 1))
                    for k in range(KT if c < TPB - 1 else 0):
                        mm = pe.matmul(ps_state[:, k * P:(k + 1) * P], roped[:, c % 2, C + k * P:C + (k + 1) * P],
                                       v[:, c % 2, k * P:(k + 1) * P], start=True, stop=True)
                    mm.then_inc(y_in_psum, 1)

                pe.wait_ge(consts_loaded, 16 * len(consts))
                with pe.Fori(0, B) as b:
                    for t in range(TPB + 2):
                        if t < TPB:
                            transpose_x(b, t)
                        if t >= 2:
                            outputs(b, t - 2)
                        if t < TPB:
                            project(b, t)
                        if 1 <= t <= TPB:
                            scores(b, t - 1)
                        if t < TPB:
                            transpose_qk(b, t)
                    pe.wait_ge(probs_ready, (b + 1) * TPB * 4)
                    for k in range(KT):
                        for n in range(2):
                            for kk in range(KT):
                                mm = pe.matmul(score[:, 2 * k + n, :], w_gate[:, kk, k * P:(k + 1) * P],
                                               xnt[:, kk, n * HALF:(n + 1) * HALF],
                                               start=(kk == 0), stop=(kk == KT - 1))
                    mm.then_inc(gate_in_psum, 1)
                    pe.wait_ge(gn_step, b * GN_STEPS + 1)
                    pe.matmul(ps_qk[:, 0:KT], head_mean[:], gn_sum[:], start=True, stop=True) \
                        .then_inc(gn_sums, 1)
                    pe.wait_ge(gn_step, b * GN_STEPS + 8)
                    pe.matmul(ps_qk[:, KT:2 * KT], head_mean[:], gn_var[:], start=True, stop=True) \
                        .then_inc(gn_sums, 1)
                    pe.wait_ge(ynorm_ready, (b + 1) * 4)
                    for c in range(TPB):
                        if c >= 2:
                            pe.wait_ge(x_added, b * TPB + (c - 1))
                        for k in range(KT):
                            mm = pe.matmul(out_banks[c % 2][:, 0:C], ynorm[:, k, c * P:(c + 1) * P],
                                           w_proj[:, k, :], start=(k == 0), stop=(k == KT - 1))
                        mm.then_inc(out_in_psum, 1)

            @block.vector
            def _(dve):
                def rotate(b, c):
                    dve.wait_ge(qk_in_psum, b * TPB + (c + 1))
                    if c >= 1:
                        dve.wait_ge(rope_done, b * TPB + c)
                    pairs = ps_qk[:].rearrange("p (j two) -> p j two", two=2)
                    sin = rope_sin[:, c, :].rearrange("p (j two) -> p j two", two=2)
                    t2 = rope_t2[:].rearrange("p (j two) -> p j two", two=2)
                    dve.tensor_tensor(rope_t1[:], ps_qk[:], rope_cos[:, c, :], ALU.mult).then_inc(rope_parts, 1)
                    for e in range(2):
                        dve.tensor_tensor(t2[:, :, e], pairs[:, :, 1 - e], sin[:, :, e], ALU.mult) \
                            .then_inc(rope_parts, 1)

                def mask(b, c):
                    if c >= 1:
                        dve.wait_ge(y_in_psum, b * TPB + c)
                    for bank in range(4):
                        dve.wait_ge(score_in_psum, (b * TPB + c) * 4 + (bank + 1))
                        dve.tensor_tensor(probs[:, 4 * bank:4 * bank + 4, :],
                                          score[:, bank, :].rearrange("p (h t) -> p h t", h=4),
                                          causal[:].unsqueeze(1).to_broadcast([P, 4, P]), ALU.mult) \
                            .then_inc(probs_ready, 1)

                def spread_q(b, c):
                    dve.wait_ge(qkt_ready, 1 + b * TPB + (c + 1))
                    if c >= 1:
                        dve.wait_ge(score_in_psum, (b * TPB + c) * 4)
                    for k in range(KT):
                        dve.tensor_tensor(q_heads[:, k * HPT:(k + 1) * HPT, :],
                                          qkt[:, c % 2, k, :].unsqueeze(1).to_broadcast([P, HPT, P]),
                                          head_of[:].unsqueeze(2).to_broadcast([P, HPT, P]), ALU.mult) \
                            .then_inc(q_heads_ready, 1)

                def add_state(b, c):
                    dve.wait_ge(yt_ready, 1 + b * TPB + (c + 1))
                    if c == 0:
                        dve.wait_ge(state_ready, 1 + b * (TPB - 2))
                    if c >= 2:
                        dve.wait_ge(state_ready, 1 + b * (TPB - 2) + (c - 1))
                    into = state if c == 0 else state_add
                    dve.tensor_tensor(into[:], ps_state.rearrange("p (k e) -> p k e", k=KT),
                                      same_head[:].unsqueeze(1).to_broadcast([P, KT, P]), ALU.mult) \
                        .then_inc(state_masked, 1)

                dve.wait_ge(consts_loaded, 16 * len(consts))
                with dve.Fori(0, B) as b:
                    dve.wait_ge(x_loaded, (b + 1) * 16)
                    for c in range(TPB):
                        dve.bn_stats(stats[:, c, :], x[:, b * TPB + c, :]).then_inc(ln_stats, 1)
                    dve.wait_ge(ln_stats, (b + 1) * TPB)
                    moments(dve, stats, scratch, mean[:], vare[:], ln_moments, b * MOMENT_STEPS, C)
                    dve.wait_ge(ln_rstd, b + 1)
                    for c in range(TPB):
                        dve.tensor_scalar(xn[:, c, :], x[:, b * TPB + c, :], mean[:, c:c + 1], rstd[:, c:c + 1],
                                          ALU.subtract, ALU.mult).then_inc(xn_ready, 1)
                    for t in range(TPB + 2):
                        if 2 <= t <= TPB:
                            add_state(b, t - 2)
                        if t < TPB:
                            rotate(b, t)
                        if 1 <= t <= TPB:
                            mask(b, t - 1)
                        if t < TPB:
                            spread_q(b, t)
                    dve.wait_ge(yt_ready, 1 + (b + 1) * TPB)
                    for k in range(KT):
                        for n in range(2):
                            dve.bn_stats(gn_stats[:, k, n, :], yt[:, k, n * HALF:(n + 1) * HALF]) \
                                .then_inc(gn_half_stats, 1)
                    parts = gn_stats[:].rearrange("p k n (g s) -> p k (n g) s", s=3)
                    dve.wait_ge(gn_half_stats, (b + 1) * 4)
                    dve.tensor_reduce(gn_sum[:], parts[:, :, :, 1], AX, ALU.add).then_inc(gn_step, 1)
                    dve.tensor_reduce(gn_squares[:], parts[:, :, :, 2], AX, ALU.add).then_inc(gn_step, 1)
                    dve.wait_ge(gn_sums, b * 2 + 1)
                    dve.tensor_scalar(gn_mean[:], ps_qk[:, 0:KT], 0.25, None, ALU.mult).then_inc(gn_step, 1)
                    dve.wait_ge(gn_step, b * GN_STEPS + 3)
                    dve.tensor_tensor(gn_dev[:], parts[:, :, :, 1], gn_mean[:].unsqueeze(2).to_broadcast([P, KT, 4]),
                                      ALU.subtract).then_inc(gn_step, 1)
                    dve.wait_ge(gn_step, b * GN_STEPS + 4)
                    dve.tensor_tensor(gn_dev[:], gn_dev[:], gn_dev[:], ALU.mult).then_inc(gn_step, 1)
                    dve.wait_ge(gn_step, b * GN_STEPS + 5)
                    dve.tensor_reduce(gn_dev_sum[:], gn_dev[:], AX, ALU.add).then_inc(gn_step, 1)
                    dve.tensor_scalar(gn_squares[:], gn_squares[:], 1.0 / T, None, ALU.mult).then_inc(gn_step, 1)
                    dve.wait_ge(gn_step, b * GN_STEPS + 7)
                    dve.scalar_tensor_tensor(gn_var[:], gn_dev_sum[:], 0.25, gn_squares[:], ALU.mult, ALU.add) \
                        .then_inc(gn_step, 1)
                    dve.wait_ge(gn_sums, b * 2 + 2)
                    dve.tensor_scalar(gn_vare[:], ps_qk[:, KT:2 * KT], EPS, None, ALU.add).then_inc(gn_step, 1)
                    dve.wait_ge(gn_root, b + 1)
                    dve.tensor_tensor(gn_scale[:], gn_rstd[:], gn_w[:], ALU.mult).then_inc(gn_step, 1)
                    dve.wait_ge(gn_step, b * GN_STEPS + 10)
                    dve.tensor_tensor(gn_shift[:], gn_mean[:], gn_scale[:], ALU.mult).then_inc(gn_step, 1)
                    dve.wait_ge(gn_step, b * GN_STEPS + 11)
                    dve.tensor_tensor(gn_shift[:], gn_b[:], gn_shift[:], ALU.subtract).then_inc(gn_step, 1)
                    dve.wait_ge(gn_step, b * GN_STEPS + 12)
                    for k in range(KT):
                        dve.tensor_scalar(ynorm[:, k, :], yt[:, k, :], gn_scale[:, k:k + 1], gn_shift[:, k:k + 1],
                                          ALU.mult, ALU.add).then_inc(ynorm_ready, 1)
                    dve.wait_ge(gate_ready, 1 + b + 1)
                    for k in range(KT):
                        dve.wait_ge(ynorm_ready, b * 4 + 2 + k)
                        dve.tensor_tensor(ynorm[:, k, :], ynorm[:, k, :], silu_g[:, k, :], ALU.mult) \
                            .then_inc(ynorm_ready, 1)
                    for c in range(TPB):
                        dve.wait_ge(out_in_psum, b * TPB + (c + 1))
                        dve.tensor_tensor(x[:, b * TPB + c, :], x[:, b * TPB + c, :],
                                          out_banks[c % 2][:, 0:C], ALU.add).then_inc(x_added, 1)
                dve.wait_ge(x_added, TILES)


NE = 8
FF = 256
TOPK = 2
HALVES = 2
TPH = TILES // HALVES
UNROLL = 4
RTILES = -(-(TOPK * TPH + NE - 1) // UNROLL) * UNROLL
NTILES = HALVES * RTILES
DIGIT = (NE - 1).bit_length()
LAG = 2
ROWS = RTILES * P


def experts(nc, d, x, name, x_sorted, y_sorted, clear):
    with ExitStack() as ctx:
        def sb(n, shape, dt=F32):
            return ctx.enter_context(nc.sbuf_tensor(f"{name}_{n}", shape, dt))

        def ps(n, shape):
            return ctx.enter_context(nc.psum_tensor(f"{name}_{n}", shape, F32))

        def sem(n):
            return ctx.enter_context(nc.semaphore(f"{name}_{n}"))

        w1 = sb("w1", [P, NE, KT, 2 * FF])
        w2 = sb("w2", [P, NE, KT, C])
        w_gate = sb("w_gate", [P, KT, NE])
        b_gate = sb("b_gate", [P, NE])
        ident = sb("ident", [P, P])
        tri_f = sb("tri_f", [P, P])
        tri = sb("tri", [P, P], BF16)
        ones = sb("ones", [P, P], BF16)
        ones_row = sb("ones_row", [P, TPH])
        rank_of = sb("rank_of", [P, NE])
        fills = sb("fills", [P, TPH])
        tile_no = sb("tile_no", [P, RTILES])
        expo = sb("expo", [P, TILES])
        zeros = sb("zeros", [P, 8, C])

        stats = sb("stats", [P, TILES, 6])
        scratch = sb("scratch", [P, 3, TILES])
        mean = sb("mean", [P, TILES])
        vare = sb("vare", [P, TILES])
        rstd = sb("rstd", [P, TILES])
        xn = sb("xn", [P, TILES, C])
        xn_turn = sb("xn_turn", [P, 2, UNROLL, C])
        xnt = sb("xnt", [P, 2, KT, UNROLL * P])
        logits = sb("logits", [P, TILES, NE])
        first = sb("first", [P, TILES, NE])
        second = sb("second", [P, TILES, NE])
        hits = sb("hits", [P, TILES, NE])
        rest = sb("rest", [P, TILES, NE])
        top = sb("top", [P, TOPK, TILES])
        best = sb("best", [P, TOPK, TILES])
        gap = sb("gap", [P, TILES])
        odds = sb("odds", [P, TILES])
        total = sb("total", [P, TILES])
        weight = sb("weight", [P, TOPK, TILES])
        chosen = sb("chosen", [P, TILES, NE], BF16)
        running = sb("running", [P, TILES, NE])
        slot = sb("slot", [P, TILES, NE])
        over = sb("over", [P, HALVES * NE, TPH])
        tiles_of = sb("tiles_of", [P, HALVES, NE])
        tiles_end = sb("tiles_end", [P, HALVES, NE])
        row_of = sb("row_of", [P, HALVES, NE])
        passed = sb("passed", [P, HALVES, RTILES, NE])
        expert_f = sb("expert_f", [P, LAG + NTILES])
        experts_f = sb("experts_f", [P, NTILES // UNROLL])
        experts_of = sb("experts_of", [P, NTILES // UNROLL], mybir.dt.int32)
        place_f = sb("place_f", [P, TOPK, TILES])
        place = sb("place", [P, TOPK, TILES], mybir.dt.uint32)

        xs = sb("xs", [P, UNROLL, C])
        xst = sb("xst", [P, 2, KT, P])
        silu_g = sb("silu_g", [P, 2, FF])
        act_in = sb("act_in", [P, 2, FF])
        act_t = sb("act_t", [P, 2, KT, P])
        ys = sb("ys", [P, UNROLL, C])
        back = sb("back", [P, 4, TOPK, C])

        ps_t = ps("ps_t", [P, KT, BANK])
        ps_l = ps("ps_l", [P, BANK])
        ps_h = ps("ps_h", [P, 2, BANK])
        ps_a = ps("ps_a", [P, BANK])
        ps_o = ps("ps_o", [P, 2, BANK])
        ps_xt = [ps_t, ps_h]

        weights_loaded = sem("weights_loaded")
        consts_loaded = sem("consts_loaded")
        constants_ready = sem("constants_ready")
        cleared = sem("cleared")
        ln_stats = sem("ln_stats")
        ln_moments = sem("ln_moments")
        ln_rstd = sem("ln_rstd")
        xn_ready = sem("xn_ready")
        xn_kept = sem("xn_kept")
        xt_in_psum = sem("xt_in_psum")
        xnt_ready = sem("xnt_ready")
        logits_in_psum = sem("logits_in_psum")
        logits_ready = sem("logits_ready")
        route_step = sem("route_step")
        odds_ready = sem("odds_ready")
        packing = sem("packing")
        counts_in_psum = sem("counts_in_psum")
        scattered = [sem(f"scattered{h}") for h in range(HALVES)]
        xs_loaded = [sem(f"xs_loaded{u}") for u in range(UNROLL)]
        xst_in_psum = sem("xst_in_psum")
        xst_ready = sem("xst_ready")
        h_in_psum = sem("h_in_psum")
        silu_ready = sem("silu_ready")
        act_ready = sem("act_ready")
        act_t_in_psum = sem("act_t_in_psum")
        act_t_ready = sem("act_t_ready")
        y_in_psum = sem("y_in_psum")
        ys_ready = sem("ys_ready")
        ys_stored = [sem(f"ys_stored{u}") for u in range(UNROLL)]
        gathered = [sem(f"gathered{u}") for u in range(4)]
        x_added = sem("x_added")

        weights = [(w1, "f_w1"), (w2, "f_w2")]
        consts = [(w_gate, "f_w_gate"), (b_gate, "f_b_gate"), (ident, "ident"), (tri_f, "tri"),
                  (rank_of, "rank_of"), (fills, "fills"), (tile_no, "tile_no")]
        STEPS = TILES // UNROLL
        TURNS = RTILES // UNROLL

        (TOP1, EQ1, RANK1, BEST1, FIRST, REST, TOP2, EQ2, RANK2, BEST2, SECOND, GAP, CHOSEN, SUM, SHARE, SHARE2,
         RUN, EXCL, SLOT, OVER, TILES_OF, TILES_END, ROW, SHIFT, PLACED, HIT1, POS1, HIT2, POS2, PLACE, PASSED,
         EXPERT, CLAMP, EXPERTS_OF) = range(1, 35)

        starts_at_one = [xst_ready, act_ready, act_t_ready, ys_ready, *ys_stored]
        with nc.Block() as block:
            @block.sync
            def _(sp):
                for s in starts_at_one:
                    sp.sem_inc(s, 1)

        with nc.Block() as block:

            @block.sync
            def _(sp):
                for tile, n in consts:
                    sp.dma_start(tile[:], d[n]).then_inc(consts_loaded, 16)
                for tile, n in weights:
                    sp.dma_start(tile[:], d[n]).then_inc(weights_loaded, 16)
                if clear:
                    sp.wait_ge(constants_ready, 1)
                    for half in range(HALVES):
                        for r in range(0, ROWS, 8 * P):
                            sp.dma_start(x_sorted[half][r:r + 8 * P, :].rearrange("(p i) c -> p i c", p=P), zeros[:]) \
                                .then_inc(cleared, 16)
                def load(half, tile, u):
                    rows = x_sorted[half].rearrange("(i p) c -> i p c", p=P)
                    sp.dma_start(xs[:, u, :], rows[tile]).then_inc(xs_loaded[u], 16)

                for half in range(HALVES):
                    if half == 0:
                        sp.wait_ge(scattered[half], 16 * TOPK * TPH)
                        for u in range(UNROLL):
                            load(half, u, u)
                    with sp.Fori(1 if half == 0 else 0, TURNS) as turn:
                        for u in range(UNROLL):
                            sp.wait_ge(xst_in_psum, half * RTILES - UNROLL + 1 + turn * UNROLL + u)
                            sp.wait_ge(scattered[half], 16 * TOPK * TPH)
                            load(half, turn * UNROLL + u, u)
                for u in range(UNROLL):
                    sp.wait_ge(ys_stored[u], 1 + 16 * HALVES * TURNS)
                sp.wait_ge(weights_loaded, 16 * len(weights))

            @block.gpsimd
            def _(pool):
                pool.memset(zeros[:], 0.0).then_inc(constants_ready, 1)
                pool.memset(expo[:], -0.5).then_inc(constants_ready, 1)
                pool.memset(ones[:], 1.0).then_inc(constants_ready, 1)
                pool.memset(ones_row[:], 1.0).then_inc(constants_ready, 1)
                pool.memset(expert_f[:, 0:LAG], 0.0).then_inc(constants_ready, 1)
                pool.wait_ge(ln_moments, MOMENT_STEPS)
                pool.wait_ge(constants_ready, 5)
                pool.tensor_tensor(rstd[:], vare[:], expo[:], ALU.pow).then_inc(ln_rstd, 1)
                pool.wait_ge(route_step, PLACE)
                pool.wait_ge(xn_kept, STEPS)
                if clear:
                    pool.wait_ge(cleared, 16 * HALVES * (ROWS // (8 * P)))
                for half in range(HALVES):
                    for i in range(half * TPH, (half + 1) * TPH):
                        for s in range(TOPK):
                            pool.indirect_dma_start(
                                x_sorted[half][:], bass.IndirectOffsetOnAxis(ap=place[:, s, i:i + 1], axis=0),
                                xn[:, i, :], None).then_inc(scattered[half], 16)
                for half in range(HALVES):
                    for u in range(UNROLL):
                        pool.wait_ge(ys_stored[u], 1 + 16 * TURNS * (half + 1))
                    for i in range(half * TPH, (half + 1) * TPH):
                        if i >= 4:
                            pool.wait_ge(x_added, TOPK * (i - 3))
                        for s in range(TOPK):
                            pool.indirect_dma_start(
                                back[:, i % 4, s, :], None, y_sorted[half][:],
                                bass.IndirectOffsetOnAxis(ap=place[:, s, i:i + 1], axis=0)) \
                                .then_inc(gathered[i % 4], 16)

            @block.scalar
            def _(act):
                def norm_out(turn):
                    for h in range(2):
                        n = turn * 2 + h
                        act.wait_ge(xn_ready, n + 1)
                        act.activation(xn[:, h * UNROLL:, :][:, bass.ds(turn * 2 * UNROLL, UNROLL), :], xn_turn[:, h, :, :],
                                       ACT.Copy).then_inc(xn_kept, 1)
                        act.wait_ge(xt_in_psum, n + 1)
                        if not isinstance(turn, int):
                            act.wait_ge(logits_in_psum, n - 1)
                        act.activation(xnt[:, h, :, :], ps_xt[h][:], ACT.Copy).then_inc(xnt_ready, 1)

                norm_out(0)
                with act.Fori(1, STEPS // 2) as turn:
                    norm_out(turn)
                act.wait_ge(route_step, GAP)
                act.activation(odds[:], gap[:], ACT.Exp).then_inc(odds_ready, 1)

                def x_out(n, u):
                    act.wait_ge(xst_in_psum, n + 1)
                    act.activation(xst[:, u % 2, :, :], ps_t[:, u % 2, 0:C].rearrange("p (k t) -> p k t", k=KT),
                                   ACT.Copy).then_inc(xst_ready, 1)

                def silu(n, u):
                    act.wait_ge(h_in_psum, n + 1)
                    act.activation(silu_g[:, u % 2, :], ps_h[:, u % 2, 0:FF], ACT.Silu).then_inc(silu_ready, 1)

                def y_out(n, u):
                    act.wait_ge(y_in_psum, n + 1)
                    if not (isinstance(n, int) and n < UNROLL):
                        act.wait_ge(ys_stored[u], 1 + stores_before(n, u))
                    act.activation(ys[:, u, :], ps_o[:, u % 2, 0:C], ACT.Copy).then_inc(ys_ready, 1)

                def store(n, u, half):
                    act.wait_ge(ys_ready, 1 + n + 1)
                    act.dma_start(y_sorted[half].rearrange("(i p) c -> i p c", p=P)[n - half * RTILES], ys[:, u, :]) \
                        .then_inc(ys_stored[u], 16)

                def stores_before(n, u):
                    return (n - u) * (16 // UNROLL)

                def turn_of_loop(turn, half):
                    first, last = (isinstance(turn, int) and turn == t for t in (0, HALVES * TURNS - 1))
                    for u in range(UNROLL):
                        n = turn * UNROLL + u
                        silu(n, u)
                        if not last or u + 2 < UNROLL:
                            x_out(n + 2, (u + 2) % UNROLL)
                        if not first or u >= LAG:
                            y_out(n - LAG, (u - LAG) % UNROLL)
                        if not first or u > LAG:
                            of_last_half = isinstance(turn, int) and turn == half * TURNS and u <= LAG
                            store(n - LAG - 1, (u - LAG - 1) % UNROLL, half - of_last_half)
                    if last:
                        for u in range(UNROLL - LAG - 1, UNROLL):
                            if u >= UNROLL - LAG:
                                y_out(turn * UNROLL + u, u)
                            store(turn * UNROLL + u, u, half)

                x_out(0, 0)
                x_out(1, 1)
                turn_of_loop(0, 0)
                for half in range(HALVES):
                    if half > 0:
                        turn_of_loop(half * TURNS, half)
                    last = half == HALVES - 1
                    with act.Fori(half * TURNS + 1, (half + 1) * TURNS - last) as turn:
                        turn_of_loop(turn, half)
                turn_of_loop(HALVES * TURNS - 1, HALVES - 1)

            @block.tensor
            def _(pe):
                pe.wait_ge(consts_loaded, 16 * len(consts))
                def transpose_norm(turn, h):
                    n = turn * 2 + h
                    pe.wait_ge(xn_ready, n + 1)
                    if not isinstance(turn, int):
                        pe.wait_ge(xnt_ready, n - 1)
                    for j in range(UNROLL):
                        for k in range(KT):
                            mm = pe.transpose(ps_xt[h][:, k, j * P:(j + 1) * P],
                                              xn_turn[:, h, j, k * P:(k + 1) * P], ident[:])
                    mm.then_inc(xt_in_psum, 1)

                def gate_logits(n, h):
                    pe.wait_ge(xnt_ready, n + 1)
                    for j in range(UNROLL):
                        for k in range(KT):
                            mm = pe.matmul(ps_l[:, j * NE:][:, bass.ds(n * UNROLL * NE, NE)],
                                           xnt[:, h, k, j * P:(j + 1) * P], w_gate[:, k, :],
                                           start=(k == 0), stop=(k == KT - 1))
                    mm.then_inc(logits_in_psum, 1)

                transpose_norm(0, 0)
                transpose_norm(0, 1)
                gate_logits(0, 0)
                with pe.Fori(1, STEPS // 2) as turn:
                    transpose_norm(turn, 0)
                    gate_logits(turn * 2 - 1, 1)
                    transpose_norm(turn, 1)
                    gate_logits(turn * 2, 0)
                gate_logits(STEPS - 1, 1)
                pe.wait_ge(route_step, CHOSEN)
                pe.matmul(ps_l[:, 0:TILES * NE], tri[:], chosen[:], start=True, stop=True)
                pe.matmul(ps_l[:, TILES * NE:2 * TILES * NE], ones[:], chosen[:], start=True, stop=True) \
                    .then_inc(counts_in_psum, 1)

                def transpose_x(n, u):
                    pe.wait_ge(xs_loaded[u], (n - u) * (16 // UNROLL) + 16)
                    if not (isinstance(n, int) and n < 2):
                        pe.wait_ge(xst_ready, 1 + n - 1)
                    for k in range(KT):
                        mm = pe.transpose(ps_t[:, u % 2, k * P:(k + 1) * P], xs[:, u, k * P:(k + 1) * P], ident[:])
                    mm.then_inc(xst_in_psum, 1)

                def hidden(n, u, e):
                    pe.wait_ge(xst_ready, 1 + n + 1)
                    if not (isinstance(n, int) and n < 2):
                        pe.wait_ge(act_ready, 1 + n - 1)
                    for k in range(KT):
                        mm = pe.matmul(ps_h[:, u % 2, :], xst[:, u % 2, k, :], w1[:, :, k, :][:, bass.ds(e, 1), :],
                                       start=(k == 0), stop=(k == KT - 1))
                    mm.then_inc(h_in_psum, 1)

                def transpose_act(n, u):
                    pe.wait_ge(act_ready, 1 + n + 1)
                    pe.wait_ge(act_t_ready, 1 + n)
                    for k in range(KT):
                        mm = pe.transpose(ps_a[:, k * P:(k + 1) * P], act_in[:, u % 2, k * P:(k + 1) * P], ident[:])
                    mm.then_inc(act_t_in_psum, 1)

                def output(n, u, e):
                    pe.wait_ge(act_t_ready, 1 + n + 1)
                    if not (isinstance(n, int) and n < 2):
                        pe.wait_ge(ys_ready, 1 + n - 1)
                    for k in range(KT):
                        mm = pe.matmul(ps_o[:, u % 2, 0:C], act_t[:, u % 2, k, :], w2[:, :, k, :][:, bass.ds(e, 1), :],
                                       start=(k == 0), stop=(k == KT - 1))
                    mm.then_inc(y_in_psum, 1)

                def turn_of_loop(turn):
                    first, last = (isinstance(turn, int) and turn == t for t in (0, HALVES * TURNS - 1))
                    digits = pe.value_load(experts_of[0:1, bass.ds(turn, 1)], min_val=0, max_val=NE ** (LAG + UNROLL) - 1)

                    def expert(u):
                        return pe.snap((digits >> (DIGIT * (LAG + u))) & (NE - 1), min_val=0, max_val=NE - 1)

                    for u in range(UNROLL):
                        n = turn * UNROLL + u
                        hidden(n, u, expert(u))
                        if not first or u >= 1:
                            transpose_act(n - 1, (u - 1) % UNROLL)
                        if not last or u + 2 < UNROLL:
                            transpose_x(n + 2, (u + 2) % UNROLL)
                        if not first or u >= LAG:
                            output(n - LAG, (u - LAG) % UNROLL, expert(u - LAG))
                    if last:
                        transpose_act(NTILES - 1, UNROLL - 1)
                        for u in range(UNROLL - LAG, UNROLL):
                            output(turn * UNROLL + u, u, expert(u))

                pe.wait_ge(weights_loaded, 16 * len(weights))
                pe.wait_ge(route_step, EXPERTS_OF)
                transpose_x(0, 0)
                transpose_x(1, 1)
                turn_of_loop(0)
                with pe.Fori(1, HALVES * TURNS - 1) as turn:
                    turn_of_loop(turn)
                turn_of_loop(HALVES * TURNS - 1)

            @block.vector
            def _(dve):
                def each(ap, n=NE):
                    return ap.unsqueeze(2).to_broadcast([P, TILES, n])

                ranks = rank_of[:].unsqueeze(1).to_broadcast([P, TILES, NE])
                with dve.Fori(0, STEPS) as g:
                    for j in range(UNROLL):
                        dve.bn_stats(stats[:, j:, :][:, bass.ds(g * UNROLL, 1), :], x[:, j:, :][:, bass.ds(g * UNROLL, 1), :]) \
                            .then_inc(ln_stats, 1)
                dve.wait_ge(ln_stats, TILES)
                moments(dve, stats, scratch, mean[:], vare[:], ln_moments, 0, C)
                dve.wait_ge(ln_rstd, 1)
                dve.wait_ge(consts_loaded, 16 * len(consts))
                dve.tensor_copy(tri[:], tri_f[:]).then_inc(constants_ready, 1)
                def norm(turn):
                    for h in range(2):
                        n = turn * 2 + h
                        if not isinstance(turn, int):
                            dve.wait_ge(xn_kept, n - 1)
                            dve.wait_ge(xt_in_psum, n - 1)
                        for j in range(UNROLL):
                            def tile(ap):
                                return ap[:, h * UNROLL + j:][:, bass.ds(turn * 2 * UNROLL, 1)]

                            op = dve.tensor_scalar(xn_turn[:, h, j, :], tile(x), tile(mean), tile(rstd),
                                                   ALU.subtract, ALU.mult)
                        op.then_inc(xn_ready, 1)

                norm(0)
                with dve.Fori(1, STEPS // 2) as turn:
                    norm(turn)

                def done(op):
                    op.then_inc(route_step, 1)

                dve.wait_ge(logits_in_psum, STEPS)
                dve.tensor_tensor(logits[:], ps_l[:, 0:TILES * NE].rearrange("p (i e) -> p i e", e=NE),
                                  b_gate[:].unsqueeze(1).to_broadcast([P, TILES, NE]), ALU.add).then_inc(logits_ready, 1)
                dve.wait_ge(logits_ready, 1)
                done(dve.tensor_reduce(top[:, 0, :], logits[:], AX, ALU.max))
                dve.wait_ge(route_step, TOP1)
                done(dve.tensor_tensor(hits[:], logits[:], each(top[:, 0, :]), ALU.is_equal))
                dve.wait_ge(route_step, EQ1)
                done(dve.tensor_tensor(hits[:], hits[:], ranks, ALU.mult))
                dve.wait_ge(route_step, RANK1)
                done(dve.tensor_reduce(best[:, 0, :], hits[:], AX, ALU.max))
                dve.wait_ge(route_step, BEST1)
                done(dve.tensor_tensor(first[:], ranks, each(best[:, 0, :]), ALU.is_equal))
                dve.wait_ge(route_step, FIRST)
                done(dve.scalar_tensor_tensor(rest[:], first[:], -3.0e38, logits[:], ALU.mult, ALU.add))
                dve.wait_ge(route_step, REST)
                done(dve.tensor_reduce(top[:, 1, :], rest[:], AX, ALU.max))
                dve.wait_ge(route_step, TOP2)
                done(dve.tensor_tensor(hits[:], rest[:], each(top[:, 1, :]), ALU.is_equal))
                dve.wait_ge(route_step, EQ2)
                done(dve.tensor_tensor(hits[:], hits[:], ranks, ALU.mult))
                dve.wait_ge(route_step, RANK2)
                done(dve.tensor_reduce(best[:, 1, :], hits[:], AX, ALU.max))
                dve.wait_ge(route_step, BEST2)
                done(dve.tensor_tensor(second[:], ranks, each(best[:, 1, :]), ALU.is_equal))
                done(dve.tensor_tensor(gap[:], top[:, 1, :], top[:, 0, :], ALU.subtract))
                dve.wait_ge(route_step, SECOND)
                done(dve.tensor_tensor(chosen[:], first[:], second[:], ALU.add))
                dve.wait_ge(odds_ready, 1)
                done(dve.tensor_scalar(total[:], odds[:], 1.0, None, ALU.add))
                dve.wait_ge(route_step, SUM)
                done(dve.reciprocal(weight[:, 0, :], total[:]))
                dve.wait_ge(route_step, SHARE)
                done(dve.tensor_tensor(weight[:, 1, :], weight[:, 0, :], odds[:], ALU.mult))
                dve.wait_ge(counts_in_psum, 1)
                before = ps_l[:, 0:TILES * NE].rearrange("p (i e) -> p i e", e=NE)
                counts = ps_l[:, TILES * NE:2 * TILES * NE].rearrange("p (i e) -> p i e", e=NE)
                for half in range(HALVES):
                    for e in range(NE):
                        mine = slice(half * TPH, (half + 1) * TPH)
                        op = dve.tensor_tensor_scan(running[:, mine, e], ones_row[:], counts[:, mine, e], 0.0,
                                                    ALU.mult, ALU.add)
                done(op)
                dve.wait_ge(route_step, RUN)
                done(dve.tensor_tensor(slot[:], running[:], counts, ALU.subtract))
                dve.wait_ge(route_step, EXCL)
                done(dve.tensor_tensor(slot[:], slot[:], before, ALU.add))
                for half in range(HALVES):
                    op = dve.tensor_tensor(over[:, half * NE:(half + 1) * NE, :],
                                           running[:, (half + 1) * TPH - 1, :].unsqueeze(2)
                                           .to_broadcast([P, NE, TPH]),
                                           fills[:].unsqueeze(1).to_broadcast([P, NE, TPH]), ALU.is_gt)
                done(op)
                dve.wait_ge(route_step, OVER)
                done(dve.tensor_reduce(tiles_of[:].rearrange("p h e -> p (h e)"), over[:], AX, ALU.add))
                dve.wait_ge(route_step, TILES_OF)
                for half in range(HALVES):
                    op = dve.tensor_tensor_scan(tiles_end[:, half, :], ones_row[:, 0:NE], tiles_of[:, half, :], 0.0,
                                                ALU.mult, ALU.add)
                done(op)
                dve.wait_ge(route_step, TILES_END)
                done(dve.tensor_tensor(row_of[:], tiles_end[:], tiles_of[:], ALU.subtract))
                dve.wait_ge(route_step, ROW)
                done(dve.tensor_scalar(row_of[:], row_of[:], float(P), None, ALU.mult))
                dve.wait_ge(route_step, SHIFT)
                done(dve.tensor_tensor(slot[:].rearrange("p (h i) e -> p h i e", h=HALVES),
                                       slot[:].rearrange("p (h i) e -> p h i e", h=HALVES),
                                       row_of[:].unsqueeze(2).to_broadcast([P, HALVES, TPH, NE]), ALU.add))
                dve.wait_ge(route_step, PLACED)
                done(dve.tensor_tensor(hits[:], slot[:], first[:], ALU.mult))
                dve.wait_ge(route_step, HIT1)
                done(dve.tensor_reduce(place_f[:, 0, :], hits[:], AX, ALU.add))
                dve.wait_ge(route_step, POS1)
                done(dve.tensor_tensor(hits[:], slot[:], second[:], ALU.mult))
                dve.wait_ge(route_step, HIT2)
                done(dve.tensor_reduce(place_f[:, 1, :], hits[:], AX, ALU.add))
                dve.wait_ge(route_step, POS2)
                done(dve.tensor_copy(place[:], place_f[:]))
                for half in range(HALVES):
                    op = dve.tensor_tensor(passed[:, half, :, :],
                                           tiles_end[:, half, :].unsqueeze(1).to_broadcast([P, RTILES, NE]),
                                           tile_no[:].unsqueeze(2).to_broadcast([P, RTILES, NE]), ALU.is_le)
                done(op)
                dve.wait_ge(route_step, PASSED)
                done(dve.tensor_reduce(expert_f[:, LAG:].rearrange("p (h r) -> p h r", h=HALVES), passed[:], AX, ALU.add))
                dve.wait_ge(route_step, EXPERT)
                done(dve.tensor_scalar(expert_f[:, LAG:], expert_f[:, LAG:], float(NE - 1), None, ALU.min))
                for u in reversed(range(LAG + UNROLL)):
                    digits = expert_f[:, u:u + NTILES - UNROLL + 1:UNROLL]
                    if u == LAG + UNROLL - 1:
                        dve.wait_ge(constants_ready, 6)
                        dve.wait_ge(route_step, CLAMP)
                        dve.tensor_copy(experts_f[:], digits).then_inc(packing, 1)
                    else:
                        dve.wait_ge(packing, LAG + UNROLL - 1 - u)
                        dve.scalar_tensor_tensor(experts_f[:], experts_f[:], float(NE), digits, ALU.mult, ALU.add) \
                            .then_inc(packing, 1)
                dve.wait_ge(packing, LAG + UNROLL)
                done(dve.tensor_copy(experts_of[:], experts_f[:]))

                def gate(n, u):
                    dve.wait_ge(silu_ready, n + 1)
                    dve.tensor_tensor(act_in[:, u % 2, :], silu_g[:, u % 2, :], ps_h[:, u % 2, FF:2 * FF], ALU.mult) \
                        .then_inc(act_ready, 1)

                def act_out(n, u):
                    dve.wait_ge(act_t_in_psum, n + 1)
                    dve.tensor_copy(act_t[:, u % 2, :, :], ps_a[:, 0:C].rearrange("p (k t) -> p k t", k=KT)) \
                        .then_inc(act_t_ready, 1)

                def combine(half):
                    for i in range(half * TPH, (half + 1) * TPH):
                        dve.wait_ge(gathered[i % 4], 16 * TOPK * (i // 4 + 1))
                        for s in range(TOPK):
                            dve.scalar_tensor_tensor(x[:, i, :], back[:, i % 4, s, :], weight[:, s, i:i + 1],
                                                     x[:, i, :], ALU.mult, ALU.add).then_inc(x_added, 1)
                            dve.wait_ge(x_added, TOPK * i + s + 1)

                with dve.Fori(0, HALVES * TURNS) as turn:
                    for u in range(UNROLL):
                        gate(turn * UNROLL + u, u)
                        act_out(turn * UNROLL + u, u)
                for half in range(HALVES):
                    combine(half)


NMIX = 5
LORA = 32
LORA_D = 64


def recurrence(nc, d, x, name="rec"):
    with ExitStack() as ctx:
        def sb(n, shape, dt=F32):
            return ctx.enter_context(nc.sbuf_tensor(f"{name}_{n}", shape, dt))

        def ps(n, shape):
            return ctx.enter_context(nc.psum_tensor(f"{name}_{n}", shape, F32))

        def sem(n):
            return ctx.enter_context(nc.semaphore(f"{name}_{n}"))

        ident = sb("ident", [P, P])
        v_centre = sb("v_centre", [P, P])
        v_mean = sb("v_mean", [P, P])
        k_to_v = sb("k_to_v", [P, P])
        collect = sb("collect", [P, HD, P])
        spread_f = sb("spread_f", [P, 4, P])
        spread = sb("spread", [P, 4, P], BF16)
        maa_x = sb("maa_x", [P, KT])
        maa = sb("maa", [P, NMIX, KT])
        tm_w1 = sb("tm_w1", [P, KT, NMIX * LORA])
        tm_w2 = sb("tm_w2", [P, NMIX, C])
        decay = sb("decay", [P, KT])
        td_w1 = sb("td_w1", [P, KT, LORA_D])
        td_w2 = sb("td_w2", [P, C])
        bonus = sb("bonus", [P, KT])
        w_of = {f: sb("w_" + f, [P, KT, C]) for f in "kvrgo"}
        ln_w = sb("ln_w", [P, KT])
        ln_b = sb("ln_b", [P, KT])
        expo = sb("expo", [P, TPB])
        eps = sb("eps", [P, 1])

        stats = sb("stats", [P, TPB, 6])
        scratch = sb("scratch", [P, 3, TPB])
        mean = sb("mean", [P, TPB])
        vare = sb("vare", [P, TPB])
        rstd = sb("rstd", [P, TPB])
        xn = sb("xn", [P, TPB, C])
        xnt = sb("xnt", [P, KT, T + 1])
        sx = sb("sx", [P, KT, T])
        mixed = sb("mixed", [P, 2, KT, T])
        hidden = sb("hidden", [P, T])
        hidden_g = sb("hidden_g", [P, T])
        hidden_d = sb("hidden_d", [P, T])
        wt = sb("wt", [P, KT, T])
        kt = sb("kt", [P, KT, T])
        rt = sb("rt", [P, KT, T])
        vt = sb("vt", [P, KT, T])
        silu_g = sb("silu_g", [P, KT, T])
        v_part = [sb(f"v_part{i}", [P, T], BF16) for i in range(3)]
        v_rest = sb("v_rest", [P, T])
        v_rows = sb("v_rows", [P, 4, T], BF16)
        rku = mixed[:, 0, 0, :]
        y_bonus = mixed[:, 0, 1, :]
        add = [mixed[:, 1, n, :] for n in range(2)]
        state = [sb(f"state{n}", [P, T + 1]) for n in range(2)]
        read = [sx[:, n, :] for n in range(2)]
        square = xn[:].rearrange("p i c -> p (i c)")[:, 0:T]
        root = xn[:].rearrange("p i c -> p (i c)")[:, T:2 * T]
        y_rstd = hidden[:, :]
        gated = sb("gated", [P, KT, T])

        pa = ps("pa", [P, 4, BANK])
        pb = ps("pb", [P, 4, BANK])

        loaded = sem("loaded")
        zeroed = sem("zeroed")
        constants_ready = sem("constants_ready")
        ln_stats = sem("ln_stats")
        ln_moments = sem("ln_moments")
        ln_rstd = sem("ln_rstd")
        xn_ready = sem("xn_ready")
        xt_in_psum = sem("xt_in_psum")
        xnt_ready = sem("xnt_ready")
        sx_ready = sem("sx_ready")
        mix_scaled = sem("mix_scaled")
        mix_ready = sem("mix_ready")
        hidden_in_psum = sem("hidden_in_psum")
        hidden_ready = sem("hidden_ready")
        delta_in_psum = sem("delta_in_psum")
        linear_in_psum = sem("linear_in_psum")
        linear_out = sem("linear_out")
        decay_step = sem("decay_step")
        bonus_step = sem("bonus_step")
        bonus_in_psum = sem("bonus_in_psum")
        v_split = sem("v_split")
        v_rows_loaded = sem("v_rows_loaded")
        v_in_psum = sem("v_in_psum")
        add_ready = sem("add_ready")
        state_ready = sem("state_ready")
        read_ready = sem("read_ready")
        y_in_psum = sem("y_in_psum")
        square_ready = sem("square_ready")
        var_in_psum = sem("var_in_psum")
        root_ready = sem("root_ready")
        norm_step = sem("norm_step")
        out_in_psum = sem("out_in_psum")
        x_added = sem("x_added")

        consts = [(ident[:], "ident"), (v_centre[:], "v_centre"), (v_mean[:], "v_mean"), (k_to_v[:], "k_to_v"),
                  (collect[:], "collect"), (spread_f[:], "spread"), (maa_x[:], "b_maa_x"), (maa[:], "b_maa"),
                  (tm_w1[:], "b_tm_w1"), (decay[:], "b_decay"), (td_w1[:], "b_td_w1"), (bonus[:], "b_bonus"),
                  (ln_w[:], "b_ln_w"), (ln_b[:], "b_ln_b")] + [(w_of[f][:], "b_w_" + f) for f in "kvrgo"]
        N_CONSTS = len(consts) + NMIX + 1
        FS = range(NMIX)
        W, K, V, R, G = FS

        def wide(bank):
            return bank.rearrange("p n t -> p (n t)")

        starts_at_one = [v_rows_loaded]
        with nc.Block() as block:
            @block.sync
            def _(sp):
                for s in starts_at_one:
                    sp.sem_inc(s, 1)

        with nc.Block() as block:

            @block.sync
            def _(sp):
                for tile, n in consts:
                    sp.dma_start(tile, d[n]).then_inc(loaded, 16)
                sp.wait_ge(zeroed, 2)
                for f in FS:
                    row = LORA * f % P
                    sp.dma_start(tm_w2[row:row + LORA, f, :], d["b_tm_w2"][LORA * f:LORA * (f + 1), :]) \
                        .then_inc(loaded, 16)
                sp.dma_start(td_w2[0:LORA_D, :], d["b_td_w2"]).then_inc(loaded, 16)
                sp.wait_ge(zeroed, 3)
                with sp.Fori(0, B) as b:
                    for k in range(KT):
                        sp.wait_ge(v_split, b * 10 + 5 * (k + 1))
                        for part in range(3):
                            for g in range(4):
                                sp.dma_start(v_rows[32 * part:32 * part + 32, g, :],
                                             v_part[part][32 * g:32 * g + 32, :]).then_inc(v_rows_loaded, 16)
                sp.wait_ge(v_rows_loaded, 1 + 16 * 12 * KT * B)

            @block.gpsimd
            def _(pool):
                pool.memset(tm_w2[:], 0.0).then_inc(zeroed, 1)
                pool.memset(td_w2[:], 0.0).then_inc(zeroed, 1)
                pool.memset(v_rows[:], 0.0).then_inc(zeroed, 1)
                pool.memset(expo[:], -0.5).then_inc(zeroed, 1)
                pool.memset(hidden_g[:], 0.0).then_inc(zeroed, 1)
                pool.memset(hidden_d[:], 0.0).then_inc(zeroed, 1)
                pool.memset(xnt[:, :, 0:1], 0.0).then_inc(zeroed, 1)
                for n in range(2):
                    pool.memset(state[n][:, 0:1], 0.0).then_inc(zeroed, 1)
                pool.memset(eps[:], EPS).then_inc(zeroed, 1)
                pool.wait_ge(zeroed, 10)
                with pool.Fori(0, B) as b:
                    pool.wait_ge(ln_moments, (b + 1) * MOMENT_STEPS)
                    pool.tensor_tensor(rstd[:], vare[:], expo[:], ALU.pow).then_inc(ln_rstd, 1)
                    for f in FS:
                        for k in range(KT):
                            pool.wait_ge(mix_scaled, b * 2 * NMIX + f * KT + k + 1)
                            pool.tensor_tensor(mixed[:, f % 2, k, :], mixed[:, f % 2, k, :], xnt[:, k, 1:T + 1],
                                               ALU.add).then_inc(mix_ready, 1)
                    for k in range(KT):
                        for j in range(HD):
                            n = k * HD + j
                            pool.wait_ge(state_ready, b * 2 * HD + n + 1)
                            if n >= 2:
                                pool.wait_ge(y_in_psum, b * 2 * HD + n - 1)
                            pool.tensor_tensor(read[n % 2], rt[:, k, :], state[n % 2][:, 0:T], ALU.mult) \
                                .then_inc(read_ready, 1)

            @block.scalar
            def _(act):
                act.wait_ge(loaded, 16 * N_CONSTS)
                act.activation(spread[:], spread_f[:], ACT.Copy).then_inc(constants_ready, 1)
                act.wait_ge(zeroed, 10)
                with act.Fori(0, B) as b:
                    for c in range(TPB):
                        act.wait_ge(xt_in_psum, b * TPB + c + 1)
                        act.activation(xnt[:, :, 1 + c * P:1 + (c + 1) * P],
                                       pa[:, c % 4, 0:C].rearrange("p (k t) -> p k t", k=KT), ACT.Copy) \
                            .then_inc(xnt_ready, 1)
                    act.wait_ge(hidden_in_psum, b * 2 + 1)
                    act.activation(hidden[:], wide(pb[:, 0:2, :]), ACT.Tanh).then_inc(hidden_ready, 1)
                    act.wait_ge(hidden_in_psum, b * 2 + 2)
                    act.activation(hidden_g[0:LORA, :], wide(pb[0:LORA, 2:4, :]), ACT.Tanh).then_inc(hidden_ready, 1)
                    act.wait_ge(linear_in_psum, b * 6 + 1)
                    act.activation(hidden_d[0:LORA_D, :], wide(pb[0:LORA_D, 0:2, :]), ACT.Tanh).then_inc(linear_out, 1)
                    act.wait_ge(linear_in_psum, b * 6 + 2)
                    for k in range(KT):
                        act.activation(wt[:, k, :], wide(pb[:, 2 * k:2 * k + 2, :]), ACT.Exp, bias=decay[:, k:k + 1]) \
                            .then_inc(decay_step, 1)
                    act.wait_ge(decay_step, b * 3 + 2)
                    act.activation(wt[:], wt[:], ACT.Exp, scale=-1.0).then_inc(decay_step, 1)
                    act.wait_ge(linear_in_psum, b * 6 + 3)
                    act.activation(kt[:], pb[:].rearrange("p (k n) t -> p k (n t)", k=KT), ACT.Copy) \
                        .then_inc(linear_out, 1)
                    act.wait_ge(linear_in_psum, b * 6 + 4)
                    act.activation(vt[:], pb[:].rearrange("p (k n) t -> p k (n t)", k=KT), ACT.Copy) \
                        .then_inc(linear_out, 1)
                    act.wait_ge(linear_in_psum, b * 6 + 5)
                    act.activation(rt[:], pb[:].rearrange("p (k n) t -> p k (n t)", k=KT), ACT.Copy) \
                        .then_inc(linear_out, 1)
                    act.wait_ge(linear_in_psum, b * 6 + 6)
                    act.activation(silu_g[:], pb[:].rearrange("p (k n) t -> p k (n t)", k=KT), ACT.Silu) \
                        .then_inc(linear_out, 1)
                    for k in range(KT):
                        act.wait_ge(v_rows_loaded, 1 + (b * KT + k) * 12 * 16)
                        act.wait_ge(linear_out, b * 5 + 3)
                        act.activation(v_part[0][:], vt[:, k, :], ACT.Copy).then_inc(v_split, 1)
                        act.wait_ge(v_split, b * 10 + 5 * k + 2)
                        act.activation(v_part[1][:], v_rest[:], ACT.Copy).then_inc(v_split, 1)
                        act.wait_ge(v_split, b * 10 + 5 * k + 4)
                        act.activation(v_part[2][:], v_rest[:], ACT.Copy).then_inc(v_split, 1)
                        act.wait_ge(y_in_psum, (b * KT + k + 1) * HD)
                        act.activation(square, wide(pb[:, 2 * k:2 * k + 2, :]), ACT.Square).then_inc(square_ready, 1)
                        act.wait_ge(var_in_psum, b * KT + k + 1)
                        act.activation(root, wide(pa[:, 0:2, :]), ACT.Sqrt, bias=eps[:]).then_inc(root_ready, 1)

            @block.tensor
            def _(pe):
                pe.wait_ge(loaded, 16 * N_CONSTS)
                pe.wait_ge(constants_ready, 1)
                pe.wait_ge(zeroed, 10)

                def linear(w, src):
                    outs = w.shape[2]
                    for m in range(0, outs, P):
                        for n in range(2):
                            for k in range(KT):
                                mm = pe.matmul(pb[0:min(P, outs), 2 * (m // P) + n, :], w[:, k, m:m + min(P, outs)],
                                               src[:, k, n * BANK:(n + 1) * BANK], start=(k == 0), stop=(k == KT - 1))
                    return mm

                with pe.Fori(0, B) as b:
                    for c in range(TPB):
                        pe.wait_ge(xn_ready, b * TPB + c + 1)
                        if c >= 4:
                            pe.wait_ge(xnt_ready, b * TPB + c - 3)
                        for k in range(KT):
                            mm = pe.transpose(pa[:, c % 4, k * P:(k + 1) * P], xn[:, c, k * P:(k + 1) * P], ident[:])
                        mm.then_inc(xt_in_psum, 1)
                    pe.wait_ge(sx_ready, b * 4 + 4)
                    for n in range(2):
                        for k in range(KT):
                            mm = pe.matmul(pb[:, n, :], tm_w1[:, k, 0:P], mixed[:, 0, k, n * BANK:(n + 1) * BANK],
                                           start=(k == 0), stop=(k == KT - 1))
                    mm.then_inc(hidden_in_psum, 1)
                    for n in range(2):
                        for k in range(KT):
                            mm = pe.matmul(pb[0:LORA, 2 + n, :], tm_w1[:, k, P:P + LORA],
                                           mixed[:, 0, k, n * BANK:(n + 1) * BANK],
                                           start=(k == 0), stop=(k == KT - 1))
                    mm.then_inc(hidden_in_psum, 1)

                    def delta(f):
                        for k in range(KT):
                            if f >= 1:
                                pe.wait_ge(mix_scaled, b * 2 * NMIX + (f - 1) * KT + k + 1)
                            for n in range(2):
                                mm = pe.matmul(pa[:, 2 * k + n, :], tm_w2[:, f, k * P:(k + 1) * P],
                                               (hidden if f < 4 else hidden_g)[:, n * BANK:(n + 1) * BANK],
                                               start=True, stop=True)
                            mm.then_inc(delta_in_psum, 1)

                    pe.wait_ge(hidden_ready, b * 2 + 2)
                    pe.wait_ge(xnt_ready, (b + 1) * TPB)
                    delta(W)
                    delta(K)
                    pe.wait_ge(mix_ready, b * 2 * NMIX + 2 * (W + 1))
                    linear(td_w1, mixed[:, W % 2]).then_inc(linear_in_psum, 1)
                    delta(V)
                    pe.wait_ge(linear_out, b * 5 + 1)
                    for k in range(KT):
                        for n in range(2):
                            mm = pe.matmul(pb[:, 2 * k + n, :], td_w2[:, k * P:(k + 1) * P],
                                           hidden_d[:, n * BANK:(n + 1) * BANK], start=True, stop=True)
                    mm.then_inc(linear_in_psum, 1)
                    for f, w in ((K, "k"), (V, "v"), (R, "r"), (G, "g")):
                        pe.wait_ge(mix_ready, b * 2 * NMIX + 2 * (f + 1))
                        if f == K:
                            pe.wait_ge(decay_step, b * 3 + 2)
                        else:
                            pe.wait_ge(linear_out, b * 5 + f)
                        linear(w_of[w], mixed[:, f % 2]).then_inc(linear_in_psum, 1)
                        if f + 2 < NMIX:
                            delta(f + 2)

                    for k in range(KT):
                        pe.wait_ge(bonus_step, b * 4 + 2 * k + 1)
                        if k >= 1:
                            pe.wait_ge(norm_step, b * 8 + 4 * k)
                        for n in range(2):
                            mm = pe.matmul(pa[:, n, :], k_to_v[:], rku[:, n * BANK:(n + 1) * BANK], start=True, stop=True)
                        mm.then_inc(bonus_in_psum, 1)
                        pe.wait_ge(linear_out, (b + 1) * 5)
                        pe.wait_ge(bonus_step, b * 4 + 2 * k + 2)
                        for n in range(2):
                            pe.matmul(pb[:, 2 * k + n, :], v_centre[:], y_bonus[:, n * BANK:(n + 1) * BANK],
                                      start=True, stop=False)

                        def spread_v(j):
                            m = k * HD + j
                            if j >= 2:
                                pe.wait_ge(add_ready, b * 2 * HD + m - 1)
                            for n in range(2):
                                mm = pe.matmul(pa[:, 2 * (j % 2) + n, :], spread[:, j % 4, :],
                                               v_rows[:, j // 4, n * BANK:(n + 1) * BANK], start=True, stop=True)
                            mm.then_inc(v_in_psum, 1)

                        pe.wait_ge(v_rows_loaded, 1 + (b * KT + k + 1) * 12 * 16)
                        spread_v(0)
                        spread_v(1)
                        for j in range(HD):
                            m = k * HD + j
                            if j + 2 < HD:
                                spread_v(j + 2)
                            pe.wait_ge(read_ready, b * 2 * HD + m + 1)
                            for n in range(2):
                                mm = pe.matmul(pb[:, 2 * k + n, :], collect[:, j, :], read[m % 2][:, n * BANK:(n + 1) * BANK],
                                               start=False, stop=(j == HD - 1))
                            mm.then_inc(y_in_psum, 1)
                        pe.wait_ge(square_ready, b * KT + k + 1)
                        for n in range(2):
                            mm = pe.matmul(pa[:, n, :], v_mean[:], square[:, n * BANK:(n + 1) * BANK], start=True, stop=True)
                        mm.then_inc(var_in_psum, 1)
                    pe.wait_ge(norm_step, (b + 1) * 8)
                    for c in range(TPB):
                        if c >= 2:
                            pe.wait_ge(x_added, b * TPB + c - 1)
                        for k in range(KT):
                            mm = pe.matmul(pa[:, 2 + c % 2, 0:C], gated[:, k, c * P:(c + 1) * P], w_of["o"][:, k, :],
                                           start=(k == 0), stop=(k == KT - 1))
                        mm.then_inc(out_in_psum, 1)

            @block.vector
            def _(dve):
                dve.wait_ge(loaded, 16 * N_CONSTS)
                dve.wait_ge(zeroed, 10)
                with dve.Fori(0, B) as b:
                    for c in range(TPB):
                        dve.bn_stats(stats[:, c, :], x[:, b * TPB + c, :]).then_inc(ln_stats, 1)
                    dve.wait_ge(ln_stats, (b + 1) * TPB)
                    moments(dve, stats, scratch, mean[:], vare[:], ln_moments, b * MOMENT_STEPS, C)
                    dve.wait_ge(ln_rstd, b + 1)
                    for c in range(TPB):
                        dve.tensor_scalar(xn[:, c, :], x[:, b * TPB + c, :], mean[:, c:c + 1], rstd[:, c:c + 1],
                                          ALU.subtract, ALU.mult).then_inc(xn_ready, 1)
                    dve.wait_ge(xnt_ready, (b + 1) * TPB)
                    for k in range(KT):
                        dve.tensor_tensor(sx[:, k, :], xnt[:, k, 0:T], xnt[:, k, 1:T + 1], ALU.subtract) \
                            .then_inc(sx_ready, 1)
                    for k in range(KT):
                        dve.wait_ge(sx_ready, b * 4 + k + 1)
                        dve.scalar_tensor_tensor(mixed[:, 0, k, :], sx[:, k, :], maa_x[:, k:k + 1], xnt[:, k, 1:T + 1],
                                                 ALU.mult, ALU.add).then_inc(sx_ready, 1)
                    for f in FS:
                        if f >= 2:
                            dve.wait_ge(linear_in_psum, b * 6 + (1 if f == 2 else f))
                        for k in range(KT):
                            dve.wait_ge(delta_in_psum, b * 2 * NMIX + f * KT + k + 1)
                            dve.scalar_tensor_tensor(mixed[:, f % 2, k, :], wide(pa[:, 2 * k:2 * k + 2, :]),
                                                     maa[:, f, k:k + 1], sx[:, k, :], ALU.add, ALU.mult) \
                                .then_inc(mix_scaled, 1)

                    dve.wait_ge(linear_in_psum, b * 6 + 6)
                    dve.wait_ge(linear_out, b * 5 + 4)
                    dve.wait_ge(decay_step, (b + 1) * 3)
                    for k in range(KT):
                        dve.scalar_tensor_tensor(rku, rt[:, k, :], bonus[:, k:k + 1], kt[:, k, :], ALU.mult, ALU.mult) \
                            .then_inc(bonus_step, 1)
                        dve.wait_ge(v_split, b * 10 + 5 * k + 1)
                        dve.tensor_tensor(v_rest[:], vt[:, k, :], v_part[0][:], ALU.subtract).then_inc(v_split, 1)
                        dve.wait_ge(v_split, b * 10 + 5 * k + 3)
                        dve.tensor_tensor(v_rest[:], v_rest[:], v_part[1][:], ALU.subtract).then_inc(v_split, 1)
                        dve.wait_ge(bonus_in_psum, b * KT + k + 1)
                        dve.tensor_tensor(y_bonus, wide(pa[:, 0:2, :]), vt[:, k, :], ALU.mult).then_inc(bonus_step, 1)
                        for j in range(HD):
                            m = k * HD + j
                            dve.wait_ge(v_in_psum, b * 2 * HD + m + 1)
                            dve.tensor_tensor(add[m % 2], wide(pa[:, 2 * (j % 2):2 * (j % 2) + 2, :]), kt[:, k, :],
                                              ALU.mult).then_inc(add_ready, 1)
                            dve.wait_ge(add_ready, b * 2 * HD + m + 1)
                            if m >= 2:
                                dve.wait_ge(read_ready, b * 2 * HD + m - 1)
                            dve.tensor_tensor_scan(state[m % 2][:, 1:T + 1], wt[:, k, :], add[m % 2], 0.0,
                                                   ALU.mult, ALU.add).then_inc(state_ready, 1)
                        dve.wait_ge(root_ready, b * KT + k + 1)
                        dve.reciprocal(y_rstd, root).then_inc(norm_step, 1)
                        dve.wait_ge(norm_step, b * 8 + 4 * k + 1)
                        dve.tensor_tensor(gated[:, k, :], wide(pb[:, 2 * k:2 * k + 2, :]), y_rstd, ALU.mult) \
                            .then_inc(norm_step, 1)
                        dve.wait_ge(norm_step, b * 8 + 4 * k + 2)
                        dve.tensor_scalar(gated[:, k, :], gated[:, k, :], ln_w[:, k:k + 1], ln_b[:, k:k + 1],
                                          ALU.mult, ALU.add).then_inc(norm_step, 1)
                        dve.wait_ge(norm_step, b * 8 + 4 * k + 3)
                        dve.wait_ge(linear_out, (b + 1) * 5)
                        dve.tensor_tensor(gated[:, k, :], gated[:, k, :], silu_g[:, k, :], ALU.mult) \
                            .then_inc(norm_step, 1)
                    for c in range(TPB):
                        dve.wait_ge(out_in_psum, b * TPB + (c + 1))
                        dve.tensor_tensor(x[:, b * TPB + c, :], x[:, b * TPB + c, :], pa[:, 2 + c % 2, 0:C], ALU.add) \
                            .then_inc(x_added, 1)
                dve.wait_ge(x_added, TILES)


def _shape_constants():
    import numpy as np
    f = np.float32
    half = np.arange(0, HD, 2, dtype=f)
    inv_freq = (f(1.0) / f(10000.0) ** (half / f(HD))).astype(f)
    t = np.arange(T, dtype=f)
    freqs = np.repeat((t[:, None] * inv_freq[None, :]).astype(f), 2, axis=1)
    scale_vec = (half + f(0.4 * HD)) / f(1.4 * HD)
    power = (t - T // 2) / f(512.0)
    scale = np.repeat(scale_vec[None, :].astype(np.float64) ** power[:, None], 2, axis=1)
    cos, sin = np.cos(freqs).astype(np.float64), np.sin(freqs).astype(np.float64)
    sin[:, 0::2] *= -1.0
    gamma = (f(1.0) - f(2.0) ** (f(-5.0) - np.arange(NH, dtype=f))).astype(np.float64)
    decay = gamma[None, :, None] ** np.arange(T, dtype=np.float64)[:, None, None]
    both = []
    for wave in (cos, sin):
        q = decay * (wave * scale)[:, None, :] * HD ** -0.5
        k = (wave / scale)[:, None, :] / decay
        table = np.concatenate([q.reshape(T, C), k.reshape(T, C)], axis=1)
        both.append(np.ascontiguousarray(table.reshape(TPB, P, 2 * C).transpose(1, 0, 2)).astype(f))
    i = np.arange(P)
    head = i // HD
    same = (head[:, None] == head[None, :]).astype(f)
    vrow_v, vrow_h = i // HPT, i % HPT
    vsame = (vrow_h[:, None] == vrow_h[None, :]).astype(f)
    k_to_v = (head[:, None] == vrow_h[None, :]).astype(f)
    pick = (vrow_v[None, :] == np.arange(HD)[:, None]).astype(f)
    collect = (k_to_v[:, None, :] * (pick[None, :, :] - f(1.0 / HD))).astype(f)
    spread = np.zeros((P, 4, P), f)
    for part in range(3):
        for jj in range(4):
            for h in range(HPT):
                spread[part * 32 + jj * HPT + h, jj, h * HD:(h + 1) * HD] = 1.0
    tri = (i[:, None] < i[None, :]).astype(f)
    return {
        "rope_cos": both[0], "rope_sin": both[1], "ident": np.eye(P, dtype=f),
        "causal": (i[None, :] >= i[:, None]).astype(f),
        "head_of": (head[:, None] == np.arange(HPT)[None, :]).astype(f),
        "same_head": same, "head_mean": (same / f(HD)).astype(f),
        "v_centre": (vsame * (np.eye(P, dtype=f) * 0 + (vrow_v[:, None] == vrow_v[None, :]) - f(1.0 / HD))).astype(f),
        "v_mean": (vsame / f(HD)).astype(f), "k_to_v": k_to_v, "collect": collect, "spread": spread,
        "tri": tri, "ones": np.ones((P, P), f),
    }


def _laid_out(i):
    import numpy as np
    i = {k: np.asarray(v) for k, v in i.items()}

    def rows(w):
        return w.reshape(-1, P, w.shape[1]).transpose(1, 0, 2)

    def column(w):
        return w.reshape(-1, P).T

    def by_value(w, axis):
        s = w.shape
        w = w.reshape(*s[:axis], KT, HPT, HD, *s[axis + 1:])
        return np.swapaxes(w, axis + 1, axis + 2).reshape(s)

    w_qkv = i["L0_attn_a_w_qkv"]
    b = {k.removeprefix("L0_attn_b_"): v for k, v in i.items() if k.startswith("L0_attn_b_")}
    w1, w2 = i["L0_ffn_w1"], i["L0_ffn_w2"]
    out = {
        "x": i["L0_attn_a_x"].reshape(TILES, P, C).transpose(1, 0, 2),
        "a_w_qk": rows(w_qkv[:2 * C].T), "a_w_v": rows(w_qkv[2 * C:].T),
        "a_w_gate": rows(i["L0_attn_a_w_gated"].T), "a_w_proj": rows(i["L0_attn_a_w_proj"].T),
        "a_gn_w": column(i["L0_attn_a_gn_weight"]), "a_gn_b": column(i["L0_attn_a_gn_bias"]),
        "f_w_gate": rows(i["L0_ffn_Wg"].T), "f_b_gate": np.broadcast_to(i["L0_ffn_bg"], (P, NE)),
        "f_w1": w1.transpose(2, 0, 1).reshape(KT, P, NE, 2 * FF).transpose(1, 2, 0, 3),
        "f_w2": w2.transpose(2, 0, 1).reshape(FF // P, P, NE, C).transpose(1, 2, 0, 3),
        "b_maa_x": column(b["time_maa_x"]),
        "b_maa": b["time_maa_wkvrg"].reshape(5, KT, P).transpose(2, 0, 1),
        "b_tm_w1": rows(b["tm_w1"]),
        "b_tm_w2": b["tm_w2"].reshape(-1, C),
        "b_decay": column(b["time_decay"]), "b_td_w1": rows(b["td_w1"]), "b_td_w2": b["td_w2"],
        "b_bonus": column(b["time_faaaa"].reshape(-1)),
        "b_w_r": rows(b["Wr"]), "b_w_k": rows(b["Wk"]),
        "b_w_v": rows(by_value(b["Wv"], 1)), "b_w_g": rows(by_value(b["Wg"], 1)),
        "b_w_o": rows(by_value(b["Wo"], 0)),
        "b_ln_w": column(by_value(b["ln_w"], 0)), "b_ln_b": column(by_value(b["ln_b"], 0)),
    }
    return {k: np.ascontiguousarray(v) for k, v in out.items()}


def _route_constants():
    import numpy as np
    f = np.float32
    return {
        "rank_of": np.broadcast_to(NE - np.arange(NE, dtype=f), (P, NE)).copy(),
        "fills": np.broadcast_to(P * np.arange(TPH, dtype=f), (P, TPH)).copy(),
        "tile_no": np.broadcast_to(np.arange(RTILES, dtype=f), (P, RTILES)).copy(),
    }


_NAMES = ["L0_attn_a_x", "L0_attn_a_w_qkv", "L0_attn_a_w_gated", "L0_attn_a_w_proj", "L0_attn_a_gn_weight",
          "L0_attn_a_gn_bias", "L0_attn_b_time_maa_x", "L0_attn_b_time_maa_wkvrg", "L0_attn_b_tm_w1",
          "L0_attn_b_tm_w2", "L0_attn_b_time_decay", "L0_attn_b_td_w1", "L0_attn_b_td_w2", "L0_attn_b_time_faaaa",
          "L0_attn_b_Wr", "L0_attn_b_Wk", "L0_attn_b_Wv", "L0_attn_b_Wg", "L0_attn_b_Wo", "L0_attn_b_ln_w",
          "L0_attn_b_ln_b", "L0_ffn_Wg", "L0_ffn_bg", "L0_ffn_w1", "L0_ffn_w2"]


def program(nc, d, out):
    x_sorted = [nc.dram_tensor(f"x_sorted{h}", (ROWS, C), F32, kind="Internal").ap() for h in range(HALVES)]
    y_sorted = [nc.dram_tensor(f"y_sorted{h}", (ROWS, C), F32, kind="Internal").ap() for h in range(HALVES)]
    with ExitStack() as ctx:
        x = ctx.enter_context(nc.sbuf_tensor("x", [P, TILES, C], F32))
        x_loaded = ctx.enter_context(nc.semaphore("x_loaded"))
        out_stored = ctx.enter_context(nc.semaphore("out_stored"))
        retention(nc, d, x, x_loaded)
        experts(nc, d, x, "ffn1", x_sorted, y_sorted, True)
        recurrence(nc, d, x)
        experts(nc, d, x, "ffn2", x_sorted, y_sorted, False)
        with nc.Block() as block:
            @block.sync
            def _(sp):
                sp.dma_start(out, x[:]).then_inc(out_stored, 16)
                sp.wait_ge(out_stored, 16)


def kernel(**inputs):
    import numpy as np
    import concourse.bacc as bacc
    from concourse.bass_utils import run_bass_kernel_spmd

    arrays = {**_laid_out({n: inputs[n] for n in _NAMES}), **_shape_constants(), **_route_constants()}
    nc = bacc.Bacc("TRN2", target_bir_lowering=False, num_devices=1)
    d = {n: nc.dram_tensor("in_" + n, a.shape, F32, kind="ExternalInput").ap() for n, a in arrays.items()}
    out = nc.dram_tensor("out", (P, TILES, C), F32, kind="ExternalOutput").ap()
    program(nc, d, out)
    got = run_bass_kernel_spmd(nc, [{"in_" + n: a for n, a in arrays.items()}], core_ids=[0])
    return np.ascontiguousarray(got.results[0]["out"].transpose(1, 0, 2)).reshape(B, T, C)
```

```python
from contextlib import ExitStack

import concourse.bass as bass
from concourse import mybir

ALU = mybir.AluOpType
ACT = mybir.ActivationFunctionType
F32 = mybir.dt.float32
BF16 = mybir.dt.bfloat16
AX = mybir.AxisListType.X

P = 128
C = 256
KT = C // P
B, T = 4, 1024
TILES = B * T // P
TPB = T // P
NH, HD = 16, 16
HPT = P // HD
EPS = 1e-5
BANK = 512


def moments(dve, stats, scratch, mean, vare, step, first, n):
    even, odd = stats[:, :, 0:3], stats[:, :, 3:6]
    total, apart, squares = scratch[:, 0, :], scratch[:, 1, :], scratch[:, 2, :]
    dve.tensor_tensor(total, even[:, :, 1], odd[:, :, 1], ALU.add).then_inc(step, 1)
    dve.tensor_tensor(apart, even[:, :, 1], odd[:, :, 1], ALU.subtract).then_inc(step, 1)
    dve.tensor_tensor(squares, even[:, :, 2], odd[:, :, 2], ALU.add).then_inc(step, 1)
    dve.wait_ge(step, first + 1)
    dve.tensor_scalar(mean, total, 0.5, None, ALU.mult).then_inc(step, 1)
    dve.wait_ge(step, first + 2)
    dve.tensor_tensor(apart, apart, apart, ALU.mult).then_inc(step, 1)
    dve.wait_ge(step, first + 3)
    dve.tensor_scalar(squares, squares, 1.0 / n, EPS, ALU.mult, ALU.add).then_inc(step, 1)
    dve.wait_ge(step, first + 6)
    dve.scalar_tensor_tensor(vare, apart, 0.25, squares, ALU.mult, ALU.add).then_inc(step, 1)


MOMENT_STEPS = 7


def retention(nc, d, x, x_loaded):
    with ExitStack() as ctx:
        def sb(name, shape, dt=F32):
            return ctx.enter_context(nc.sbuf_tensor("ret_" + name, shape, dt))

        def ps(name, shape):
            return ctx.enter_context(nc.psum_tensor("ret_" + name, shape, F32))

        def sem(name):
            return ctx.enter_context(nc.semaphore("ret_" + name))

        w_qk = sb("w_qk", [P, KT, 2 * C])
        w_v = sb("w_v", [P, KT, C])
        w_gate = sb("w_gate", [P, KT, C])
        w_proj = sb("w_proj", [P, KT, C])
        rope_cos = sb("rope_cos", [P, TPB, 2 * C])
        rope_sin = sb("rope_sin", [P, TPB, 2 * C])
        ident = sb("ident", [P, P])
        causal = sb("causal", [P, P])
        head_of = sb("head_of", [P, HPT])
        same_head = sb("same_head", [P, P])
        head_mean = sb("head_mean", [P, P])
        gn_w = sb("gn_w", [P, KT])
        gn_b = sb("gn_b", [P, KT])
        expo = sb("expo", [P, TPB])
        stats = sb("stats", [P, TPB, 6])
        scratch = sb("scratch", [P, 3, TPB])
        mean = sb("mean", [P, TPB])
        vare = sb("vare", [P, TPB])
        rstd = sb("rstd", [P, TPB])
        xn = sb("xn", [P, TPB, C])
        xnt = sb("xnt", [P, KT, T])
        roped = sb("roped", [P, 2, 2 * C])
        rope_t1 = sb("rope_t1", [P, 2 * C])
        rope_t2 = sb("rope_t2", [P, 2 * C])
        v = sb("v", [P, 2, C])
        v_heads = sb("v_heads", [P, 2, NH, P])
        qkt = sb("qkt", [P, 2, 4, P])
        q_heads = sb("q_heads", [P, NH, P])
        probs = sb("probs", [P, NH, P])
        state = sb("state", [P, KT, P])
        state_add = sb("state_add", [P, KT, P])
        yt = sb("yt", [P, KT, T])
        silu_g = sb("silu_g", [P, KT, T])
        ynorm = sb("ynorm", [P, KT, T])
        gn_stats = sb("gn_stats", [P, KT, 2, 6])
        gn_sum = sb("gn_sum", [P, KT])
        gn_dev = sb("gn_dev", [P, KT, 4])
        gn_dev_sum = sb("gn_dev_sum", [P, KT])
        gn_squares = sb("gn_squares", [P, KT])
        gn_var = sb("gn_var", [P, KT])
        gn_mean = sb("gn_mean", [P, KT])
        gn_vare = sb("gn_vare", [P, KT])
        gn_rstd = sb("gn_rstd", [P, KT])
        gn_scale = sb("gn_scale", [P, KT])
        gn_shift = sb("gn_shift", [P, KT])

        score = ps("score", [P, 4, BANK])
        ps_qk = ps("ps_qk", [P, BANK])
        ps_xv = ps("ps_xv", [P, BANK])
        ps_xt, ps_v = ps_xv[:, 0:C], ps_xv[:, C:2 * C]
        ps_qkt = ps("ps_qkt", [P, BANK])
        ps_ys = ps("ps_ys", [P, BANK])
        out_banks = [ps_qkt, ps_xv]
        ps_y, ps_state = ps_ys[:, 0:C], ps_ys[:, C:2 * C]

        consts_loaded = sem("consts_loaded")
        zeroed = sem("zeroed")
        ln_stats = sem("ln_stats")
        ln_moments = sem("ln_moments")
        ln_rstd = sem("ln_rstd")
        xn_ready = sem("xn_ready")
        xt_in_psum = sem("xt_in_psum")
        xnt_ready = sem("xnt_ready")
        qk_in_psum = sem("qk_in_psum")
        v_in_psum = sem("v_in_psum")
        v_ready = sem("v_ready")
        rope_parts = sem("rope_parts")
        rope_done = sem("rope_done")
        qkt_in_psum = sem("qkt_in_psum")
        qkt_ready = sem("qkt_ready")
        q_heads_ready = sem("q_heads_ready")
        score_in_psum = sem("score_in_psum")
        probs_ready = sem("probs_ready")
        y_in_psum = sem("y_in_psum")
        yt_ready = sem("yt_ready")
        state_masked = sem("state_masked")
        state_ready = sem("state_ready")
        gate_in_psum = sem("gate_in_psum")
        gate_ready = sem("gate_ready")
        gn_half_stats = sem("gn_half_stats")
        gn_step = sem("gn_step")
        gn_sums = sem("gn_sums")
        gn_root = sem("gn_root")
        ynorm_ready = sem("ynorm_ready")
        out_in_psum = sem("out_in_psum")
        x_added = sem("x_added")

        consts = [(w_qk, "a_w_qk"), (w_v, "a_w_v"), (w_gate, "a_w_gate"), (w_proj, "a_w_proj"),
                  (rope_cos, "rope_cos"), (rope_sin, "rope_sin"), (ident, "ident"), (causal, "causal"),
                  (head_of, "head_of"), (same_head, "same_head"), (head_mean, "head_mean"),
                  (gn_w, "a_gn_w"), (gn_b, "a_gn_b")]
        HALF = T // 2
        GN_STEPS = 12

        starts_at_one = [xnt_ready, v_ready, rope_parts, qkt_ready, q_heads_ready, gate_ready, yt_ready, state_masked, state_ready]
        with nc.Block() as block:
            @block.sync
            def _(sp):
                for s in starts_at_one:
                    sp.sem_inc(s, 1)

        with nc.Block() as block:

            @block.sync
            def _(sp):
                for tile, name in consts:
                    sp.dma_start(tile[:], d[name]).then_inc(consts_loaded, 16)
                for b in range(B):
                    sp.wait_ge(x_loaded, b * 16)
                    sp.dma_start(x[:, b * TPB:(b + 1) * TPB, :], d["x"][:, b * TPB:(b + 1) * TPB, :]) \
                        .then_inc(x_loaded, 16)
                sp.wait_ge(x_loaded, 16 * B)
                sp.wait_ge(consts_loaded, 16 * len(consts))

            @block.gpsimd
            def _(pool):
                pool.memset(expo[:], -0.5).then_inc(zeroed, 1)
                pool.memset(v_heads[:], 0.0).then_inc(zeroed, 1)
                pool.wait_ge(zeroed, 2)
                with pool.Fori(0, B) as b:
                    pool.wait_ge(ln_moments, (b + 1) * MOMENT_STEPS)
                    pool.tensor_tensor(rstd[:], vare[:], expo[:], ALU.pow).then_inc(ln_rstd, 1)
                    for c in range(TPB):
                        pool.wait_ge(rope_parts, 1 + (b * TPB + (c + 1)) * 3)
                        if c >= 2:
                            pool.wait_ge(y_in_psum, b * TPB + (c - 1))
                        pool.tensor_tensor(roped[:, c % 2, :], rope_t1[:], rope_t2[:], ALU.add) \
                            .then_inc(rope_done, 1)
                        if c >= 3:
                            pool.wait_ge(state_masked, 1 + b * (TPB - 1) + (c - 1))
                            pool.tensor_tensor(state[:], state[:], state_add[:], ALU.add).then_inc(state_ready, 1)
                    pool.wait_ge(state_masked, 1 + (b + 1) * (TPB - 1))
                    pool.tensor_tensor(state[:], state[:], state_add[:], ALU.add).then_inc(state_ready, 1)
                    pool.wait_ge(gn_step, b * GN_STEPS + 9)
                    pool.tensor_tensor(gn_rstd[:], gn_vare[:], expo[:, 0:KT], ALU.pow).then_inc(gn_root, 1)

            @block.scalar
            def _(act):
                def x_transposed(b, c):
                    act.wait_ge(xt_in_psum, b * TPB + (c + 1))
                    act.activation(xnt[:, :, c * P:(c + 1) * P], ps_xt.rearrange("p (k t) -> p k t", k=KT),
                                   ACT.Copy).then_inc(xnt_ready, 1)

                def y_out(b, c):
                    act.wait_ge(y_in_psum, b * TPB + (c + 1))
                    act.activation(yt[:, :, c * P:(c + 1) * P], ps_y.rearrange("p (k t) -> p k t", k=KT),
                                   ACT.Copy).then_inc(yt_ready, 1)

                def v_out(b, c):
                    act.wait_ge(v_in_psum, b * TPB + (c + 1))
                    act.activation(v[:, c % 2, :], ps_v, ACT.Copy).then_inc(v_ready, 1)
                    for k in range(KT):
                        blocks = v_heads[:, c % 2, k * HPT:(k + 1) * HPT, :]
                        diagonal = bass.AP(blocks.tensor, blocks.offset,
                                           [blocks.ap[0], [P + HD, HPT], [1, HD]])
                        act.activation(diagonal, ps_v[:, k * P:(k + 1) * P].rearrange("p (h e) -> p h e", e=HD),
                                       ACT.Copy).then_inc(v_ready, 1)

                def qk_out(b, c):
                    act.wait_ge(qkt_in_psum, b * TPB + (c + 1))
                    act.activation(qkt[:, c % 2, :, :], ps_qkt[:].rearrange("p (j t) -> p j t", j=4),
                                   ACT.Copy).then_inc(qkt_ready, 1)

                act.wait_ge(zeroed, 2)
                with act.Fori(0, B) as b:
                    for t in range(TPB + 2):
                        if t < TPB:
                            x_transposed(b, t)
                        if t >= 2:
                            y_out(b, t - 2)
                        if t < TPB:
                            v_out(b, t)
                            qk_out(b, t)
                    act.wait_ge(gate_in_psum, b + 1)
                    act.activation(silu_g[:], score[:].rearrange("p (k n) t -> p k (n t)", k=KT),
                                   ACT.Silu).then_inc(gate_ready, 1)

            @block.tensor
            def _(pe):
                def transpose_x(b, c):
                    pe.wait_ge(xn_ready, b * TPB + (c + 1))
                    pe.wait_ge(xnt_ready, 1 + b * TPB + c)
                    pe.wait_ge(v_ready, 1 + (b * TPB + c) * 3)
                    for k in range(KT):
                        mm = pe.transpose(ps_xt[:, k * P:(k + 1) * P], xn[:, c, k * P:(k + 1) * P], ident[:])
                    mm.then_inc(xt_in_psum, 1)

                def project(b, c):
                    pe.wait_ge(xnt_ready, 1 + b * TPB + (c + 1))
                    pe.wait_ge(rope_parts, 1 + (b * TPB + c) * 3)
                    for k in range(KT):
                        mm = pe.matmul(ps_qk[:], xnt[:, k, c * P:(c + 1) * P], w_qk[:, k, :],
                                       start=(k == 0), stop=(k == KT - 1))
                    mm.then_inc(qk_in_psum, 1)
                    for k in range(KT):
                        mm = pe.matmul(ps_v, xnt[:, k, c * P:(c + 1) * P], w_v[:, k, :],
                                       start=(k == 0), stop=(k == KT - 1))
                    mm.then_inc(v_in_psum, 1)

                def transpose_qk(b, c):
                    pe.wait_ge(rope_done, b * TPB + (c + 1))
                    pe.wait_ge(qkt_ready, 1 + b * TPB + c)
                    pe.wait_ge(q_heads_ready, 1 + (b * TPB + c) * 2)
                    for j in range(4):
                        mm = pe.transpose(ps_qkt[:, j * P:(j + 1) * P], roped[:, c % 2, j * P:(j + 1) * P], ident[:])
                    mm.then_inc(qkt_in_psum, 1)

                def scores(b, c):
                    pe.wait_ge(qkt_ready, 1 + b * TPB + (c + 1))
                    for k in range(KT):
                        pe.wait_ge(q_heads_ready, 1 + (b * TPB + c) * 2 + (k + 1))
                        for n in range(2):
                            bank = 2 * k + n
                            if c == 0:
                                pe.wait_ge(gate_ready, 1 + b)
                            else:
                                pe.wait_ge(probs_ready, (b * TPB + (c - 1)) * 4 + (bank + 1))
                            pe.matmul(score[:, bank, :], qkt[:, c % 2, 2 + k, :],
                                      q_heads[:, 4 * bank:4 * bank + 4, :], start=True, stop=True) \
                                .then_inc(score_in_psum, 1)

                def outputs(b, c):
                    pe.wait_ge(yt_ready, 1 + b * TPB + c)
                    pe.wait_ge(state_masked, 1 + b * (TPB - 1) + c)
                    pe.wait_ge(v_ready, 1 + (b * TPB + (c + 1)) * 3)
                    if c >= 2:
                        pe.wait_ge(state_ready, 1 + b * (TPB - 2) + (c - 1))
                    for k in range(KT):
                        y_half = ps_y[:, k * P:(k + 1) * P]
                        if c >= 1:
                            pe.matmul(y_half, state[:, k, :], qkt[:, c % 2, k, :], start=True, stop=False)
                        for h in range(HPT):
                            head = k * HPT + h
                            if h % 4 == 0:
                                pe.wait_ge(probs_ready, (b * TPB + c) * 4 + (head // 4 + 1))
                            mm = pe.matmul(y_half, v_heads[:, c % 2, head, :], probs[:, head, :],
                                      start=(h == 0 and c == 0), stop=(h == HPT - 1))
                    for k in range(KT if c < TPB - 1 else 0):
                        mm = pe.matmul(ps_state[:, k * P:(k + 1) * P], roped[:, c % 2, C + k * P:C + (k + 1) * P],
                                       v[:, c % 2, k * P:(k + 1) * P], start=True, stop=True)
                    mm.then_inc(y_in_psum, 1)

                pe.wait_ge(consts_loaded, 16 * len(consts))
                with pe.Fori(0, B) as b:
                    for t in range(TPB + 2):
                        if t < TPB:
                            transpose_x(b, t)
                        if t >= 2:
                            outputs(b, t - 2)
                        if t < TPB:
                            project(b, t)
                        if 1 <= t <= TPB:
                            scores(b, t - 1)
                        if t < TPB:
                            transpose_qk(b, t)
                    pe.wait_ge(probs_ready, (b + 1) * TPB * 4)
                    for k in range(KT):
                        for n in range(2):
                            for kk in range(KT):
                                mm = pe.matmul(score[:, 2 * k + n, :], w_gate[:, kk, k * P:(k + 1) * P],
                                               xnt[:, kk, n * HALF:(n + 1) * HALF],
                                               start=(kk == 0), stop=(kk == KT - 1))
                    mm.then_inc(gate_in_psum, 1)
                    pe.wait_ge(gn_step, b * GN_STEPS + 1)
                    pe.matmul(ps_qk[:, 0:KT], head_mean[:], gn_sum[:], start=True, stop=True) \
                        .then_inc(gn_sums, 1)
                    pe.wait_ge(gn_step, b * GN_STEPS + 8)
                    pe.matmul(ps_qk[:, KT:2 * KT], head_mean[:], gn_var[:], start=True, stop=True) \
                        .then_inc(gn_sums, 1)
                    pe.wait_ge(ynorm_ready, (b + 1) * 4)
                    for c in range(TPB):
                        if c >= 2:
                            pe.wait_ge(x_added, b * TPB + (c - 1))
                        for k in range(KT):
                            mm = pe.matmul(out_banks[c % 2][:, 0:C], ynorm[:, k, c * P:(c + 1) * P],
                                           w_proj[:, k, :], start=(k == 0), stop=(k == KT - 1))
                        mm.then_inc(out_in_psum, 1)

            @block.vector
            def _(dve):
                def rotate(b, c):
                    dve.wait_ge(qk_in_psum, b * TPB + (c + 1))
                    if c >= 1:
                        dve.wait_ge(rope_done, b * TPB + c)
                    pairs = ps_qk[:].rearrange("p (j two) -> p j two", two=2)
                    sin = rope_sin[:, c, :].rearrange("p (j two) -> p j two", two=2)
                    t2 = rope_t2[:].rearrange("p (j two) -> p j two", two=2)
                    dve.tensor_tensor(rope_t1[:], ps_qk[:], rope_cos[:, c, :], ALU.mult).then_inc(rope_parts, 1)
                    for e in range(2):
                        dve.tensor_tensor(t2[:, :, e], pairs[:, :, 1 - e], sin[:, :, e], ALU.mult) \
                            .then_inc(rope_parts, 1)

                def mask(b, c):
                    if c >= 1:
                        dve.wait_ge(y_in_psum, b * TPB + c)
                    for bank in range(4):
                        dve.wait_ge(score_in_psum, (b * TPB + c) * 4 + (bank + 1))
                        dve.tensor_tensor(probs[:, 4 * bank:4 * bank + 4, :],
                                          score[:, bank, :].rearrange("p (h t) -> p h t", h=4),
                                          causal[:].unsqueeze(1).to_broadcast([P, 4, P]), ALU.mult) \
                            .then_inc(probs_ready, 1)

                def spread_q(b, c):
                    dve.wait_ge(qkt_ready, 1 + b * TPB + (c + 1))
                    if c >= 1:
                        dve.wait_ge(score_in_psum, (b * TPB + c) * 4)
                    for k in range(KT):
                        dve.tensor_tensor(q_heads[:, k * HPT:(k + 1) * HPT, :],
                                          qkt[:, c % 2, k, :].unsqueeze(1).to_broadcast([P, HPT, P]),
                                          head_of[:].unsqueeze(2).to_broadcast([P, HPT, P]), ALU.mult) \
                            .then_inc(q_heads_ready, 1)

                def add_state(b, c):
                    dve.wait_ge(yt_ready, 1 + b * TPB + (c + 1))
                    if c == 0:
                        dve.wait_ge(state_ready, 1 + b * (TPB - 2))
                    if c >= 2:
                        dve.wait_ge(state_ready, 1 + b * (TPB - 2) + (c - 1))
                    into = state if c == 0 else state_add
                    dve.tensor_tensor(into[:], ps_state.rearrange("p (k e) -> p k e", k=KT),
                                      same_head[:].unsqueeze(1).to_broadcast([P, KT, P]), ALU.mult) \
                        .then_inc(state_masked, 1)

                dve.wait_ge(consts_loaded, 16 * len(consts))
                with dve.Fori(0, B) as b:
                    dve.wait_ge(x_loaded, (b + 1) * 16)
                    for c in range(TPB):
                        dve.bn_stats(stats[:, c, :], x[:, b * TPB + c, :]).then_inc(ln_stats, 1)
                    dve.wait_ge(ln_stats, (b + 1) * TPB)
                    moments(dve, stats, scratch, mean[:], vare[:], ln_moments, b * MOMENT_STEPS, C)
                    dve.wait_ge(ln_rstd, b + 1)
                    for c in range(TPB):
                        dve.tensor_scalar(xn[:, c, :], x[:, b * TPB + c, :], mean[:, c:c + 1], rstd[:, c:c + 1],
                                          ALU.subtract, ALU.mult).then_inc(xn_ready, 1)
                    for t in range(TPB + 2):
                        if 2 <= t <= TPB:
                            add_state(b, t - 2)
                        if t < TPB:
                            rotate(b, t)
                        if 1 <= t <= TPB:
                            mask(b, t - 1)
                        if t < TPB:
                            spread_q(b, t)
                    dve.wait_ge(yt_ready, 1 + (b + 1) * TPB)
                    for k in range(KT):
                        for n in range(2):
                            dve.bn_stats(gn_stats[:, k, n, :], yt[:, k, n * HALF:(n + 1) * HALF]) \
                                .then_inc(gn_half_stats, 1)
                    parts = gn_stats[:].rearrange("p k n (g s) -> p k (n g) s", s=3)
                    dve.wait_ge(gn_half_stats, (b + 1) * 4)
                    dve.tensor_reduce(gn_sum[:], parts[:, :, :, 1], AX, ALU.add).then_inc(gn_step, 1)
                    dve.tensor_reduce(gn_squares[:], parts[:, :, :, 2], AX, ALU.add).then_inc(gn_step, 1)
                    dve.wait_ge(gn_sums, b * 2 + 1)
                    dve.tensor_scalar(gn_mean[:], ps_qk[:, 0:KT], 0.25, None, ALU.mult).then_inc(gn_step, 1)
                    dve.wait_ge(gn_step, b * GN_STEPS + 3)
                    dve.tensor_tensor(gn_dev[:], parts[:, :, :, 1], gn_mean[:].unsqueeze(2).to_broadcast([P, KT, 4]),
                                      ALU.subtract).then_inc(gn_step, 1)
                    dve.wait_ge(gn_step, b * GN_STEPS + 4)
                    dve.tensor_tensor(gn_dev[:], gn_dev[:], gn_dev[:], ALU.mult).then_inc(gn_step, 1)
                    dve.wait_ge(gn_step, b * GN_STEPS + 5)
                    dve.tensor_reduce(gn_dev_sum[:], gn_dev[:], AX, ALU.add).then_inc(gn_step, 1)
                    dve.tensor_scalar(gn_squares[:], gn_squares[:], 1.0 / T, None, ALU.mult).then_inc(gn_step, 1)
                    dve.wait_ge(gn_step, b * GN_STEPS + 7)
                    dve.scalar_tensor_tensor(gn_var[:], gn_dev_sum[:], 0.25, gn_squares[:], ALU.mult, ALU.add) \
                        .then_inc(gn_step, 1)
                    dve.wait_ge(gn_sums, b * 2 + 2)
                    dve.tensor_scalar(gn_vare[:], ps_qk[:, KT:2 * KT], EPS, None, ALU.add).then_inc(gn_step, 1)
                    dve.wait_ge(gn_root, b + 1)
                    dve.tensor_tensor(gn_scale[:], gn_rstd[:], gn_w[:], ALU.mult).then_inc(gn_step, 1)
                    dve.wait_ge(gn_step, b * GN_STEPS + 10)
                    dve.tensor_tensor(gn_shift[:], gn_mean[:], gn_scale[:], ALU.mult).then_inc(gn_step, 1)
                    dve.wait_ge(gn_step, b * GN_STEPS + 11)
                    dve.tensor_tensor(gn_shift[:], gn_b[:], gn_shift[:], ALU.subtract).then_inc(gn_step, 1)
                    dve.wait_ge(gn_step, b * GN_STEPS + 12)
                    for k in range(KT):
                        dve.tensor_scalar(ynorm[:, k, :], yt[:, k, :], gn_scale[:, k:k + 1], gn_shift[:, k:k + 1],
                                          ALU.mult, ALU.add).then_inc(ynorm_ready, 1)
                    dve.wait_ge(gate_ready, 1 + b + 1)
                    for k in range(KT):
                        dve.wait_ge(ynorm_ready, b * 4 + 2 + k)
                        dve.tensor_tensor(ynorm[:, k, :], ynorm[:, k, :], silu_g[:, k, :], ALU.mult) \
                            .then_inc(ynorm_ready, 1)
                    for c in range(TPB):
                        dve.wait_ge(out_in_psum, b * TPB + (c + 1))
                        dve.tensor_tensor(x[:, b * TPB + c, :], x[:, b * TPB + c, :],
                                          out_banks[c % 2][:, 0:C], ALU.add).then_inc(x_added, 1)
                dve.wait_ge(x_added, TILES)


NE = 8
FF = 256
TOPK = 2
HALVES = 2
TPH = TILES // HALVES
UNROLL = 4
RTILES = -(-(TOPK * TPH + NE - 1) // UNROLL) * UNROLL
NTILES = HALVES * RTILES
DIGIT = (NE - 1).bit_length()
LAG = 2
ROWS = RTILES * P


def experts(nc, d, x, name, x_sorted, y_sorted, clear):
    with ExitStack() as ctx:
        def sb(n, shape, dt=F32):
            return ctx.enter_context(nc.sbuf_tensor(f"{name}_{n}", shape, dt))

        def ps(n, shape):
            return ctx.enter_context(nc.psum_tensor(f"{name}_{n}", shape, F32))

        def sem(n):
            return ctx.enter_context(nc.semaphore(f"{name}_{n}"))

        w1 = sb("w1", [P, NE, KT, 2 * FF])
        w2 = sb("w2", [P, NE, KT, C])
        w_gate = sb("w_gate", [P, KT, NE])
        b_gate = sb("b_gate", [P, NE])
        ident = sb("ident", [P, P])
        tri_f = sb("tri_f", [P, P])
        tri = sb("tri", [P, P], BF16)
        ones = sb("ones", [P, P], BF16)
        ones_row = sb("ones_row", [P, TPH])
        rank_of = sb("rank_of", [P, NE])
        fills = sb("fills", [P, TPH])
        tile_no = sb("tile_no", [P, RTILES])
        expo = sb("expo", [P, TILES])
        zeros = sb("zeros", [P, 8, C])

        stats = sb("stats", [P, TILES, 6])
        scratch = sb("scratch", [P, 3, TILES])
        mean = sb("mean", [P, TILES])
        vare = sb("vare", [P, TILES])
        rstd = sb("rstd", [P, TILES])
        xn = sb("xn", [P, TILES, C])
        xn_turn = sb("xn_turn", [P, 2, UNROLL, C])
        xnt = sb("xnt", [P, 2, KT, UNROLL * P])
        logits = sb("logits", [P, TILES, NE])
        first = sb("first", [P, TILES, NE])
        second = sb("second", [P, TILES, NE])
        hits = sb("hits", [P, TILES, NE])
        rest = sb("rest", [P, TILES, NE])
        top = sb("top", [P, TOPK, TILES])
        best = sb("best", [P, TOPK, TILES])
        gap = sb("gap", [P, TILES])
        odds = sb("odds", [P, TILES])
        total = sb("total", [P, TILES])
        weight = sb("weight", [P, TOPK, TILES])
        chosen = sb("chosen", [P, TILES, NE], BF16)
        running = sb("running", [P, TILES, NE])
        slot = sb("slot", [P, TILES, NE])
        over = sb("over", [P, HALVES * NE, TPH])
        tiles_of = sb("tiles_of", [P, HALVES, NE])
        tiles_end = sb("tiles_end", [P, HALVES, NE])
        row_of = sb("row_of", [P, HALVES, NE])
        passed = sb("passed", [P, HALVES, RTILES, NE])
        expert_f = sb("expert_f", [P, LAG + NTILES])
        experts_f = sb("experts_f", [P, NTILES // UNROLL])
        experts_of = sb("experts_of", [P, NTILES // UNROLL], mybir.dt.int32)
        place_f = sb("place_f", [P, TOPK, TILES])
        place = sb("place", [P, TOPK, TILES], mybir.dt.uint32)

        xs = sb("xs", [P, UNROLL, C])
        xst = sb("xst", [P, 2, KT, P])
        silu_g = sb("silu_g", [P, 2, FF])
        act_in = sb("act_in", [P, 2, FF])
        act_t = sb("act_t", [P, 2, KT, P])
        ys = sb("ys", [P, UNROLL, C])
        back = sb("back", [P, 4, TOPK, C])

        ps_t = ps("ps_t", [P, KT, BANK])
        ps_l = ps("ps_l", [P, BANK])
        ps_h = ps("ps_h", [P, 2, BANK])
        ps_a = ps("ps_a", [P, BANK])
        ps_o = ps("ps_o", [P, 2, BANK])
        ps_xt = [ps_t, ps_h]

        weights_loaded = sem("weights_loaded")
        consts_loaded = sem("consts_loaded")
        constants_ready = sem("constants_ready")
        cleared = sem("cleared")
        ln_stats = sem("ln_stats")
        ln_moments = sem("ln_moments")
        ln_rstd = sem("ln_rstd")
        xn_ready = sem("xn_ready")
        xn_kept = sem("xn_kept")
        xt_in_psum = sem("xt_in_psum")
        xnt_ready = sem("xnt_ready")
        logits_in_psum = sem("logits_in_psum")
        logits_ready = sem("logits_ready")
        route_step = sem("route_step")
        odds_ready = sem("odds_ready")
        packing = sem("packing")
        counts_in_psum = sem("counts_in_psum")
        scattered = [sem(f"scattered{h}") for h in range(HALVES)]
        xs_loaded = [sem(f"xs_loaded{u}") for u in range(UNROLL)]
        xst_in_psum = sem("xst_in_psum")
        xst_ready = sem("xst_ready")
        h_in_psum = sem("h_in_psum")
        silu_ready = sem("silu_ready")
        act_ready = sem("act_ready")
        act_t_in_psum = sem("act_t_in_psum")
        act_t_ready = sem("act_t_ready")
        y_in_psum = sem("y_in_psum")
        ys_ready = sem("ys_ready")
        ys_stored = [sem(f"ys_stored{u}") for u in range(UNROLL)]
        gathered = [sem(f"gathered{u}") for u in range(4)]
        x_added = sem("x_added")

        weights = [(w1, "f_w1"), (w2, "f_w2")]
        consts = [(w_gate, "f_w_gate"), (b_gate, "f_b_gate"), (ident, "ident"), (tri_f, "tri"),
                  (rank_of, "rank_of"), (fills, "fills"), (tile_no, "tile_no")]
        STEPS = TILES // UNROLL
        TURNS = RTILES // UNROLL

        (TOP1, EQ1, RANK1, BEST1, FIRST, REST, TOP2, EQ2, RANK2, BEST2, SECOND, GAP, CHOSEN, SUM, SHARE, SHARE2,
         RUN, EXCL, SLOT, OVER, TILES_OF, TILES_END, ROW, SHIFT, PLACED, HIT1, POS1, HIT2, POS2, PLACE, PASSED,
         EXPERT, CLAMP, EXPERTS_OF) = range(1, 35)

        starts_at_one = [xst_ready, act_ready, act_t_ready, ys_ready, *ys_stored]
        with nc.Block() as block:
            @block.sync
            def _(sp):
                for s in starts_at_one:
                    sp.sem_inc(s, 1)

        with nc.Block() as block:

            @block.sync
            def _(sp):
                for tile, n in consts:
                    sp.dma_start(tile[:], d[n]).then_inc(consts_loaded, 16)
                for tile, n in weights:
                    sp.dma_start(tile[:], d[n]).then_inc(weights_loaded, 16)
                if clear:
                    sp.wait_ge(constants_ready, 1)
                    for half in range(HALVES):
                        for r in range(0, ROWS, 8 * P):
                            sp.dma_start(x_sorted[half][r:r + 8 * P, :].rearrange("(p i) c -> p i c", p=P), zeros[:]) \
                                .then_inc(cleared, 16)
                def load(half, tile, u):
                    rows = x_sorted[half].rearrange("(i p) c -> i p c", p=P)
                    sp.dma_start(xs[:, u, :], rows[tile]).then_inc(xs_loaded[u], 16)

                for half in range(HALVES):
                    if half == 0:
                        sp.wait_ge(scattered[half], 16 * TOPK * TPH)
                        for u in range(UNROLL):
                            load(half, u, u)
                    with sp.Fori(1 if half == 0 else 0, TURNS) as turn:
                        for u in range(UNROLL):
                            sp.wait_ge(xst_in_psum, half * RTILES - UNROLL + 1 + turn * UNROLL + u)
                            sp.wait_ge(scattered[half], 16 * TOPK * TPH)
                            load(half, turn * UNROLL + u, u)
                for u in range(UNROLL):
                    sp.wait_ge(ys_stored[u], 1 + 16 * HALVES * TURNS)
                sp.wait_ge(weights_loaded, 16 * len(weights))

            @block.gpsimd
            def _(pool):
                pool.memset(zeros[:], 0.0).then_inc(constants_ready, 1)
                pool.memset(expo[:], -0.5).then_inc(constants_ready, 1)
                pool.memset(ones[:], 1.0).then_inc(constants_ready, 1)
                pool.memset(ones_row[:], 1.0).then_inc(constants_ready, 1)
                pool.memset(expert_f[:, 0:LAG], 0.0).then_inc(constants_ready, 1)
                pool.wait_ge(ln_moments, MOMENT_STEPS)
                pool.wait_ge(constants_ready, 5)
                pool.tensor_tensor(rstd[:], vare[:], expo[:], ALU.pow).then_inc(ln_rstd, 1)
                pool.wait_ge(route_step, PLACE)
                pool.wait_ge(xn_kept, STEPS)
                if clear:
                    pool.wait_ge(cleared, 16 * HALVES * (ROWS // (8 * P)))
                for half in range(HALVES):
                    for i in range(half * TPH, (half + 1) * TPH):
                        for s in range(TOPK):
                            pool.indirect_dma_start(
                                x_sorted[half][:], bass.IndirectOffsetOnAxis(ap=place[:, s, i:i + 1], axis=0),
                                xn[:, i, :], None).then_inc(scattered[half], 16)
                for half in range(HALVES):
                    for u in range(UNROLL):
                        pool.wait_ge(ys_stored[u], 1 + 16 * TURNS * (half + 1))
                    for i in range(half * TPH, (half + 1) * TPH):
                        if i >= 4:
                            pool.wait_ge(x_added, TOPK * (i - 3))
                        for s in range(TOPK):
                            pool.indirect_dma_start(
                                back[:, i % 4, s, :], None, y_sorted[half][:],
                                bass.IndirectOffsetOnAxis(ap=place[:, s, i:i + 1], axis=0)) \
                                .then_inc(gathered[i % 4], 16)

            @block.scalar
            def _(act):
                def norm_out(turn):
                    for h in range(2):
                        n = turn * 2 + h
                        act.wait_ge(xn_ready, n + 1)
                        act.activation(xn[:, h * UNROLL:, :][:, bass.ds(turn * 2 * UNROLL, UNROLL), :], xn_turn[:, h, :, :],
                                       ACT.Copy).then_inc(xn_kept, 1)
                        act.wait_ge(xt_in_psum, n + 1)
                        if not isinstance(turn, int):
                            act.wait_ge(logits_in_psum, n - 1)
                        act.activation(xnt[:, h, :, :], ps_xt[h][:], ACT.Copy).then_inc(xnt_ready, 1)

                norm_out(0)
                with act.Fori(1, STEPS // 2) as turn:
                    norm_out(turn)
                act.wait_ge(route_step, GAP)
                act.activation(odds[:], gap[:], ACT.Exp).then_inc(odds_ready, 1)

                def x_out(n, u):
                    act.wait_ge(xst_in_psum, n + 1)
                    act.activation(xst[:, u % 2, :, :], ps_t[:, u % 2, 0:C].rearrange("p (k t) -> p k t", k=KT),
                                   ACT.Copy).then_inc(xst_ready, 1)

                def silu(n, u):
                    act.wait_ge(h_in_psum, n + 1)
                    act.activation(silu_g[:, u % 2, :], ps_h[:, u % 2, 0:FF], ACT.Silu).then_inc(silu_ready, 1)

                def y_out(n, u):
                    act.wait_ge(y_in_psum, n + 1)
                    if not (isinstance(n, int) and n < UNROLL):
                        act.wait_ge(ys_stored[u], 1 + stores_before(n, u))
                    act.activation(ys[:, u, :], ps_o[:, u % 2, 0:C], ACT.Copy).then_inc(ys_ready, 1)

                def store(n, u, half):
                    act.wait_ge(ys_ready, 1 + n + 1)
                    act.dma_start(y_sorted[half].rearrange("(i p) c -> i p c", p=P)[n - half * RTILES], ys[:, u, :]) \
                        .then_inc(ys_stored[u], 16)

                def stores_before(n, u):
                    return (n - u) * (16 // UNROLL)

                def turn_of_loop(turn, half):
                    first, last = (isinstance(turn, int) and turn == t for t in (0, HALVES * TURNS - 1))
                    for u in range(UNROLL):
                        n = turn * UNROLL + u
                        silu(n, u)
                        if not last or u + 2 < UNROLL:
                            x_out(n + 2, (u + 2) % UNROLL)
                        if not first or u >= LAG:
                            y_out(n - LAG, (u - LAG) % UNROLL)
                        if not first or u > LAG:
                            of_last_half = isinstance(turn, int) and turn == half * TURNS and u <= LAG
                            store(n - LAG - 1, (u - LAG - 1) % UNROLL, half - of_last_half)
                    if last:
                        for u in range(UNROLL - LAG - 1, UNROLL):
                            if u >= UNROLL - LAG:
                                y_out(turn * UNROLL + u, u)
                            store(turn * UNROLL + u, u, half)

                x_out(0, 0)
                x_out(1, 1)
                turn_of_loop(0, 0)
                for half in range(HALVES):
                    if half > 0:
                        turn_of_loop(half * TURNS, half)
                    last = half == HALVES - 1
                    with act.Fori(half * TURNS + 1, (half + 1) * TURNS - last) as turn:
                        turn_of_loop(turn, half)
                turn_of_loop(HALVES * TURNS - 1, HALVES - 1)

            @block.tensor
            def _(pe):
                pe.wait_ge(consts_loaded, 16 * len(consts))
                def transpose_norm(turn, h):
                    n = turn * 2 + h
                    pe.wait_ge(xn_ready, n + 1)
                    if not isinstance(turn, int):
                        pe.wait_ge(xnt_ready, n - 1)
                    for j in range(UNROLL):
                        for k in range(KT):
                            mm = pe.transpose(ps_xt[h][:, k, j * P:(j + 1) * P],
                                              xn_turn[:, h, j, k * P:(k + 1) * P], ident[:])
                    mm.then_inc(xt_in_psum, 1)

                def gate_logits(n, h):
                    pe.wait_ge(xnt_ready, n + 1)
                    for j in range(UNROLL):
                        for k in range(KT):
                            mm = pe.matmul(ps_l[:, j * NE:][:, bass.ds(n * UNROLL * NE, NE)],
                                           xnt[:, h, k, j * P:(j + 1) * P], w_gate[:, k, :],
                                           start=(k == 0), stop=(k == KT - 1))
                    mm.then_inc(logits_in_psum, 1)

                transpose_norm(0, 0)
                transpose_norm(0, 1)
                gate_logits(0, 0)
                with pe.Fori(1, STEPS // 2) as turn:
                    transpose_norm(turn, 0)
                    gate_logits(turn * 2 - 1, 1)
                    transpose_norm(turn, 1)
                    gate_logits(turn * 2, 0)
                gate_logits(STEPS - 1, 1)
                pe.wait_ge(route_step, CHOSEN)
                pe.matmul(ps_l[:, 0:TILES * NE], tri[:], chosen[:], start=True, stop=True)
                pe.matmul(ps_l[:, TILES * NE:2 * TILES * NE], ones[:], chosen[:], start=True, stop=True) \
                    .then_inc(counts_in_psum, 1)

                def transpose_x(n, u):
                    pe.wait_ge(xs_loaded[u], (n - u) * (16 // UNROLL) + 16)
                    if not (isinstance(n, int) and n < 2):
                        pe.wait_ge(xst_ready, 1 + n - 1)
                    for k in range(KT):
                        mm = pe.transpose(ps_t[:, u % 2, k * P:(k + 1) * P], xs[:, u, k * P:(k + 1) * P], ident[:])
                    mm.then_inc(xst_in_psum, 1)

                def hidden(n, u, e):
                    pe.wait_ge(xst_ready, 1 + n + 1)
                    if not (isinstance(n, int) and n < 2):
                        pe.wait_ge(act_ready, 1 + n - 1)
                    for k in range(KT):
                        mm = pe.matmul(ps_h[:, u % 2, :], xst[:, u % 2, k, :], w1[:, :, k, :][:, bass.ds(e, 1), :],
                                       start=(k == 0), stop=(k == KT - 1))
                    mm.then_inc(h_in_psum, 1)

                def transpose_act(n, u):
                    pe.wait_ge(act_ready, 1 + n + 1)
                    pe.wait_ge(act_t_ready, 1 + n)
                    for k in range(KT):
                        mm = pe.transpose(ps_a[:, k * P:(k + 1) * P], act_in[:, u % 2, k * P:(k + 1) * P], ident[:])
                    mm.then_inc(act_t_in_psum, 1)

                def output(n, u, e):
                    pe.wait_ge(act_t_ready, 1 + n + 1)
                    if not (isinstance(n, int) and n < 2):
                        pe.wait_ge(ys_ready, 1 + n - 1)
                    for k in range(KT):
                        mm = pe.matmul(ps_o[:, u % 2, 0:C], act_t[:, u % 2, k, :], w2[:, :, k, :][:, bass.ds(e, 1), :],
                                       start=(k == 0), stop=(k == KT - 1))
                    mm.then_inc(y_in_psum, 1)

                def turn_of_loop(turn):
                    first, last = (isinstance(turn, int) and turn == t for t in (0, HALVES * TURNS - 1))
                    digits = pe.value_load(experts_of[0:1, bass.ds(turn, 1)], min_val=0, max_val=NE ** (LAG + UNROLL) - 1)

                    def expert(u):
                        return pe.snap((digits >> (DIGIT * (LAG + u))) & (NE - 1), min_val=0, max_val=NE - 1)

                    for u in range(UNROLL):
                        n = turn * UNROLL + u
                        hidden(n, u, expert(u))
                        if not first or u >= 1:
                            transpose_act(n - 1, (u - 1) % UNROLL)
                        if not last or u + 2 < UNROLL:
                            transpose_x(n + 2, (u + 2) % UNROLL)
                        if not first or u >= LAG:
                            output(n - LAG, (u - LAG) % UNROLL, expert(u - LAG))
                    if last:
                        transpose_act(NTILES - 1, UNROLL - 1)
                        for u in range(UNROLL - LAG, UNROLL):
                            output(turn * UNROLL + u, u, expert(u))

                pe.wait_ge(weights_loaded, 16 * len(weights))
                pe.wait_ge(route_step, EXPERTS_OF)
                transpose_x(0, 0)
                transpose_x(1, 1)
                turn_of_loop(0)
                with pe.Fori(1, HALVES * TURNS - 1) as turn:
                    turn_of_loop(turn)
                turn_of_loop(HALVES * TURNS - 1)

            @block.vector
            def _(dve):
                def each(ap, n=NE):
                    return ap.unsqueeze(2).to_broadcast([P, TILES, n])

                ranks = rank_of[:].unsqueeze(1).to_broadcast([P, TILES, NE])
                with dve.Fori(0, STEPS) as g:
                    for j in range(UNROLL):
                        dve.bn_stats(stats[:, j:, :][:, bass.ds(g * UNROLL, 1), :], x[:, j:, :][:, bass.ds(g * UNROLL, 1), :]) \
                            .then_inc(ln_stats, 1)
                dve.wait_ge(ln_stats, TILES)
                moments(dve, stats, scratch, mean[:], vare[:], ln_moments, 0, C)
                dve.wait_ge(ln_rstd, 1)
                dve.wait_ge(consts_loaded, 16 * len(consts))
                dve.tensor_copy(tri[:], tri_f[:]).then_inc(constants_ready, 1)
                def norm(turn):
                    for h in range(2):
                        n = turn * 2 + h
                        if not isinstance(turn, int):
                            dve.wait_ge(xn_kept, n - 1)
                            dve.wait_ge(xt_in_psum, n - 1)
                        for j in range(UNROLL):
                            def tile(ap):
                                return ap[:, h * UNROLL + j:][:, bass.ds(turn * 2 * UNROLL, 1)]

                            op = dve.tensor_scalar(xn_turn[:, h, j, :], tile(x), tile(mean), tile(rstd),
                                                   ALU.subtract, ALU.mult)
                        op.then_inc(xn_ready, 1)

                norm(0)
                with dve.Fori(1, STEPS // 2) as turn:
                    norm(turn)

                def done(op):
                    op.then_inc(route_step, 1)

                dve.wait_ge(logits_in_psum, STEPS)
                dve.tensor_tensor(logits[:], ps_l[:, 0:TILES * NE].rearrange("p (i e) -> p i e", e=NE),
                                  b_gate[:].unsqueeze(1).to_broadcast([P, TILES, NE]), ALU.add).then_inc(logits_ready, 1)
                dve.wait_ge(logits_ready, 1)
                done(dve.tensor_reduce(top[:, 0, :], logits[:], AX, ALU.max))
                dve.wait_ge(route_step, TOP1)
                done(dve.tensor_tensor(hits[:], logits[:], each(top[:, 0, :]), ALU.is_equal))
                dve.wait_ge(route_step, EQ1)
                done(dve.tensor_tensor(hits[:], hits[:], ranks, ALU.mult))
                dve.wait_ge(route_step, RANK1)
                done(dve.tensor_reduce(best[:, 0, :], hits[:], AX, ALU.max))
                dve.wait_ge(route_step, BEST1)
                done(dve.tensor_tensor(first[:], ranks, each(best[:, 0, :]), ALU.is_equal))
                dve.wait_ge(route_step, FIRST)
                done(dve.scalar_tensor_tensor(rest[:], first[:], -3.0e38, logits[:], ALU.mult, ALU.add))
                dve.wait_ge(route_step, REST)
                done(dve.tensor_reduce(top[:, 1, :], rest[:], AX, ALU.max))
                dve.wait_ge(route_step, TOP2)
                done(dve.tensor_tensor(hits[:], rest[:], each(top[:, 1, :]), ALU.is_equal))
                dve.wait_ge(route_step, EQ2)
                done(dve.tensor_tensor(hits[:], hits[:], ranks, ALU.mult))
                dve.wait_ge(route_step, RANK2)
                done(dve.tensor_reduce(best[:, 1, :], hits[:], AX, ALU.max))
                dve.wait_ge(route_step, BEST2)
                done(dve.tensor_tensor(second[:], ranks, each(best[:, 1, :]), ALU.is_equal))
                done(dve.tensor_tensor(gap[:], top[:, 1, :], top[:, 0, :], ALU.subtract))
                dve.wait_ge(route_step, SECOND)
                done(dve.tensor_tensor(chosen[:], first[:], second[:], ALU.add))
                dve.wait_ge(odds_ready, 1)
                done(dve.tensor_scalar(total[:], odds[:], 1.0, None, ALU.add))
                dve.wait_ge(route_step, SUM)
                done(dve.reciprocal(weight[:, 0, :], total[:]))
                dve.wait_ge(route_step, SHARE)
                done(dve.tensor_tensor(weight[:, 1, :], weight[:, 0, :], odds[:], ALU.mult))
                dve.wait_ge(counts_in_psum, 1)
                before = ps_l[:, 0:TILES * NE].rearrange("p (i e) -> p i e", e=NE)
                counts = ps_l[:, TILES * NE:2 * TILES * NE].rearrange("p (i e) -> p i e", e=NE)
                for half in range(HALVES):
                    for e in range(NE):
                        mine = slice(half * TPH, (half + 1) * TPH)
                        op = dve.tensor_tensor_scan(running[:, mine, e], ones_row[:], counts[:, mine, e], 0.0,
                                                    ALU.mult, ALU.add)
                done(op)
                dve.wait_ge(route_step, RUN)
                done(dve.tensor_tensor(slot[:], running[:], counts, ALU.subtract))
                dve.wait_ge(route_step, EXCL)
                done(dve.tensor_tensor(slot[:], slot[:], before, ALU.add))
                for half in range(HALVES):
                    op = dve.tensor_tensor(over[:, half * NE:(half + 1) * NE, :],
                                           running[:, (half + 1) * TPH - 1, :].unsqueeze(2)
                                           .to_broadcast([P, NE, TPH]),
                                           fills[:].unsqueeze(1).to_broadcast([P, NE, TPH]), ALU.is_gt)
                done(op)
                dve.wait_ge(route_step, OVER)
                done(dve.tensor_reduce(tiles_of[:].rearrange("p h e -> p (h e)"), over[:], AX, ALU.add))
                dve.wait_ge(route_step, TILES_OF)
                for half in range(HALVES):
                    op = dve.tensor_tensor_scan(tiles_end[:, half, :], ones_row[:, 0:NE], tiles_of[:, half, :], 0.0,
                                                ALU.mult, ALU.add)
                done(op)
                dve.wait_ge(route_step, TILES_END)
                done(dve.tensor_tensor(row_of[:], tiles_end[:], tiles_of[:], ALU.subtract))
                dve.wait_ge(route_step, ROW)
                done(dve.tensor_scalar(row_of[:], row_of[:], float(P), None, ALU.mult))
                dve.wait_ge(route_step, SHIFT)
                done(dve.tensor_tensor(slot[:].rearrange("p (h i) e -> p h i e", h=HALVES),
                                       slot[:].rearrange("p (h i) e -> p h i e", h=HALVES),
                                       row_of[:].unsqueeze(2).to_broadcast([P, HALVES, TPH, NE]), ALU.add))
                dve.wait_ge(route_step, PLACED)
                done(dve.tensor_tensor(hits[:], slot[:], first[:], ALU.mult))
                dve.wait_ge(route_step, HIT1)
                done(dve.tensor_reduce(place_f[:, 0, :], hits[:], AX, ALU.add))
                dve.wait_ge(route_step, POS1)
                done(dve.tensor_tensor(hits[:], slot[:], second[:], ALU.mult))
                dve.wait_ge(route_step, HIT2)
                done(dve.tensor_reduce(place_f[:, 1, :], hits[:], AX, ALU.add))
                dve.wait_ge(route_step, POS2)
                done(dve.tensor_copy(place[:], place_f[:]))
                for half in range(HALVES):
                    op = dve.tensor_tensor(passed[:, half, :, :],
                                           tiles_end[:, half, :].unsqueeze(1).to_broadcast([P, RTILES, NE]),
                                           tile_no[:].unsqueeze(2).to_broadcast([P, RTILES, NE]), ALU.is_le)
                done(op)
                dve.wait_ge(route_step, PASSED)
                done(dve.tensor_reduce(expert_f[:, LAG:].rearrange("p (h r) -> p h r", h=HALVES), passed[:], AX, ALU.add))
                dve.wait_ge(route_step, EXPERT)
                done(dve.tensor_scalar(expert_f[:, LAG:], expert_f[:, LAG:], float(NE - 1), None, ALU.min))
                for u in reversed(range(LAG + UNROLL)):
                    digits = expert_f[:, u:u + NTILES - UNROLL + 1:UNROLL]
                    if u == LAG + UNROLL - 1:
                        dve.wait_ge(constants_ready, 6)
                        dve.wait_ge(route_step, CLAMP)
                        dve.tensor_copy(experts_f[:], digits).then_inc(packing, 1)
                    else:
                        dve.wait_ge(packing, LAG + UNROLL - 1 - u)
                        dve.scalar_tensor_tensor(experts_f[:], experts_f[:], float(NE), digits, ALU.mult, ALU.add) \
                            .then_inc(packing, 1)
                dve.wait_ge(packing, LAG + UNROLL)
                done(dve.tensor_copy(experts_of[:], experts_f[:]))

                def gate(n, u):
                    dve.wait_ge(silu_ready, n + 1)
                    dve.tensor_tensor(act_in[:, u % 2, :], silu_g[:, u % 2, :], ps_h[:, u % 2, FF:2 * FF], ALU.mult) \
                        .then_inc(act_ready, 1)

                def act_out(n, u):
                    dve.wait_ge(act_t_in_psum, n + 1)
                    dve.tensor_copy(act_t[:, u % 2, :, :], ps_a[:, 0:C].rearrange("p (k t) -> p k t", k=KT)) \
                        .then_inc(act_t_ready, 1)

                def combine(half):
                    for i in range(half * TPH, (half + 1) * TPH):
                        dve.wait_ge(gathered[i % 4], 16 * TOPK * (i // 4 + 1))
                        for s in range(TOPK):
                            dve.scalar_tensor_tensor(x[:, i, :], back[:, i % 4, s, :], weight[:, s, i:i + 1],
                                                     x[:, i, :], ALU.mult, ALU.add).then_inc(x_added, 1)
                            dve.wait_ge(x_added, TOPK * i + s + 1)

                with dve.Fori(0, HALVES * TURNS) as turn:
                    for u in range(UNROLL):
                        gate(turn * UNROLL + u, u)
                        act_out(turn * UNROLL + u, u)
                for half in range(HALVES):
                    combine(half)


NMIX = 5
LORA = 32
LORA_D = 64
TC = 512
CT = TC // P
CPB = T // TC
CHUNKS = B * CPB
SCANS = KT * HD


def recurrence(nc, d, x, name="rec"):
    with ExitStack() as ctx:
        def sb(n, shape, dt=F32):
            return ctx.enter_context(nc.sbuf_tensor(f"{name}_{n}", shape, dt))

        def ps(n, shape):
            return ctx.enter_context(nc.psum_tensor(f"{name}_{n}", shape, F32))

        def sem(n):
            return ctx.enter_context(nc.semaphore(f"{name}_{n}"))

        ident = sb("ident", [P, P])
        v_centre = sb("v_centre", [P, P])
        v_mean = sb("v_mean", [P, P])
        k_to_v = sb("k_to_v", [P, P])
        collect = sb("collect", [P, HD, P])
        spread_f = sb("spread_f", [P, 4, P])
        spread = sb("spread", [P, 4, P], BF16)
        maa_x = sb("maa_x", [P, KT])
        maa = sb("maa", [P, NMIX, KT])
        tm_w1 = sb("tm_w1", [P, KT, NMIX * LORA])
        tm_w2 = sb("tm_w2", [P, NMIX, C])
        decay = sb("decay", [P, KT])
        td_w1 = sb("td_w1", [P, KT, LORA_D])
        td_w2 = sb("td_w2", [P, C])
        bonus = sb("bonus", [P, KT])
        w_of = {f: sb("w_" + f, [P, KT, C]) for f in "kvrgo"}
        ln_w = sb("ln_w", [P, KT])
        ln_b = sb("ln_b", [P, KT])
        eps = sb("eps", [P, 1])
        no_token = sb("no_token", [P, KT, 1])

        stats = sb("stats", [P, CT, 6])
        scratch = sb("scratch", [P, 3, CT])
        mean = sb("mean", [P, CT])
        vare = sb("vare", [P, CT])
        expo = sb("expo", [P, CT])
        rstd = sb("rstd", [P, CT])
        xn = sb("xn", [P, CT, C])
        xnt = sb("xnt", [P, KT, TC + 1])
        sx = sb("sx", [P, KT, TC])
        mixed = sb("mixed", [P, 2, KT, TC])
        hidden = sb("hidden", [P, TC])
        hidden_g = sb("hidden_g", [P, TC])
        hidden_d = sb("hidden_d", [P, TC])
        wt = [sb(f"wt{h}", [P, KT, TC + 1]) for h in range(CPB)]
        kt = [sb(f"kt{h}", [P, KT, TC]) for h in range(CPB)]
        rt = [sb(f"rt{h}", [P, KT, TC]) for h in range(CPB)]
        silu_g = [sb(f"silu_g{h}", [P, KT, TC]) for h in range(CPB)]
        v_rows = [sb(f"v_rows{h}", [P, KT, 4, TC], BF16) for h in range(CPB)]
        vt = sb("vt", [P, KT, TC])
        v_part = [sb(f"v_part{i}", [P, KT, TC], BF16) for i in range(3)]
        v_rest = sb("v_rest", [P, KT, TC])
        rku = sb("rku", [P, KT, TC])
        y_bonus = sb("y_bonus", [P, KT, TC])
        add = [sb(f"add{n}", [P, TC + 1]) for n in range(4)]
        state = [sb(f"state{n}", [P, TC + 1]) for n in range(4)]
        carry = sb("carry", [P, SCANS])
        read = [sb(f"read{n}", [P, TC]) for n in range(4)]
        square = sb("square", [P, TC])
        log_var = sb("log_var", [P, TC])
        y_rstd = sb("y_rstd", [P, TC])
        gated = sb("gated", [P, KT, TC])

        ps_v = ps("ps_v", [P, 2, BANK])
        ps_y = ps("ps_y", [P, KT, BANK])
        ps_m = ps("ps_m", [P, 4, BANK])

        loaded = sem("loaded")
        zeroed = sem("zeroed")
        constants_ready = sem("constants_ready")
        ln_stats = sem("ln_stats")
        ln_moments = sem("ln_moments")
        ln_rstd = sem("ln_rstd")
        xn_ready = sem("xn_ready")
        xt_in_psum = sem("xt_in_psum")
        first_column = sem("first_column")
        xnt_ready = sem("xnt_ready")
        sx_ready = sem("sx_ready")
        mixed_x_ready = sem("mixed_x_ready")
        hidden_in_psum = sem("hidden_in_psum")
        hidden_ready = sem("hidden_ready")
        delta_in_psum = sem("delta_in_psum")
        mix_scaled = sem("mix_scaled")
        mix_ready = sem("mix_ready")
        linear_in_psum = sem("linear_in_psum")
        linear_out = sem("linear_out")
        decay_ready = sem("decay_ready")
        v_split = sem("v_split")
        v_rows_loaded = sem("v_rows_loaded")
        rku_ready = sem("rku_ready")
        bonus_in_psum = sem("bonus_in_psum")
        y_bonus_ready = sem("y_bonus_ready")
        v_in_psum = sem("v_in_psum")
        add_ready = sem("add_ready")
        state_ready = sem("state_ready")
        carried = sem("carried")
        read_ready = sem("read_ready")
        y_in_psum = sem("y_in_psum")
        square_ready = sem("square_ready")
        var_in_psum = sem("var_in_psum")
        log_ready = sem("log_ready")
        y_rstd_ready = sem("y_rstd_ready")
        normed = sem("normed")
        gated_ready = sem("gated_ready")
        out_in_psum = sem("out_in_psum")
        x_added = sem("x_added")

        consts = [(ident[:], "ident"), (v_centre[:], "v_centre"), (v_mean[:], "v_mean"), (k_to_v[:], "k_to_v"),
                  (collect[:], "collect"), (spread_f[:], "spread"), (maa_x[:], "b_maa_x"), (maa[:], "b_maa"),
                  (tm_w1[:], "b_tm_w1"), (decay[:], "b_decay"), (td_w1[:], "b_td_w1"), (bonus[:], "b_bonus"),
                  (ln_w[:], "b_ln_w"), (ln_b[:], "b_ln_b")] + [(w_of[f][:], "b_w_" + f) for f in "kvrgo"]
        N_CONSTS = len(consts) + NMIX + 1
        N_ZEROED = 14
        W, K, V, R, G = range(NMIX)
        D_HID, D_0, D_1, K_0, K_1, V_0, V_1, R_0, R_1, G_0, G_1 = range(1, 12)
        LINEARS = 11
        PARTS = ["x0", "x1", "var_last", "hid0", "hid1", "out0", "w0", "w1", "out1", "k0", "k1", "d", "v0", "v1",
                 "d0", "d1", "lk0", "lk1", "r0", "r1", "lv0", "lv1", "var", "g0", "g1", "lr0", "lr1", "lg0", "lg1",
                 "b0", "b1"]

        def bank(part):
            return ps_m[:, PARTS.index(part) % 4, :]

        def halves(turns):
            run, loop = turns
            run(-1, 1, False, True, False)
            run(0, 0, True, True, True)
            with loop(0, B - 1) as b:
                run(b, 1, True, True, False)
                run(b + 1, 0, True, True, False)
            run(B - 1, 1, True, False, False)

        with nc.Block() as block:

            @block.sync
            def _(sp):
                for tile, n in consts:
                    sp.dma_start(tile, d[n]).then_inc(loaded, 16)
                sp.wait_ge(zeroed, 2)
                for f in range(NMIX):
                    row = LORA * f % P
                    sp.dma_start(tm_w2[row:row + LORA, f, :], d["b_tm_w2"][LORA * f:LORA * (f + 1), :]) \
                        .then_inc(loaded, 16)
                sp.dma_start(td_w2[0:LORA_D, :], d["b_td_w2"]).then_inc(loaded, 16)
                sp.wait_ge(zeroed, 4)
                with sp.Fori(0, B) as b:
                    for h in range(CPB):
                        sp.wait_ge(v_split, (b * CPB + h + 1) * 5)
                        for part in range(3):
                            for g in range(4):
                                sp.dma_start(v_rows[h][32 * part:32 * part + 32, :, g, :],
                                             v_part[part][32 * g:32 * g + 32, :, :]).then_inc(v_rows_loaded, 16)
                sp.wait_ge(v_rows_loaded, 16 * 12 * CHUNKS)

            @block.gpsimd
            def _(pool):
                pool.memset(tm_w2[:], 0.0).then_inc(zeroed, 1)
                pool.memset(td_w2[:], 0.0).then_inc(zeroed, 1)
                for h in range(CPB):
                    pool.memset(v_rows[h][:], 0.0).then_inc(zeroed, 1)
                pool.memset(hidden_g[:], 0.0).then_inc(zeroed, 1)
                pool.memset(hidden_d[:], 0.0).then_inc(zeroed, 1)
                pool.memset(no_token[:], 0.0).then_inc(zeroed, 1)
                pool.memset(expo[:], -0.5).then_inc(zeroed, 1)
                pool.memset(eps[:], EPS).then_inc(zeroed, 1)
                for n in range(4):
                    pool.memset(add[n][:, 0:1], 0.0).then_inc(zeroed, 1)
                for h in range(CPB):
                    op = pool.memset(wt[h][:, :, 0:1], 1.0)
                op.then_inc(zeroed, 1)
                pool.wait_ge(zeroed, N_ZEROED)

                def mix(nxt, f):
                    for k in range(KT):
                        pool.wait_ge(mix_scaled, nxt * NMIX * KT + f * KT + k + 1)
                        pool.tensor_tensor(mixed[:, f % 2, k, :], mixed[:, f % 2, k, :], xnt[:, k, 1:TC + 1], ALU.add) \
                            .then_inc(mix_ready, 1)

                def run(batch, h, scan, maps, first):
                    c = batch * CPB + h
                    for m in range(SCANS):
                        if scan:
                            pool.wait_ge(state_ready, c * SCANS + m + 1)
                            if m == 0:
                                pool.wait_ge(linear_out, c * LINEARS + R_1)
                            if m >= 4 or not first:
                                pool.wait_ge(y_in_psum, c * SCANS + m - 3)
                            pool.tensor_tensor(read[m % 4][:], rt[h][:, m // HD, :], state[m % 4][:, 0:TC], ALU.mult) \
                                .then_inc(read_ready, 1)
                        if maps:
                            if m == 0:
                                pool.wait_ge(ln_moments, (c + 2) * MOMENT_STEPS)
                                pool.tensor_tensor(rstd[:], vare[:], expo[:], ALU.pow).then_inc(ln_rstd, 1)
                            if m == 9:
                                mix(c + 1, W)
                            if m == 11:
                                mix(c + 1, K)
                            if m == 13:
                                mix(c + 1, V)
                            if m == 17:
                                mix(c + 1, R)
                            if m == 23:
                                mix(c + 1, G)

                halves((run, pool.Fori))

            @block.scalar
            def _(act):
                act.wait_ge(loaded, 16 * N_CONSTS)
                act.activation(spread[:], spread_f[:], ACT.Copy).then_inc(constants_ready, 1)
                act.wait_ge(zeroed, N_ZEROED)

                def squares(c, k):
                    act.wait_ge(y_in_psum, c * SCANS + (k + 1) * HD)
                    act.activation(square[:], ps_y[:, k, :], ACT.Square).then_inc(square_ready, 1)

                def root(c, k):
                    act.wait_ge(var_in_psum, c * KT + k + 1)
                    act.activation(log_var[:], bank("var" if k == 0 else "var_last"), ACT.Ln, bias=eps[:]) \
                        .then_inc(log_ready, 1)
                    act.wait_ge(log_ready, c * KT + k + 1)
                    if not (isinstance(c, int) and c == 0 and k == 0):
                        act.wait_ge(normed, c * KT + k)
                    act.activation(y_rstd[:], log_var[:], ACT.Exp, scale=-0.5).then_inc(y_rstd_ready, 1)

                def out(nxt, which, tile, part, fn=ACT.Copy, bias=0.0):
                    act.wait_ge(linear_in_psum, nxt * LINEARS + which)
                    act.activation(tile, bank(part), fn, bias=bias).then_inc(linear_out, 1)

                def run(batch, h, scan, maps, first):
                    c = batch * CPB + h
                    q = 1 - h
                    nxt = c + 1
                    for m in range(SCANS):
                        if scan and h == 0:
                            act.wait_ge(state_ready, c * SCANS + m + 1)
                            act.activation(carry[:, m:m + 1], state[m % 4][:, TC:TC + 1], ACT.Copy).then_inc(carried, 1)
                        if scan and m == 1 and not first:
                            squares(c - 1, 1)
                        if scan and m == 3 and not first:
                            root(c - 1, 1)
                        if scan and m == 17:
                            squares(c, 0)
                        if scan and m == 20:
                            root(c, 0)
                        if not maps:
                            continue
                        if m == 2:
                            last = xnt[:, :, TC:TC + 1] if q == 1 else no_token[:]
                            act.wait_ge(xt_in_psum, nxt * 2 + 1)
                            act.activation(xnt[:, :, 0:1], last, ACT.Copy).then_inc(first_column, 1)
                            act.wait_ge(first_column, nxt + 1)
                            for i in range(2):
                                act.wait_ge(xt_in_psum, nxt * 2 + i + 1)
                                act.activation(xnt[:, :, 1 + i * C:1 + (i + 1) * C],
                                               bank(f"x{i}").rearrange("p (k t) -> p k t", k=KT), ACT.Copy) \
                                    .then_inc(xnt_ready, 1)
                        if m == 5:
                            act.wait_ge(hidden_in_psum, nxt * 2 + 1)
                            act.activation(hidden[:], bank("hid0"), ACT.Tanh).then_inc(hidden_ready, 1)
                        if m == 6:
                            act.wait_ge(hidden_in_psum, nxt * 2 + 2)
                            act.activation(hidden_g[0:LORA, :], bank("hid1")[0:LORA, :], ACT.Tanh).then_inc(hidden_ready, 1)
                        if m == 11:
                            act.wait_ge(linear_in_psum, nxt * LINEARS + D_HID)
                            act.activation(hidden_d[0:LORA_D, :], bank("d")[0:LORA_D, :], ACT.Tanh).then_inc(linear_out, 1)
                        if m == 13:
                            for k in range(KT):
                                out(nxt, D_0 + k, wt[q][:, k, 1:TC + 1], f"d{k}", ACT.Exp, decay[:, k:k + 1])
                        if m == 14:
                            act.wait_ge(linear_out, nxt * LINEARS + D_1)
                            act.activation(wt[q][:, :, 1:TC + 1], wt[q][:, :, 1:TC + 1], ACT.Exp, scale=-1.0) \
                                .then_inc(decay_ready, 1)
                        if m in (14, 15):
                            out(nxt, K_0 + m - 14, kt[q][:, m - 14, :], f"lk{m - 14}")
                        if m in (18, 19):
                            out(nxt, V_0 + m - 18, vt[:, m - 18, :], f"lv{m - 18}")
                        if m == 19:
                            if not (isinstance(nxt, int) and nxt == 0):
                                act.wait_ge(v_rows_loaded, nxt * 16 * 12)
                            act.wait_ge(linear_out, nxt * LINEARS + V_1)
                            act.activation(v_part[0][:], vt[:], ACT.Copy).then_inc(v_split, 1)
                        if m == 21:
                            act.wait_ge(v_split, nxt * 5 + 2)
                            act.activation(v_part[1][:], v_rest[:], ACT.Copy).then_inc(v_split, 1)
                        if m == 22:
                            act.wait_ge(v_split, nxt * 5 + 4)
                            act.activation(v_part[2][:], v_rest[:], ACT.Copy).then_inc(v_split, 1)
                        if m in (23, 24):
                            out(nxt, R_0 + m - 23, rt[q][:, m - 23, :], f"lr{m - 23}")
                        if m in (25, 26):
                            out(nxt, G_0 + m - 25, silu_g[q][:, m - 25, :], f"lg{m - 25}", ACT.Silu)

                halves((run, act.Fori))
                squares(CHUNKS - 1, 1)
                root(CHUNKS - 1, 1)

            @block.tensor
            def _(pe):
                pe.wait_ge(loaded, 16 * N_CONSTS)
                pe.wait_ge(constants_ready, 1)
                pe.wait_ge(zeroed, N_ZEROED)

                def spread_v(c, h, m, first):
                    if m == 0:
                        pe.wait_ge(v_rows_loaded, (c + 1) * 16 * 12)
                    if m >= 2 or not first:
                        pe.wait_ge(add_ready, c * SCANS + m - 1)
                    pe.matmul(ps_v[:, m % 2, :], spread[:, m % 4, :], v_rows[h][:, m // HD, m % HD // 4, :],
                              start=True, stop=True).then_inc(v_in_psum, 1)

                def sum_keys(c, m):
                    pe.wait_ge(read_ready, c * SCANS + m + 1)
                    pe.matmul(ps_y[:, m // HD, :], collect[:, m % HD, :], read[m % 4][:], start=False,
                              stop=(m % HD == HD - 1)).then_inc(y_in_psum, 1)

                def begin_y(c, k, first):
                    pe.wait_ge(y_bonus_ready, c * KT + k + 1)
                    if not first:
                        pe.wait_ge(normed, (c - 1) * KT + k + 1)
                    pe.matmul(ps_y[:, k, :], v_centre[:], y_bonus[:, k, :], start=True, stop=False)

                def variance(c, k):
                    pe.wait_ge(square_ready, c * KT + k + 1)
                    pe.matmul(bank("var" if k == 0 else "var_last"), v_mean[:], square[:], start=True, stop=True) \
                        .then_inc(var_in_psum, 1)

                def output(c, i):
                    pe.wait_ge(gated_ready, (c + 1) * KT)
                    for t in range(2):
                        for k in range(KT):
                            mm = pe.matmul(bank(f"out{i}")[:, t * C:(t + 1) * C],
                                           gated[:, k, (2 * i + t) * P:(2 * i + t + 1) * P], w_of["o"][:, k, :],
                                           start=(k == 0), stop=(k == KT - 1))
                    mm.then_inc(out_in_psum, 1)

                def delta(nxt, f, part, left, count):
                    for k in range(KT):
                        pe.wait_ge(left[k], count[k])
                        pe.matmul(bank(f"{part}{k}"), tm_w2[:, f, k * P:(k + 1) * P], (hidden if f < G else hidden_g)[:],
                                  start=True, stop=True).then_inc(delta_in_psum, 1)

                def linear(nxt, w, src, part, m0, m1, signal):
                    for k in range(KT):
                        mm = pe.matmul(bank(part)[0:m1 - m0, :], w[:, k, m0:m1], src[:, k, :], start=(k == 0),
                                       stop=(k == KT - 1))
                    mm.then_inc(signal, 1)

                def run(batch, h, scan, maps, first):
                    c = batch * CPB + h
                    q = 1 - h
                    nxt = c + 1
                    start = isinstance(nxt, int) and nxt == 0

                    def scaled(n):
                        return nxt * NMIX * KT + n

                    def left(which):
                        return nxt * LINEARS + which

                    for m in range(SCANS):
                        if scan:
                            if m + 2 < SCANS:
                                spread_v(c, h, m + 2, first)
                            if m in (1, HD + 1):
                                begin_y(c, m // HD, first)
                        if maps and m + 2 >= SCANS:
                            spread_v(nxt, q, m + 2 - SCANS, start)
                        if scan and not first:
                            if m == 3:
                                pe.wait_ge(y_bonus_ready, nxt * KT)
                                variance(c - 1, 1)
                            if m == 7:
                                pe.wait_ge(y_bonus_ready, nxt * KT)
                                if maps:
                                    pe.wait_ge(xnt_ready, nxt * 2 + 2)
                                output(c - 1, 0)
                            if m == 9:
                                if maps:
                                    pe.wait_ge(hidden_ready, nxt * 2 + 2)
                                else:
                                    pe.wait_ge(linear_out, left(0))
                                output(c - 1, 1)
                        if scan and m == 20:
                            if maps:
                                pe.wait_ge(mix_scaled, scaled(7))
                            else:
                                pe.wait_ge(y_rstd_ready, c * KT)
                            variance(c, 0)
                        if maps:
                            if m == 2:
                                for i in range(2):
                                    pe.wait_ge(xn_ready, nxt * CT + 2 * (i + 1))
                                    if not start:
                                        if i == 0:
                                            pe.wait_ge(linear_out, left(0))
                                        pe.wait_ge(y_bonus_ready, c * KT + 1)
                                    for t in range(2):
                                        for k in range(KT):
                                            mm = pe.transpose(bank(f"x{i}")[:, k * C + t * P:k * C + (t + 1) * P],
                                                              xn[:, 2 * i + t, k * P:(k + 1) * P], ident[:])
                                    mm.then_inc(xt_in_psum, 1)
                            if m == 5:
                                pe.wait_ge(mixed_x_ready, nxt * KT + KT)
                                linear(nxt, tm_w1, mixed[:, 0], "hid0", 0, P, hidden_in_psum)
                            if m == 6:
                                pe.wait_ge(xnt_ready, nxt * 2 + 1)
                                linear(nxt, tm_w1, mixed[:, 0], "hid1", P, P + LORA, hidden_in_psum)
                            if m == 8:
                                pe.wait_ge(hidden_ready, nxt * 2 + 1)
                                if scan and not first:
                                    pe.wait_ge(y_rstd_ready, c * KT)
                                delta(nxt, W, "w", (hidden_ready, hidden_ready), (nxt * 2 + 1, nxt * 2 + 1))
                            if m == 10:
                                if scan and not first:
                                    pe.wait_ge(x_added, c * 2 - 1)
                                delta(nxt, K, "k", (xnt_ready, mix_scaled), (nxt * 2 + 2, scaled(1)))
                            if m == 11:
                                pe.wait_ge(mix_ready, scaled((W + 1) * KT))
                                linear(nxt, td_w1, mixed[:, W % 2], "d", 0, LORA_D, linear_in_psum)
                            if m == 12:
                                if scan and not first:
                                    pe.wait_ge(x_added, c * 2)
                                delta(nxt, V, "v", (hidden_ready, mix_scaled), (nxt * 2 + 2, scaled(3)))
                            if m == 13:
                                pe.wait_ge(mix_scaled, scaled(4))
                                pe.wait_ge(linear_out, left(D_HID))
                                for k in range(KT):
                                    pe.matmul(bank(f"d{k}"), td_w2[:, k * P:(k + 1) * P], hidden_d[:], start=True,
                                              stop=True).then_inc(linear_in_psum, 1)
                            if m in (14, 15):
                                k = m - 14
                                pe.wait_ge(mix_ready, scaled((K + 1) * KT))
                                pe.wait_ge(mix_scaled, scaled(5 + k))
                                linear(nxt, w_of["k"], mixed[:, K % 2], f"lk{k}", k * P, (k + 1) * P, linear_in_psum)
                            if m == 16:
                                delta(nxt, R, "r", (linear_out, linear_out), (left(D_0), left(D_1)))
                            if m in (18, 19):
                                k = m - 18
                                pe.wait_ge(mix_ready, scaled((V + 1) * KT))
                                pe.wait_ge(linear_out, left(K_0 + k))
                                linear(nxt, w_of["v"], mixed[:, V % 2], f"lv{k}", k * P, (k + 1) * P, linear_in_psum)
                            if m == 21:
                                delta(nxt, G, "g", (mix_scaled, linear_out), (scaled(8), left(V_0)))
                            if m in (23, 24):
                                k = m - 23
                                pe.wait_ge(mix_ready, scaled((R + 1) * KT))
                                pe.wait_ge(linear_out, left(V_1))
                                if k == 1 and scan:
                                    pe.wait_ge(y_rstd_ready, c * KT + 1)
                                linear(nxt, w_of["r"], mixed[:, R % 2], f"lr{k}", k * P, (k + 1) * P, linear_in_psum)
                            if m in (25, 26):
                                k = m - 25
                                pe.wait_ge(mix_ready, scaled((G + 1) * KT))
                                pe.wait_ge(mix_scaled, scaled(9 + k))
                                linear(nxt, w_of["g"], mixed[:, G % 2], f"lg{k}", k * P, (k + 1) * P, linear_in_psum)
                            if m == 28:
                                for k in range(KT):
                                    pe.wait_ge(rku_ready, nxt * KT + k + 1)
                                    pe.wait_ge(linear_out, left(R_0 + k))
                                    pe.matmul(bank(f"b{k}"), k_to_v[:], rku[:, k, :], start=True, stop=True) \
                                        .then_inc(bonus_in_psum, 1)
                        if scan and m >= 2:
                            sum_keys(c, m - 2)
                        elif scan and not first:
                            sum_keys(c - 1, SCANS + m - 2)

                halves((run, pe.Fori))
                for m in range(SCANS - 2, SCANS):
                    sum_keys(CHUNKS - 1, m)
                pe.wait_ge(y_rstd_ready, CHUNKS * KT - 1)
                variance(CHUNKS - 1, 1)
                for i in range(2):
                    pe.wait_ge(x_added, (CHUNKS - 1) * 2)
                    output(CHUNKS - 1, i)

            @block.vector
            def _(dve):
                dve.wait_ge(loaded, 16 * N_CONSTS)
                dve.wait_ge(zeroed, N_ZEROED)

                def add_v(c, h, m, first):
                    if m == 0:
                        dve.wait_ge(linear_out, c * LINEARS + K_1)
                    dve.wait_ge(v_in_psum, c * SCANS + m + 1)
                    if m >= 4 or not first:
                        dve.wait_ge(state_ready, c * SCANS + m - 3)
                    dve.tensor_tensor(add[m % 4][:, 1:TC + 1], ps_v[:, m % 2, :], kt[h][:, m // HD, :], ALU.mult) \
                        .then_inc(add_ready, 1)

                def norm_y(c, h, k):
                    dve.wait_ge(y_rstd_ready, c * KT + k + 1)
                    dve.scalar_tensor_tensor(gated[:, k, :], ps_y[:, k, :], ln_w[:, k:k + 1], y_rstd[:], ALU.mult, ALU.mult) \
                        .then_inc(normed, 1)
                    dve.wait_ge(normed, c * KT + k + 1)
                    dve.scalar_tensor_tensor(gated[:, k, :], gated[:, k, :], ln_b[:, k:k + 1], silu_g[h][:, k, :],
                                             ALU.add, ALU.mult).then_inc(gated_ready, 1)

                def add_out(c, i):
                    dve.wait_ge(out_in_psum, c * 2 + i + 1)
                    two = x[:, 2 * i:, :][:, bass.ds(c * CT, 2), :]
                    dve.tensor_tensor(two, two, bank(f"out{i}").rearrange("p (t c) -> p t c", t=2), ALU.add) \
                        .then_inc(x_added, 1)

                def mix(nxt, f, part):
                    if f >= 2:
                        dve.wait_ge(linear_in_psum, nxt * LINEARS + (D_HID, K_1, V_1)[f - 2])
                    for k in range(KT):
                        dve.wait_ge(delta_in_psum, nxt * NMIX * KT + f * KT + k + 1)
                        dve.scalar_tensor_tensor(mixed[:, f % 2, k, :], bank(f"{part}{k}"), maa[:, f, k:k + 1], sx[:, k, :],
                                                 ALU.add, ALU.mult).then_inc(mix_scaled, 1)

                def run(batch, h, scan, maps, first):
                    c = batch * CPB + h
                    q = 1 - h
                    nxt = c + 1
                    for m in range(SCANS):
                        if scan:
                            if m + 1 < SCANS:
                                add_v(c, h, m + 1, first)
                            if m == 0:
                                dve.wait_ge(decay_ready, c + 1)
                            dve.wait_ge(add_ready, c * SCANS + m + 1)
                            if m >= 4 or not first:
                                dve.wait_ge(read_ready, c * SCANS + m - 3)
                            if h == 0 and m >= 4:
                                dve.wait_ge(carried, batch * SCANS + m - 3)
                            if h == 1 and m < 4:
                                dve.wait_ge(carried, (batch + 1) * SCANS)
                            dve.tensor_tensor_scan(state[m % 4][:], wt[h][:, m // HD, :], add[m % 4][:],
                                                   carry[:, m:m + 1] if h == 1 else 0.0, ALU.mult, ALU.add) \
                                .then_inc(state_ready, 1)
                            if m == 5 and not first:
                                norm_y(c - 1, q, 1)
                            if m == 8 and not first:
                                add_out(c - 1, 0)
                            if m == 10 and not first:
                                add_out(c - 1, 1)
                            if m == 22:
                                if not first:
                                    dve.wait_ge(out_in_psum, c * 2)
                                norm_y(c, h, 0)
                        if not maps:
                            continue
                        if m == 0:
                            for i in range(CT):
                                dve.bn_stats(stats[:, i, :], x[:, i:, :][:, bass.ds(nxt * CT, 1), :]).then_inc(ln_stats, 1)
                            dve.wait_ge(ln_stats, (nxt + 1) * CT)
                            moments(dve, stats, scratch, mean[:], vare[:], ln_moments, nxt * MOMENT_STEPS, C)
                        if m == 1:
                            dve.wait_ge(ln_rstd, nxt + 1)
                            for i in range(CT):
                                dve.tensor_scalar(xn[:, i, :], x[:, i:, :][:, bass.ds(nxt * CT, 1), :], mean[:, i:i + 1],
                                                  rstd[:, i:i + 1], ALU.subtract, ALU.mult).then_inc(xn_ready, 1)
                        if m == 3:
                            dve.wait_ge(xnt_ready, (nxt + 1) * 2)
                            dve.tensor_tensor(sx[:], xnt[:, :, 0:TC], xnt[:, :, 1:TC + 1], ALU.subtract).then_inc(sx_ready, 1)
                        if m == 4:
                            dve.wait_ge(sx_ready, nxt + 1)
                            for k in range(KT):
                                dve.scalar_tensor_tensor(mixed[:, 0, k, :], sx[:, k, :], maa_x[:, k:k + 1],
                                                         xnt[:, k, 1:TC + 1], ALU.mult, ALU.add).then_inc(mixed_x_ready, 1)
                        if m == 9:
                            mix(nxt, W, "w")
                        if m == 11:
                            mix(nxt, K, "k")
                        if m == 13:
                            mix(nxt, V, "v")
                        if m == 17:
                            mix(nxt, R, "r")
                        if m in (20, 21):
                            n = m - 20
                            dve.wait_ge(v_split, nxt * 5 + 1 + 2 * n)
                            dve.tensor_tensor(v_rest[:], (vt, v_rest)[n][:], v_part[n][:], ALU.subtract).then_inc(v_split, 1)
                        if m == 23:
                            mix(nxt, G, "g")
                        if m == 26:
                            dve.wait_ge(linear_out, nxt * LINEARS + R_1)
                            for k in range(KT):
                                dve.scalar_tensor_tensor(rku[:, k, :], rt[q][:, k, :], bonus[:, k:k + 1], kt[q][:, k, :],
                                                         ALU.mult, ALU.mult).then_inc(rku_ready, 1)
                        if m == 29:
                            for k in range(KT):
                                dve.wait_ge(bonus_in_psum, nxt * KT + k + 1)
                                dve.tensor_tensor(y_bonus[:, k, :], bank(f"b{k}"), vt[:, k, :], ALU.mult) \
                                    .then_inc(y_bonus_ready, 1)
                        if m == SCANS - 1:
                            add_v(nxt, q, 0, not scan)

                halves((run, dve.Fori))
                dve.wait_ge(out_in_psum, (CHUNKS - 1) * 2)
                norm_y(CHUNKS - 1, 1, 1)
                for i in range(2):
                    add_out(CHUNKS - 1, i)
                dve.wait_ge(x_added, CHUNKS * 2)


def _shape_constants():
    import numpy as np
    f = np.float32
    half = np.arange(0, HD, 2, dtype=f)
    inv_freq = (f(1.0) / f(10000.0) ** (half / f(HD))).astype(f)
    t = np.arange(T, dtype=f)
    freqs = np.repeat((t[:, None] * inv_freq[None, :]).astype(f), 2, axis=1)
    scale_vec = (half + f(0.4 * HD)) / f(1.4 * HD)
    power = (t - T // 2) / f(512.0)
    scale = np.repeat(scale_vec[None, :].astype(np.float64) ** power[:, None], 2, axis=1)
    cos, sin = np.cos(freqs).astype(np.float64), np.sin(freqs).astype(np.float64)
    sin[:, 0::2] *= -1.0
    gamma = (f(1.0) - f(2.0) ** (f(-5.0) - np.arange(NH, dtype=f))).astype(np.float64)
    decay = gamma[None, :, None] ** np.arange(T, dtype=np.float64)[:, None, None]
    both = []
    for wave in (cos, sin):
        q = decay * (wave * scale)[:, None, :] * HD ** -0.5
        k = (wave / scale)[:, None, :] / decay
        table = np.concatenate([q.reshape(T, C), k.reshape(T, C)], axis=1)
        both.append(np.ascontiguousarray(table.reshape(TPB, P, 2 * C).transpose(1, 0, 2)).astype(f))
    i = np.arange(P)
    head = i // HD
    same = (head[:, None] == head[None, :]).astype(f)
    vrow_v, vrow_h = i // HPT, i % HPT
    vsame = (vrow_h[:, None] == vrow_h[None, :]).astype(f)
    k_to_v = (head[:, None] == vrow_h[None, :]).astype(f)
    pick = (vrow_v[None, :] == np.arange(HD)[:, None]).astype(f)
    collect = (k_to_v[:, None, :] * (pick[None, :, :] - f(1.0 / HD))).astype(f)
    spread = np.zeros((P, 4, P), f)
    for part in range(3):
        for jj in range(4):
            for h in range(HPT):
                spread[part * 32 + jj * HPT + h, jj, h * HD:(h + 1) * HD] = 1.0
    tri = (i[:, None] < i[None, :]).astype(f)
    return {
        "rope_cos": both[0], "rope_sin": both[1], "ident": np.eye(P, dtype=f),
        "causal": (i[None, :] >= i[:, None]).astype(f),
        "head_of": (head[:, None] == np.arange(HPT)[None, :]).astype(f),
        "same_head": same, "head_mean": (same / f(HD)).astype(f),
        "v_centre": (vsame * (np.eye(P, dtype=f) * 0 + (vrow_v[:, None] == vrow_v[None, :]) - f(1.0 / HD))).astype(f),
        "v_mean": (vsame / f(HD)).astype(f), "k_to_v": k_to_v, "collect": collect, "spread": spread,
        "tri": tri, "ones": np.ones((P, P), f),
    }


def _laid_out(i):
    import numpy as np
    i = {k: np.asarray(v) for k, v in i.items()}

    def rows(w):
        return w.reshape(-1, P, w.shape[1]).transpose(1, 0, 2)

    def column(w):
        return w.reshape(-1, P).T

    def by_value(w, axis):
        s = w.shape
        w = w.reshape(*s[:axis], KT, HPT, HD, *s[axis + 1:])
        return np.swapaxes(w, axis + 1, axis + 2).reshape(s)

    w_qkv = i["L0_attn_a_w_qkv"]
    b = {k.removeprefix("L0_attn_b_"): v for k, v in i.items() if k.startswith("L0_attn_b_")}
    w1, w2 = i["L0_ffn_w1"], i["L0_ffn_w2"]
    out = {
        "x": i["L0_attn_a_x"].reshape(TILES, P, C).transpose(1, 0, 2),
        "a_w_qk": rows(w_qkv[:2 * C].T), "a_w_v": rows(w_qkv[2 * C:].T),
        "a_w_gate": rows(i["L0_attn_a_w_gated"].T), "a_w_proj": rows(i["L0_attn_a_w_proj"].T),
        "a_gn_w": column(i["L0_attn_a_gn_weight"]), "a_gn_b": column(i["L0_attn_a_gn_bias"]),
        "f_w_gate": rows(i["L0_ffn_Wg"].T), "f_b_gate": np.broadcast_to(i["L0_ffn_bg"], (P, NE)),
        "f_w1": w1.transpose(2, 0, 1).reshape(KT, P, NE, 2 * FF).transpose(1, 2, 0, 3),
        "f_w2": w2.transpose(2, 0, 1).reshape(FF // P, P, NE, C).transpose(1, 2, 0, 3),
        "b_maa_x": column(b["time_maa_x"]),
        "b_maa": b["time_maa_wkvrg"].reshape(5, KT, P).transpose(2, 0, 1),
        "b_tm_w1": rows(b["tm_w1"]),
        "b_tm_w2": b["tm_w2"].reshape(-1, C),
        "b_decay": column(b["time_decay"]), "b_td_w1": rows(b["td_w1"]), "b_td_w2": b["td_w2"],
        "b_bonus": column(b["time_faaaa"].reshape(-1)),
        "b_w_r": rows(b["Wr"]), "b_w_k": rows(b["Wk"]),
        "b_w_v": rows(by_value(b["Wv"], 1)), "b_w_g": rows(by_value(b["Wg"], 1)),
        "b_w_o": rows(by_value(b["Wo"], 0)),
        "b_ln_w": column(by_value(b["ln_w"], 0)), "b_ln_b": column(by_value(b["ln_b"], 0)),
    }
    return {k: np.ascontiguousarray(v) for k, v in out.items()}


def _route_constants():
    import numpy as np
    f = np.float32
    return {
        "rank_of": np.broadcast_to(NE - np.arange(NE, dtype=f), (P, NE)).copy(),
        "fills": np.broadcast_to(P * np.arange(TPH, dtype=f), (P, TPH)).copy(),
        "tile_no": np.broadcast_to(np.arange(RTILES, dtype=f), (P, RTILES)).copy(),
    }


_NAMES = ["L0_attn_a_x", "L0_attn_a_w_qkv", "L0_attn_a_w_gated", "L0_attn_a_w_proj", "L0_attn_a_gn_weight",
          "L0_attn_a_gn_bias", "L0_attn_b_time_maa_x", "L0_attn_b_time_maa_wkvrg", "L0_attn_b_tm_w1",
          "L0_attn_b_tm_w2", "L0_attn_b_time_decay", "L0_attn_b_td_w1", "L0_attn_b_td_w2", "L0_attn_b_time_faaaa",
          "L0_attn_b_Wr", "L0_attn_b_Wk", "L0_attn_b_Wv", "L0_attn_b_Wg", "L0_attn_b_Wo", "L0_attn_b_ln_w",
          "L0_attn_b_ln_b", "L0_ffn_Wg", "L0_ffn_bg", "L0_ffn_w1", "L0_ffn_w2"]


def program(nc, d, out):
    x_sorted = [nc.dram_tensor(f"x_sorted{h}", (ROWS, C), F32, kind="Internal").ap() for h in range(HALVES)]
    y_sorted = [nc.dram_tensor(f"y_sorted{h}", (ROWS, C), F32, kind="Internal").ap() for h in range(HALVES)]
    with ExitStack() as ctx:
        x = ctx.enter_context(nc.sbuf_tensor("x", [P, TILES, C], F32))
        x_loaded = ctx.enter_context(nc.semaphore("x_loaded"))
        out_stored = ctx.enter_context(nc.semaphore("out_stored"))
        retention(nc, d, x, x_loaded)
        experts(nc, d, x, "ffn1", x_sorted, y_sorted, True)
        recurrence(nc, d, x)
        experts(nc, d, x, "ffn2", x_sorted, y_sorted, False)
        with nc.Block() as block:
            @block.sync
            def _(sp):
                sp.dma_start(out, x[:]).then_inc(out_stored, 16)
                sp.wait_ge(out_stored, 16)


def kernel(**inputs):
    import numpy as np
    import concourse.bacc as bacc
    from concourse.bass_utils import run_bass_kernel_spmd

    arrays = {**_laid_out({n: inputs[n] for n in _NAMES}), **_shape_constants(), **_route_constants()}
    nc = bacc.Bacc("TRN2", target_bir_lowering=False, num_devices=1)
    d = {n: nc.dram_tensor("in_" + n, a.shape, F32, kind="ExternalInput").ap() for n, a in arrays.items()}
    out = nc.dram_tensor("out", (P, TILES, C), F32, kind="ExternalOutput").ap()
    program(nc, d, out)
    got = run_bass_kernel_spmd(nc, [{"in_" + n: a for n, a in arrays.items()}], core_ids=[0])
    return np.ascontiguousarray(got.results[0]["out"].transpose(1, 0, 2)).reshape(B, T, C)
```

```python
from contextlib import ExitStack

import concourse.bass as bass
from concourse import mybir

ALU = mybir.AluOpType
ACT = mybir.ActivationFunctionType
F32 = mybir.dt.float32
BF16 = mybir.dt.bfloat16
AX = mybir.AxisListType.X

P = 128
C = 256
KT = C // P
B, T = 4, 1024
TILES = B * T // P
TPB = T // P
NH, HD = 16, 16
HPT = P // HD
EPS = 1e-5
BANK = 512


def moments(dve, stats, scratch, mean, vare, step, first, n):
    even, odd = stats[:, :, 0:3], stats[:, :, 3:6]
    total, apart, squares = scratch[:, 0, :], scratch[:, 1, :], scratch[:, 2, :]
    dve.tensor_tensor(total, even[:, :, 1], odd[:, :, 1], ALU.add).then_inc(step, 1)
    dve.tensor_tensor(apart, even[:, :, 1], odd[:, :, 1], ALU.subtract).then_inc(step, 1)
    dve.tensor_tensor(squares, even[:, :, 2], odd[:, :, 2], ALU.add).then_inc(step, 1)
    dve.wait_ge(step, first + 1)
    dve.tensor_scalar(mean, total, 0.5, None, ALU.mult).then_inc(step, 1)
    dve.wait_ge(step, first + 2)
    dve.tensor_tensor(apart, apart, apart, ALU.mult).then_inc(step, 1)
    dve.wait_ge(step, first + 3)
    dve.tensor_scalar(squares, squares, 1.0 / n, EPS, ALU.mult, ALU.add).then_inc(step, 1)
    dve.wait_ge(step, first + 6)
    dve.scalar_tensor_tensor(vare, apart, 0.25, squares, ALU.mult, ALU.add).then_inc(step, 1)


MOMENT_STEPS = 7


def retention(nc, d, x, x_loaded, x_stats):
    with ExitStack() as ctx:
        def sb(name, shape, dt=F32):
            return ctx.enter_context(nc.sbuf_tensor("ret_" + name, shape, dt))

        def ps(name, shape):
            return ctx.enter_context(nc.psum_tensor("ret_" + name, shape, F32))

        def sem(name):
            return ctx.enter_context(nc.semaphore("ret_" + name))

        w_qk = sb("w_qk", [P, KT, 2 * C])
        w_v = sb("w_v", [P, KT, C])
        w_gate = sb("w_gate", [P, KT, C])
        w_proj = sb("w_proj", [P, KT, C])
        rope_cos = sb("rope_cos", [P, TPB, 2 * C])
        rope_sin = sb("rope_sin", [P, TPB, 2 * C])
        ident = sb("ident", [P, P])
        causal = sb("causal", [P, P])
        head_of = sb("head_of", [P, HPT])
        same_head = sb("same_head", [P, P])
        head_mean = sb("head_mean", [P, P])
        gn_w = sb("gn_w", [P, KT])
        gn_b = sb("gn_b", [P, KT])
        expo = sb("expo", [P, TPB])
        stats = sb("stats", [P, TPB, 6])
        scratch = sb("scratch", [P, 3, TPB])
        mean = sb("mean", [P, TPB])
        vare = sb("vare", [P, TPB])
        rstd = sb("rstd", [P, TPB])
        xn = sb("xn", [P, 2, C])
        xnt = sb("xnt", [P, 2, KT, P])
        roped = sb("roped", [P, 2, 2 * C])
        rope_t1 = sb("rope_t1", [P, 2 * C])
        rope_t2 = sb("rope_t2", [P, 2 * C])
        v = sb("v", [P, 2, C])
        v_heads = sb("v_heads", [P, 2, NH, 2 * HD])
        qkt = sb("qkt", [P, 2, 4, P])
        q_heads = sb("q_heads", [P, NH, P])
        probs = sb("probs", [P, NH, P])
        state = sb("state", [P, KT, P])
        state_add = sb("state_add", [P, KT, P])
        yt = sb("yt", [P, 2, KT, T])
        silu_g = sb("silu_g", [P, 2, KT, T])
        ynorm = sb("ynorm", [P, KT, T])
        gn_stats = sb("gn_stats", [P, KT, 2, 6])
        gn_sum = sb("gn_sum", [P, KT])
        gn_dev = sb("gn_dev", [P, KT, 4])
        gn_dev_sum = sb("gn_dev_sum", [P, KT])
        gn_squares = sb("gn_squares", [P, KT])
        gn_var = sb("gn_var", [P, KT])
        gn_mean = sb("gn_mean", [P, KT])
        gn_vare = sb("gn_vare", [P, KT])
        gn_rstd = sb("gn_rstd", [P, KT])
        gn_scale = sb("gn_scale", [P, KT])
        gn_shift = sb("gn_shift", [P, KT])

        score = ps("score", [P, 2, BANK])
        ps_qk = ps("ps_qk", [P, BANK])
        ps_xv = ps("ps_xv", [P, BANK])
        ps_xt, ps_v = ps_xv[:, 0:C], ps_xv[:, C:2 * C]
        ps_qkt = ps("ps_qkt", [P, BANK])
        ps_ys = ps("ps_ys", [P, BANK])
        ps_y, ps_state = ps_ys[:, 0:C], ps_ys[:, C:2 * C]
        ps_g = ps("ps_g", [P, BANK])
        ps_p = ps("ps_p", [P, BANK])

        first_consts_loaded = sem("first_consts_loaded")
        consts_loaded = sem("consts_loaded")
        zeroed = sem("zeroed")
        ln_stats = sem("ln_stats")
        ln_moments = sem("ln_moments")
        ln_rstd = sem("ln_rstd")
        xn_ready = sem("xn_ready")
        xt_in_psum = sem("xt_in_psum")
        xnt_ready = sem("xnt_ready")
        qk_in_psum = sem("qk_in_psum")
        v_in_psum = sem("v_in_psum")
        v_ready = sem("v_ready")
        rope_parts = sem("rope_parts")
        rope_done = sem("rope_done")
        qkt_in_psum = sem("qkt_in_psum")
        qkt_ready = sem("qkt_ready")
        q_heads_ready = sem("q_heads_ready")
        score_in_psum = sem("score_in_psum")
        probs_ready = sem("probs_ready")
        y_in_psum = sem("y_in_psum")
        yt_ready = sem("yt_ready")
        state_masked = sem("state_masked")
        state_ready = sem("state_ready")
        gate_in_psum = sem("gate_in_psum")
        gate_ready = sem("gate_ready")
        gn_half_stats = sem("gn_half_stats")
        gn_step = sem("gn_step")
        gn_sums = sem("gn_sums")
        gn_root = sem("gn_root")
        ynorm_ready = sem("ynorm_ready")
        out_in_psum = sem("out_in_psum")
        x_added = sem("x_added")
        x_stats_ready = sem("x_stats_ready")

        first_consts = [(ident[:], d["ident"]), (w_qk[:], d["a_w_qk"]), (w_v[:], d["a_w_v"]),
                        (rope_cos[:, 0, :], d["rope_cos"][:, 0, :]), (rope_sin[:, 0, :], d["rope_sin"][:, 0, :]),
                        (head_of[:], d["head_of"]), (w_gate[:], d["a_w_gate"])]
        consts = [(causal[:], d["causal"]), (rope_cos[:, 1:, :], d["rope_cos"][:, 1:, :]),
                  (rope_sin[:, 1:, :], d["rope_sin"][:, 1:, :]), (same_head[:], d["same_head"]),
                  (head_mean[:], d["head_mean"]), (gn_w[:], d["a_gn_w"]), (gn_b[:], d["a_gn_b"]),
                  (w_proj[:], d["a_w_proj"])]
        HALF = T // 2
        PAIRS = TPB // 2
        GN_STEPS = 12

        starts_at_one = [xnt_ready, v_ready, rope_parts, rope_done, qkt_ready, q_heads_ready, gate_ready, yt_ready, state_masked,
                         state_ready, probs_ready, y_in_psum]
        with nc.Block() as block:
            @block.sync
            def _(sp):
                for s in starts_at_one:
                    sp.sem_inc(s, 1)

        with nc.Block() as block:

            @block.sync
            def _(sp):
                for b in range(B):
                    sp.wait_ge(x_loaded, b * 16)
                    sp.dma_start(x[:, b * TPB:(b + 1) * TPB, :], d["x"][:, b * TPB:(b + 1) * TPB, :]) \
                        .then_inc(x_loaded, 16)
                    if b == 0:
                        for tile, array in first_consts:
                            sp.dma_start(tile, array).then_inc(first_consts_loaded, 16)
                        for tile, array in consts:
                            sp.dma_start(tile, array).then_inc(consts_loaded, 16)
                sp.wait_ge(x_loaded, 16 * B)
                sp.wait_ge(first_consts_loaded, 16 * len(first_consts))
                sp.wait_ge(consts_loaded, 16 * len(consts))

            @block.gpsimd
            def _(pool):
                pool.memset(expo[:], -0.5).then_inc(zeroed, 1)
                pool.memset(v_heads[:], 0.0).then_inc(zeroed, 1)
                pool.wait_ge(zeroed, 2)

                def ln_root(b):
                    pool.wait_ge(ln_moments, (b + 1) * MOMENT_STEPS)
                    pool.tensor_tensor(rstd[:], vare[:], expo[:], ALU.pow).then_inc(ln_rstd, 1)

                def sum_rotation(b, c):
                    pool.wait_ge(rope_parts, 1 + (b * TPB + c + 1) * 3)
                    if not (isinstance(b, int) and b == 0 and c < 2):
                        pool.wait_ge(y_in_psum, 1 + b * TPB + c - 1)
                    pool.tensor_tensor(roped[:, c % 2, :], rope_t1[:], rope_t2[:], ALU.add).then_inc(rope_done, 1)

                def sum_state(b, c):
                    pool.wait_ge(state_masked, 1 + b * (TPB - 1) + c + 1)
                    pool.tensor_tensor(state[:], state[:], state_add[:], ALU.add).then_inc(state_ready, 1)

                def gn_inverse_root(b):
                    pool.wait_ge(gn_step, b * GN_STEPS + 9)
                    pool.tensor_tensor(gn_rstd[:], gn_vare[:], expo[:, 0:KT], ALU.pow).then_inc(gn_root, 1)

                def run(b, first, last):
                    for t in range(TPB):
                        if t == TPB - 2 and not last:
                            ln_root(b + 1)
                        sum_rotation(b, t)
                        if t == 0 and not first:
                            sum_state(b - 1, TPB - 2)
                        if t >= 3:
                            sum_state(b, t - 2)
                        if t == 4 and not first:
                            gn_inverse_root(b - 1)

                ln_root(0)
                run(0, True, False)
                with pool.Fori(1, B - 1) as b:
                    run(b, False, False)
                run(B - 1, False, True)
                sum_state(B - 1, TPB - 2)
                gn_inverse_root(B - 1)

            @block.scalar
            def _(act):
                def half_of(tile, b):
                    return tile[:, bass.ds(b & 1, 1), :, :]

                def x_transposed(b, c):
                    act.wait_ge(xt_in_psum, b * TPB + c + 1)
                    act.activation(xnt[:, c % 2, :, :], ps_xt.rearrange("p (k t) -> p k t", k=KT), ACT.Copy) \
                        .then_inc(xnt_ready, 1)

                def y_out(b, c):
                    act.wait_ge(y_in_psum, 1 + b * TPB + c + 1)
                    act.activation(half_of(yt[:, :, :, c * P:(c + 1) * P], b), ps_y.rearrange("p (o k t) -> p o k t", o=1, k=KT),
                                   ACT.Copy).then_inc(yt_ready, 1)

                def v_out(b, c):
                    act.wait_ge(v_in_psum, b * TPB + c + 1)
                    act.activation(v[:, c % 2, :], ps_v, ACT.Copy).then_inc(v_ready, 1)
                    for k in range(KT):
                        pairs = v_heads[:, c % 2, k * HPT:(k + 1) * HPT, :]
                        own = bass.AP(pairs.tensor, pairs.offset, [pairs.ap[0], [4 * HD, HPT // 2], [3 * HD, 2], [1, HD]])
                        act.activation(own, ps_v[:, k * P:(k + 1) * P].rearrange("p (n two e) -> p n two e", two=2, e=HD),
                                       ACT.Copy).then_inc(v_ready, 1)

                def gate_out(b, c):
                    act.wait_ge(gate_in_psum, b * TPB + c + 1)
                    act.activation(half_of(silu_g[:, :, :, c * P:(c + 1) * P], b),
                                   ps_g[:, 0:C].rearrange("p (o k t) -> p o k t", o=1, k=KT), ACT.Silu).then_inc(gate_ready, 1)

                def qk_out(b, c):
                    act.wait_ge(qkt_in_psum, b * TPB + c + 1)
                    act.activation(qkt[:, c % 2, :, :], ps_qkt[:].rearrange("p (j t) -> p j t", j=4),
                                   ACT.Copy).then_inc(qkt_ready, 1)

                def run(b, first, last):
                    for t in range(TPB):
                        x_transposed(b, t)
                        if t >= 2:
                            y_out(b, t - 2)
                        elif not first:
                            y_out(b - 1, TPB + t - 2)
                        v_out(b, t)
                        qk_out(b, t)
                        gate_out(b, t)

                act.wait_ge(zeroed, 2)
                run(0, True, False)
                with act.Fori(1, B - 1) as b:
                    run(b, False, False)
                run(B - 1, False, True)
                for t in range(2):
                    y_out(B - 1, TPB + t - 2)

            @block.tensor
            def _(pe):
                def transpose_x(b, c):
                    pe.wait_ge(xn_ready, b * TPB + c + 1)
                    pe.wait_ge(xnt_ready, 1 + b * TPB + c)
                    pe.wait_ge(v_ready, 1 + (b * TPB + c) * 3)
                    for k in range(KT):
                        mm = pe.transpose(ps_xt[:, k * P:(k + 1) * P], xn[:, c % 2, k * P:(k + 1) * P], ident[:])
                    mm.then_inc(xt_in_psum, 1)

                def project(b, c):
                    pe.wait_ge(xnt_ready, 1 + b * TPB + c + 1)
                    pe.wait_ge(rope_parts, 1 + (b * TPB + c) * 3)
                    for k in range(KT):
                        mm = pe.matmul(ps_qk[:], xnt[:, c % 2, k, :], w_qk[:, k, :], start=(k == 0), stop=(k == KT - 1))
                    mm.then_inc(qk_in_psum, 1)
                    for k in range(KT):
                        mm = pe.matmul(ps_v, xnt[:, c % 2, k, :], w_v[:, k, :], start=(k == 0), stop=(k == KT - 1))
                    mm.then_inc(v_in_psum, 1)

                def gate(b, c):
                    pe.wait_ge(gate_ready, 1 + b * TPB + c)
                    for m in range(KT):
                        for k in range(KT):
                            mm = pe.matmul(ps_g[:, m * P:(m + 1) * P], w_gate[:, k, m * P:(m + 1) * P], xnt[:, c % 2, k, :],
                                           start=(k == 0), stop=(k == KT - 1))
                    mm.then_inc(gate_in_psum, 1)

                def transpose_qk(b, c):
                    pe.wait_ge(rope_done, 1 + b * TPB + c + 1)
                    pe.wait_ge(qkt_ready, 1 + b * TPB + c)
                    pe.wait_ge(q_heads_ready, 1 + (b * TPB + c) * 2)
                    for j in range(4):
                        mm = pe.transpose(ps_qkt[:, j * P:(j + 1) * P], roped[:, c % 2, j * P:(j + 1) * P], ident[:])
                    mm.then_inc(qkt_in_psum, 1)

                def scores(b, c):
                    pe.wait_ge(qkt_ready, 1 + b * TPB + c + 1)
                    for k in range(KT):
                        pe.wait_ge(q_heads_ready, 1 + (b * TPB + c) * 2 + k + 1)
                        for n in range(2):
                            quarter = 2 * k + n
                            if not (isinstance(b, int) and b == 0 and c == 0 and quarter < 2):
                                pe.wait_ge(probs_ready, 1 + (b * TPB + c) * 4 + quarter - 1)
                            pe.matmul(score[:, n, :], qkt[:, c % 2, 2 + k, :],
                                      q_heads[:, 4 * quarter:4 * quarter + 4, :], start=True, stop=True) \
                                .then_inc(score_in_psum, 1)

                def outputs(b, c):
                    pe.wait_ge(yt_ready, 1 + b * TPB + c)
                    pe.wait_ge(state_masked, 1 + b * (TPB - 1) + c)
                    pe.wait_ge(v_ready, 1 + (b * TPB + c + 1) * 3)
                    if c >= 2:
                        pe.wait_ge(state_ready, 1 + b * (TPB - 2) + c - 1)
                    for k in range(KT):
                        y_half = ps_y[:, k * P:(k + 1) * P]
                        if c >= 1:
                            pe.matmul(y_half, state[:, k, :], qkt[:, c % 2, k, :], start=True, stop=False)
                        pe.wait_ge(probs_ready, 1 + (b * TPB + c) * 4 + 2 * k + 2)
                        for h in range(2):
                            for pair in range(HPT // 2):
                                head = k * HPT + 2 * pair + h
                                mm = pe.matmul(ps_y[2 * HD * pair:2 * HD * (pair + 1), k * P:(k + 1) * P],
                                               v_heads[:, c % 2, head, :], probs[:, head, :], start=(h == 0 and c == 0),
                                               stop=(h == 1))
                    for k in range(KT if c < TPB - 1 else 0):
                        mm = pe.matmul(ps_state[:, k * P:(k + 1) * P], roped[:, c % 2, C + k * P:C + (k + 1) * P],
                                       v[:, c % 2, k * P:(k + 1) * P], start=True, stop=True)
                    mm.then_inc(y_in_psum, 1)

                def group_mean(b):
                    pe.wait_ge(gn_step, b * GN_STEPS + 1)
                    if not (isinstance(b, int) and b == 0):
                        pe.wait_ge(x_added, b * PAIRS)
                    pe.matmul(ps_p[:, 0:KT], head_mean[:], gn_sum[:], start=True, stop=True).then_inc(gn_sums, 1)

                def group_variance(b):
                    pe.wait_ge(gn_step, b * GN_STEPS + 8)
                    pe.matmul(ps_p[:, KT:2 * KT], head_mean[:], gn_var[:], start=True, stop=True).then_inc(gn_sums, 1)

                def projection(b, pair):
                    pe.wait_ge(ynorm_ready, (b + 1) * 4)
                    if pair >= 1:
                        pe.wait_ge(x_added, b * PAIRS + pair)
                    for n in range(2):
                        for k in range(KT):
                            mm = pe.matmul(ps_p[:, n * C:(n + 1) * C], ynorm[:, k, (2 * pair + n) * P:(2 * pair + n + 1) * P],
                                           w_proj[:, k, :], start=(k == 0), stop=(k == KT - 1))
                    mm.then_inc(out_in_psum, 1)

                def run(b, first, last):
                    for t in range(TPB):
                        transpose_x(b, t)
                        if t >= 2:
                            outputs(b, t - 2)
                        elif not first:
                            outputs(b - 1, TPB + t - 2)
                        project(b, t)
                        if first and t == TPB - 1:
                            pe.wait_ge(consts_loaded, 16 * len(consts))
                        if not first:
                            if t == 3:
                                group_mean(b - 1)
                            if t == 4:
                                group_variance(b - 1)
                            if t == 6:
                                projection(b - 1, 0)
                            if t == 7:
                                projection(b - 1, 2)
                        if t >= 1:
                            scores(b, t - 1)
                        elif not first:
                            scores(b - 1, TPB - 1)
                        if not first and t == 6:
                            projection(b - 1, 1)
                        if not first and t == 7:
                            projection(b - 1, 3)
                        transpose_qk(b, t)
                        gate(b, t)

                pe.wait_ge(first_consts_loaded, 16 * len(first_consts))
                run(0, True, False)
                with pe.Fori(1, B - 1) as b:
                    run(b, False, False)
                run(B - 1, False, True)
                outputs(B - 1, TPB - 2)
                scores(B - 1, TPB - 1)
                outputs(B - 1, TPB - 1)
                group_mean(B - 1)
                group_variance(B - 1)
                for pair in range(PAIRS):
                    projection(B - 1, pair)

            @block.vector
            def _(dve):
                def half_of(tile, b):
                    return tile[:, bass.ds(b & 1, 1)]

                def ln_statistics(b, tiles):
                    dve.wait_ge(x_loaded, (b + 1) * 16)
                    if not (isinstance(b, int) and b == 0):
                        dve.wait_ge(ln_moments, b * MOMENT_STEPS)
                    for c in tiles:
                        dve.bn_stats(stats[:, c, :], x[:, c:, :][:, bass.ds(b * TPB, 1), :]).then_inc(ln_stats, 1)

                def ln_moments_of(b):
                    dve.wait_ge(ln_stats, (b + 1) * TPB)
                    moments(dve, stats, scratch, mean[:], vare[:], ln_moments, b * MOMENT_STEPS, C)

                def norm(b, c):
                    if c == 0:
                        dve.wait_ge(ln_rstd, b + 1)
                    if not (isinstance(b, int) and b == 0 and c < 2):
                        dve.wait_ge(xt_in_psum, b * TPB + c - 1)
                    dve.tensor_scalar(xn[:, c % 2, :], x[:, c:, :][:, bass.ds(b * TPB, 1), :], mean[:, c:c + 1],
                                      rstd[:, c:c + 1], ALU.subtract, ALU.mult).then_inc(xn_ready, 1)

                def rotate(b, c):
                    dve.wait_ge(qk_in_psum, b * TPB + c + 1)
                    dve.wait_ge(rope_done, 1 + b * TPB + c)
                    pairs = ps_qk[:].rearrange("p (j two) -> p j two", two=2)
                    sin = rope_sin[:, c, :].rearrange("p (j two) -> p j two", two=2)
                    t2 = rope_t2[:].rearrange("p (j two) -> p j two", two=2)
                    dve.tensor_tensor(rope_t1[:], ps_qk[:], rope_cos[:, c, :], ALU.mult).then_inc(rope_parts, 1)
                    for e in range(2):
                        dve.tensor_tensor(t2[:, :, e], pairs[:, :, 1 - e], sin[:, :, e], ALU.mult) \
                            .then_inc(rope_parts, 1)

                def mask(b, c):
                    dve.wait_ge(y_in_psum, 1 + b * TPB + c)
                    for quarter in range(4):
                        dve.wait_ge(score_in_psum, (b * TPB + c) * 4 + quarter + 1)
                        dve.tensor_tensor(probs[:, 4 * quarter:4 * quarter + 4, :],
                                          score[:, quarter % 2, :].rearrange("p (h t) -> p h t", h=4),
                                          causal[:].unsqueeze(1).to_broadcast([P, 4, P]), ALU.mult) \
                            .then_inc(probs_ready, 1)

                def spread_q(b, c):
                    dve.wait_ge(qkt_ready, 1 + b * TPB + c + 1)
                    if not (isinstance(b, int) and b == 0 and c == 0):
                        dve.wait_ge(score_in_psum, (b * TPB + c) * 4)
                    for k in range(KT):
                        dve.tensor_tensor(q_heads[:, k * HPT:(k + 1) * HPT, :],
                                          qkt[:, c % 2, k, :].unsqueeze(1).to_broadcast([P, HPT, P]),
                                          head_of[:].unsqueeze(2).to_broadcast([P, HPT, P]), ALU.mult) \
                            .then_inc(q_heads_ready, 1)

                def add_state(b, c):
                    dve.wait_ge(yt_ready, 1 + b * TPB + c + 1)
                    if c == 0:
                        dve.wait_ge(state_ready, 1 + b * (TPB - 2))
                    if c >= 2:
                        dve.wait_ge(state_ready, 1 + b * (TPB - 2) + c - 1)
                    into = state if c == 0 else state_add
                    dve.tensor_tensor(into[:], ps_state.rearrange("p (k e) -> p k e", k=KT),
                                      same_head[:].unsqueeze(1).to_broadcast([P, KT, P]), ALU.mult) \
                        .then_inc(state_masked, 1)

                parts = gn_stats[:].rearrange("p k n (g s) -> p k (n g) s", s=3)

                def gn_statistics(b):
                    dve.wait_ge(yt_ready, 1 + (b + 1) * TPB)
                    for k in range(KT):
                        for n in range(2):
                            dve.bn_stats(gn_stats[:, k, n, :], half_of(yt[:, :, k, n * HALF:(n + 1) * HALF], b)) \
                                .then_inc(gn_half_stats, 1)
                    dve.wait_ge(gn_half_stats, (b + 1) * 4)
                    dve.tensor_reduce(gn_sum[:], parts[:, :, :, 1], AX, ALU.add).then_inc(gn_step, 1)
                    dve.tensor_reduce(gn_squares[:], parts[:, :, :, 2], AX, ALU.add).then_inc(gn_step, 1)

                def gn_variance(b):
                    dve.wait_ge(gn_sums, b * 2 + 1)
                    dve.tensor_scalar(gn_mean[:], ps_p[:, 0:KT], 0.25, None, ALU.mult).then_inc(gn_step, 1)
                    dve.wait_ge(gn_step, b * GN_STEPS + 3)
                    dve.tensor_tensor(gn_dev[:], parts[:, :, :, 1], gn_mean[:].unsqueeze(2).to_broadcast([P, KT, 4]),
                                      ALU.subtract).then_inc(gn_step, 1)
                    dve.wait_ge(gn_step, b * GN_STEPS + 4)
                    dve.tensor_tensor(gn_dev[:], gn_dev[:], gn_dev[:], ALU.mult).then_inc(gn_step, 1)
                    dve.wait_ge(gn_step, b * GN_STEPS + 5)
                    dve.tensor_reduce(gn_dev_sum[:], gn_dev[:], AX, ALU.add).then_inc(gn_step, 1)
                    dve.tensor_scalar(gn_squares[:], gn_squares[:], 1.0 / T, None, ALU.mult).then_inc(gn_step, 1)
                    dve.wait_ge(gn_step, b * GN_STEPS + 7)
                    dve.scalar_tensor_tensor(gn_var[:], gn_dev_sum[:], 0.25, gn_squares[:], ALU.mult, ALU.add) \
                        .then_inc(gn_step, 1)

                def gn_vare_out(b):
                    dve.wait_ge(gn_sums, b * 2 + 2)
                    dve.tensor_scalar(gn_vare[:], ps_p[:, KT:2 * KT], EPS, None, ALU.add).then_inc(gn_step, 1)

                def normed(b):
                    dve.wait_ge(gn_root, b + 1)
                    dve.tensor_tensor(gn_scale[:], gn_rstd[:], gn_w[:], ALU.mult).then_inc(gn_step, 1)
                    dve.wait_ge(gn_step, b * GN_STEPS + 10)
                    dve.tensor_tensor(gn_shift[:], gn_mean[:], gn_scale[:], ALU.mult).then_inc(gn_step, 1)
                    dve.wait_ge(gn_step, b * GN_STEPS + 11)
                    dve.tensor_tensor(gn_shift[:], gn_b[:], gn_shift[:], ALU.subtract).then_inc(gn_step, 1)
                    dve.wait_ge(gn_step, b * GN_STEPS + 12)
                    for k in range(KT):
                        dve.tensor_scalar(ynorm[:, k, :], half_of(yt[:, :, k, :], b), gn_scale[:, k:k + 1],
                                          gn_shift[:, k:k + 1], ALU.mult, ALU.add).then_inc(ynorm_ready, 1)

                def gated(b):
                    dve.wait_ge(gate_ready, 1 + (b + 1) * TPB)
                    for k in range(KT):
                        dve.wait_ge(ynorm_ready, b * 4 + 1 + k)
                        if k == 1:
                            dve.wait_ge(ynorm_ready, b * 4 + 2)
                        dve.tensor_tensor(ynorm[:, k, :], ynorm[:, k, :], half_of(silu_g[:, :, k, :], b), ALU.mult) \
                            .then_inc(ynorm_ready, 1)

                def add_out(b, pair):
                    dve.wait_ge(out_in_psum, b * PAIRS + pair + 1)
                    two = x[:, 2 * pair:, :][:, bass.ds(b * TPB, 2), :]
                    dve.tensor_tensor(two, two, ps_p[:].rearrange("p (n c) -> p n c", n=2), ALU.add).then_inc(x_added, 1)

                def stats_of_out(b, pair):
                    dve.wait_ge(x_added, b * PAIRS + pair + 1)
                    for n in range(2):
                        def tile(ap):
                            return ap[:, 2 * pair + n:, :][:, bass.ds(b * TPB, 1), :]

                        dve.bn_stats(tile(x_stats), tile(x)).then_inc(x_stats_ready, 1)

                def run(b, first, last):
                    for t in range(TPB):
                        if t >= 2:
                            add_state(b, t - 2)
                        elif t == 0 and not first:
                            add_state(b - 1, TPB - 2)
                        if first and t == 1:
                            dve.wait_ge(consts_loaded, 16 * len(consts))
                        if t + 1 < TPB:
                            norm(b, t + 1)
                        elif not last:
                            norm(b + 1, 0)
                        if t == TPB - 2 and not last:
                            dve.wait_ge(xn_ready, (b + 1) * TPB)
                            ln_moments_of(b + 1)
                        rotate(b, t)
                        if not first and t == 6:
                            add_out(b - 1, 0)
                        if not first and t == 7:
                            add_out(b - 1, 2)
                        if t >= 1:
                            mask(b, t - 1)
                        elif not first:
                            mask(b - 1, TPB - 1)
                        if not first and t == 6:
                            add_out(b - 1, 1)
                        if not first and t == 7:
                            add_out(b - 1, 3)
                        spread_q(b, t)
                        if not first:
                            if t == 2:
                                gn_statistics(b - 1)
                            if t == 3:
                                gn_variance(b - 1)
                            if t == 4:
                                gn_vare_out(b - 1)
                                normed(b - 1)
                            if t == 5:
                                gated(b - 1)
                            if t in (6, 7):
                                for pair in (2 * t - 12, 2 * t - 11):
                                    stats_of_out(b - 1, pair)
                        if t < TPB // 2 and not last:
                            ln_statistics(b + 1, range(2 * t, 2 * t + 2))

                ln_statistics(0, range(TPB))
                ln_moments_of(0)
                norm(0, 0)
                dve.wait_ge(first_consts_loaded, 16 * len(first_consts))
                run(0, True, False)
                with dve.Fori(1, B - 1) as b:
                    run(b, False, False)
                run(B - 1, False, True)
                add_state(B - 1, TPB - 2)
                mask(B - 1, TPB - 1)
                for stage in (gn_statistics, gn_variance, gn_vare_out, normed, gated):
                    stage(B - 1)
                for pair in range(PAIRS):
                    add_out(B - 1, pair)
                    stats_of_out(B - 1, pair)
                dve.wait_ge(x_stats_ready, TILES)


NE = 8
DIGIT = (NE - 1).bit_length()
FF = 256
TOPK = 2
TOKENS = TILES * P
UNROLL = 4
NTILES = -(-(TOPK * TILES + NE - 1) // UNROLL) * UNROLL
LAG = 2
PACKS = LAG + UNROLL + 1
SPILL = TOPK * TOKENS
Y_ROWS = SPILL + NTILES * P


def experts(nc, d, x, ln_stats, name, xn_rows, y_rows, xs_loaded, ys_stored, new_stats=None, out=None):
    with ExitStack() as ctx:
        def sb(n, shape, dt=F32):
            return ctx.enter_context(nc.sbuf_tensor(f"{name}_{n}", shape, dt))

        def ps(n, shape):
            return ctx.enter_context(nc.psum_tensor(f"{name}_{n}", shape, F32))

        semaphores = []

        def sem(n):
            semaphores.append(ctx.enter_context(nc.semaphore(f"{name}_{n}")))
            return semaphores[-1]

        CHOICES = TOPK * TILES
        E_COLUMNS = 2 * FF
        w1 = [[sb(f"w1_{part}{k}", [P, NE * E_COLUMNS]) for k in range(KT)] for part in ("high", "low")]
        w2 = [sb(f"w2_{k}", [P, NE * E_COLUMNS]) for k in range(KT)]
        w_gate = sb("w_gate", [P, KT, 32])
        b_gate = sb("b_gate", [P, NE])
        ident = sb("ident", [P, P])
        tri_f = sb("tri_f", [P, P])
        tri = sb("tri", [P, P], BF16)
        ones = sb("ones", [P, P], BF16)
        ones_row = sb("ones_row", [P, TILES])
        rank_of = sb("rank_of", [P, NE])
        fills = sb("fills", [P, TILES])
        count_f = sb("count_f", [P, P])
        count = sb("count", [P, P], BF16)
        part_no = sb("part_no", [P, 1])
        spill = sb("spill", [P, NTILES])
        expo = sb("expo", [P, TILES])

        scratch = sb("scratch", [P, 3, TILES])
        mean = sb("mean", [P, TILES])
        vare = sb("vare", [P, TILES])
        rstd = sb("rstd", [P, TILES])
        logits = sb("logits", [P, TILES, NE])
        first = sb("first", [P, TILES, NE])
        second = sb("second", [P, TILES, NE])
        hits = sb("hits", [P, TILES, NE])
        rest = sb("rest", [P, TILES, NE])
        top = sb("top", [P, TOPK, TILES])
        best = sb("best", [P, TOPK, TILES])
        gap = sb("gap", [P, TILES])
        odds = sb("odds", [P, TILES])
        total = sb("total", [P, TILES])
        weight = sb("weight", [P, TOPK, TILES])
        chosen = sb("chosen", [P, TILES, NE], BF16)
        running = sb("running", [P, TILES, NE])
        slot = sb("slot", [P, TILES, NE])
        over = sb("over", [P, NE, TILES])
        tiles_of = sb("tiles_of", [P, NE])
        tiles_end = sb("tiles_end", [P, NE])
        row_of = sb("row_of", [P, NE])
        place = sb("place", [P, CHOICES])
        place_i = sb("place_i", [P, CHOICES], mybir.dt.int32)
        in_tile_i = sb("in_tile_i", [P, CHOICES], mybir.dt.int32)
        in_tile = sb("in_tile", [P, CHOICES], BF16)
        tile_row = sb("tile_row", [P, CHOICES])
        tile_of = sb("tile_of", [P, CHOICES], BF16)
        choice = sb("choice", [P, NTILES])
        choice_at = sb("choice_at", [P, NTILES])
        second_at = sb("second_at", [P, NTILES])
        spill_at = sb("spill_at", [P, NTILES])
        from_row = sb("from_row", [P, NTILES], mybir.dt.uint32)
        to_row = sb("to_row", [P, NTILES], mybir.dt.uint32)
        passed = sb("passed", [P, NTILES, NE])
        expert_f = sb("expert_f", [P, LAG + NTILES + 1])
        experts_f = sb("experts_f", [P, NTILES // UNROLL])
        experts_of = sb("experts_of", [P, NTILES // UNROLL], mybir.dt.int32)

        with ExitStack() as stage:
            def stage_sb(n, shape, dt=F32):
                return stage.enter_context(nc.sbuf_tensor(f"{name}_{n}", shape, dt))

            xn = stage_sb("xn", [P, 4, UNROLL, C])
            xnt = stage_sb("xnt", [P, 4, KT, UNROLL * P])
            logits_t = stage_sb("logits_t", [P, UNROLL * P])
        with ExitStack() as stage:
            at_row = stage_sb("at_row", [P, CHOICES, P], BF16)
            number = stage_sb("number", [P, CHOICES, 2, NTILES], BF16)
        xs = sb("xs", [P, UNROLL, C])
        xst = sb("xst", [P, 2, 2, KT, P])
        silu_g = sb("silu_g", [P, 2, FF])
        act_in = sb("act_in", [P, 2, FF])
        act_t = sb("act_t", [P, 2, 2, KT, P])
        ys = sb("ys", [P, UNROLL, C])
        back = sb("back", [P, 4, TOPK, UNROLL, C])

        ps_t = ps("ps_t", [P, KT, BANK])
        ps_l = ps("ps_l", [P, BANK])
        ps_h = ps("ps_h", [P, 2, BANK])
        ps_a = ps("ps_a", [P, BANK])
        ps_o = ps("ps_o", [P, 2, BANK])
        ps_xt = [ps_t, ps_h]

        weights_loaded = [sem(f"weights_loaded{n}") for n in range(2 * KT)]
        first_high = sem("first_high")
        other_high = sem("other_high")
        first_split = sem("first_split")
        second_split = sem("second_split")
        ident_loaded = sem("ident_loaded")
        consts_loaded = sem("consts_loaded")
        constants_ready = sem("constants_ready")
        casts_ready = sem("casts_ready")
        ln_moments = sem("ln_moments")
        ln_rstd = sem("ln_rstd")
        xn_ready = sem("xn_ready")
        xn_stored = [sem(f"xn_stored{h}") for h in range(4)]
        xt_in_psum = sem("xt_in_psum")
        xnt_ready = sem("xnt_ready")
        logits_t_in_psum = sem("logits_t_in_psum")
        logits_t_ready = sem("logits_t_ready")
        logits_in_psum = sem("logits_in_psum")
        logits_ready = sem("logits_ready")
        route_step = sem("route_step")
        odds_ready = sem("odds_ready")
        counts_in_psum = sem("counts_in_psum")
        tiles_marked = sem("tiles_marked")
        rows_marked = sem("rows_marked")
        partition_numbers = sem("partition_numbers")
        choice_numbers = sem("choice_numbers")
        choices_in_psum = sem("choices_in_psum")
        packing = sem("packing")
        xst_in_psum = sem("xst_in_psum")
        xst_high = sem("xst_high")
        xst_ready = sem("xst_ready")
        h_in_psum = sem("h_in_psum")
        silu_ready = sem("silu_ready")
        act_ready = sem("act_ready")
        act_t_in_psum = sem("act_t_in_psum")
        act_t_high = sem("act_t_high")
        act_t_ready = sem("act_t_ready")
        y_in_psum = sem("y_in_psum")
        y_half_out = sem("y_half_out")
        ys_ready = sem("ys_ready")
        back_loaded = [sem(f"back_loaded{h}") for h in range(4)]
        x_added = sem("x_added")
        pool_x_added = sem("pool_x_added")
        weighted = sem("weighted")
        out_stored = sem("out_stored")
        new_stats_ready = sem("new_stats_ready")

        weights = [(*(w1[part][k][:].rearrange("p (e c) -> p e c", e=NE) for part in range(2)), d["f_w1"][:, :, k, :])
                   for k in range(KT)] + \
                  [(*(w2[k][:].rearrange("p (e s c) -> p e s c", e=NE, s=2)[:, :, part, :] for part in range(2)),
                    d["f_w2"][:, :, k, :]) for k in range(KT)]

        def one_pass(ap):
            return ap.bitcast(mybir.dt.float32r)

        consts = [(w_gate, "f_w_gate"), (b_gate, "f_b_gate"), (tri_f, "tri"),
                  (rank_of, "rank_of"), (fills, "fills"), (count_f, "count"), (part_no, "part_no"), (spill, "spill")]
        act_t_in_bank = ps_a[:, 0:C].rearrange("p (k t) -> p k t", k=KT)

        def xt_in_bank(u):
            return ps_t[:, u % 2, 0:C].rearrange("p (k t) -> p k t", k=KT)

        STEPS = TILES // UNROLL
        ROUNDS = STEPS // 4
        TURNS = NTILES // UNROLL
        GROUPS = 4
        GROUP = CHOICES // GROUPS

        (TOP1, EQ1, RANK1, BEST1, FIRST, REST, TOP2, EQ2, RANK2, BEST2, SECOND, GAP, CHOSEN,
         RUN, EXCL, SLOT, OVER, TILES_OF, TILES_END, ROW, SHIFT, PLACED, HIT1, POS1, HIT2, POS2,
         INTEGER, MASKED, IN_TILE, TILE_ROW, TILE_OF, HUNDREDS, CHOICE, SECOND_AT, SPILL_AT, CHOICE_AT, FROM_ROW, TO_ROW,
         SUM, SHARE, SHARE2, PASSED, EXPERT, CLAMP, EXPERTS_OF) = range(1, 46)

        starts_at_one = [xst_ready, act_ready, act_t_ready, ys_ready]
        with nc.Block() as block:
            @block.gpsimd
            def _(pool):
                for s in semaphores:
                    pool.sem_clear(s)

        with nc.Block() as block:
            @block.sync
            def _(sp):
                for s in starts_at_one:
                    sp.sem_inc(s, 1)

        with nc.Block() as block:

            @block.sync
            def _(sp):
                sp.dma_start(ident[:], d["ident"]).then_inc(ident_loaded, 16)
                for tile, n in consts:
                    sp.dma_start(tile[:], d[n]).then_inc(consts_loaded, 16)
                def load_weights(n):
                    _, low, array = weights[n]
                    sp.dma_start(low[:], array).then_inc(weights_loaded[n], 16)

                for n in range(STEPS):
                    if n == 4:
                        for w in range(KT):
                            load_weights(w)
                    sp.wait_ge(xn_ready, n + 1)
                    sp.dma_start(xn_rows.rearrange("(i p) c -> p i c", p=P)[:, n * UNROLL:(n + 1) * UNROLL, :],
                                 xn[:, n % 4, :, :]).then_inc(xn_stored[n % 4], 16)
                for n in range(KT, len(weights)):
                    load_weights(n)
                for u in range(UNROLL):
                    sp.wait_ge(ys_stored[u], 16 * TURNS)
                def store_out(n):
                    sp.wait_ge(x_added, TOPK * (UNROLL - 1) * (n + 1))
                    sp.wait_ge(pool_x_added, TOPK * (n + 1))
                    if out is not None:
                        tiles = slice(n * UNROLL, (n + 1) * UNROLL)
                        sp.dma_start(out[:, tiles, :], x[:, tiles, :]).then_inc(out_stored, 16)

                for n in range(STEPS):
                    if n >= 4:
                        store_out(n - 4)
                    for s in range(TOPK):
                        sp.dma_start(back[:, n % 4, s, :, :],
                                     y_rows[s * TOKENS:(s + 1) * TOKENS, :].rearrange("(i p) c -> p i c", p=P)
                                     [:, n * UNROLL:(n + 1) * UNROLL, :]).then_inc(back_loaded[n % 4], 16)
                for n in range(STEPS - 4, STEPS):
                    store_out(n)
                if out is not None:
                    sp.wait_ge(out_stored, 16 * STEPS)
                for h in range(4):
                    sp.wait_ge(back_loaded[h], 16 * TOPK * STEPS // 4)
                for loaded in weights_loaded:
                    sp.wait_ge(loaded, 16)

            @block.gpsimd
            def _(pool):
                pool.memset(expo[:], -0.5).then_inc(constants_ready, 1)
                pool.memset(ones[:], 1.0).then_inc(constants_ready, 1)
                pool.memset(ones_row[:], 1.0).then_inc(constants_ready, 1)
                pool.memset(expert_f[:], 0.0).then_inc(constants_ready, 1)
                pool.wait_ge(ln_moments, MOMENT_STEPS)
                pool.wait_ge(constants_ready, 4)
                for g in range(GROUPS):
                    part = slice(g * TILES // GROUPS, (g + 1) * TILES // GROUPS)
                    pool.tensor_tensor(rstd[:, part], vare[:, part], expo[:, part], ALU.pow).then_inc(ln_rstd, 1)
                for n, (high, low, _) in enumerate(weights[:KT]):
                    pool.wait_ge(*((first_high, 1) if n == 0 else (other_high, n)))
                    for e in range(NE):
                        pool.tensor_tensor(one_pass(low[:, e]), low[:, e], high[:, e], ALU.subtract).then_inc(first_split, 1)
                for g in range(GROUPS):
                    group = slice(g * GROUP, (g + 1) * GROUP)
                    pool.wait_ge(casts_ready, 2)
                    pool.wait_ge(partition_numbers, g + 1)
                    pool.tensor_tensor(number[:, group, 1, :], number[:, group, 1, :],
                                       count[:, group].unsqueeze(2).to_broadcast([P, GROUP, NTILES]), ALU.mult) \
                        .then_inc(choice_numbers, 1)
                pool.wait_ge(route_step, TO_ROW)
                for h in range(4):
                    pool.wait_ge(xn_stored[h], 16 * ROUNDS)
                for n in range(NTILES + 2 * UNROLL):
                    if n < NTILES:
                        if n >= UNROLL:
                            pool.wait_ge(xst_in_psum, n - UNROLL + 1)
                        pool.indirect_dma_start(xs[:, n % UNROLL, :], None, xn_rows[:],
                                                bass.IndirectOffsetOnAxis(ap=from_row[:, n:n + 1], axis=0)) \
                            .then_inc(xs_loaded[n % UNROLL], 16)
                    m = n - 2 * UNROLL
                    if m >= 0:
                        pool.wait_ge(ys_ready, 1 + m + 1)
                        pool.indirect_dma_start(y_rows[:], bass.IndirectOffsetOnAxis(ap=to_row[:, m:m + 1], axis=0),
                                                ys[:, m % UNROLL, :], None).then_inc(ys_stored[m % UNROLL], 16)
                for n in range(STEPS):
                    i = n * UNROLL + UNROLL - 1
                    for s in range(TOPK):
                        pool.wait_ge(weighted, n * TOPK + s + 1)
                        if s > 0:
                            pool.wait_ge(pool_x_added, n * TOPK + s)
                        pool.tensor_tensor(x[:, i, :], x[:, i, :], back[:, n % 4, s, UNROLL - 1, :], ALU.add) \
                            .then_inc(pool_x_added, 1)
                pool.wait_ge(pool_x_added, STEPS * TOPK)

            @block.scalar
            def _(act):
                for n in range(STEPS):
                    act.wait_ge(xt_in_psum, n + 1)
                    if n >= 4:
                        act.wait_ge(logits_t_in_psum, n // 4)
                    act.activation(xnt[:, n % 4, :, :], ps_xt[n % 2][:], ACT.Copy).then_inc(xnt_ready, 1)
                    if n % 4 == 3:
                        act.wait_ge(logits_t_in_psum, n // 4 + 1)
                        if n >= 4:
                            act.wait_ge(logits_in_psum, n // 4)
                        act.activation(logits_t[:], ps_l[:], ACT.Copy).then_inc(logits_t_ready, 1)
                for n, (high, low, _) in list(enumerate(weights))[1:]:
                    act.wait_ge(weights_loaded[n], 16)
                    act.activation(one_pass(high[:]), low[:], ACT.Copy).then_inc(other_high, 1)
                act.wait_ge(route_step, GAP)
                act.activation(odds[:], gap[:], ACT.Exp).then_inc(odds_ready, 1)
                for g in range(GROUPS):
                    group = slice(g * GROUP, (g + 1) * GROUP)
                    act.wait_ge(tiles_marked, g + 1)
                    act.activation(number[:, group, 0, :], number[:, group, 1, :], ACT.Copy, scale=part_no[:]) \
                        .then_inc(partition_numbers, 1)

                def silu(n, u):
                    act.wait_ge(h_in_psum, n + 1)
                    act.activation(silu_g[:, u % 2, :], ps_h[:, u % 2, 0:FF], ACT.Silu).then_inc(silu_ready, 1)

                def y_half(n, u):
                    act.wait_ge(y_in_psum, n + 1)
                    if not (isinstance(n, int) and n < UNROLL):
                        act.wait_ge(ys_stored[u], (n - u) * (16 // UNROLL))
                    act.activation(ys[:, u, :], ps_o[:, u % 2, 0:C], ACT.Copy).then_inc(y_half_out, 1)

                def act_high(n, u):
                    act.wait_ge(act_t_in_psum, n + 1)
                    act.activation(one_pass(act_t[:, u % 2, 0]), act_t_in_bank, ACT.Copy).then_inc(act_t_high, 1)

                def x_high(n, u):
                    act.wait_ge(xst_in_psum, n + 1)
                    act.activation(one_pass(xst[:, u % 2, 0]), xt_in_bank(u), ACT.Copy).then_inc(xst_high, 1)

                def turn_of_loop(turn):
                    first, last = (isinstance(turn, int) and turn == t for t in (0, TURNS - 1))
                    for u in range(UNROLL):
                        n = turn * UNROLL + u
                        silu(n, u)
                        if not first or u >= 1:
                            act_high(n - 1, (u - 1) % UNROLL)
                        if not last or u + 2 < UNROLL:
                            x_high(n + 2, (u + 2) % UNROLL)
                        if not first or u >= LAG:
                            y_half(n - LAG, (u - LAG) % UNROLL)

                for n in range(2):
                    x_high(n, n)
                for turn in range(2):
                    turn_of_loop(turn)
                with act.Fori(2, TURNS - 1) as turn:
                    turn_of_loop(turn)
                turn_of_loop(TURNS - 1)
                act_high(NTILES - 1, UNROLL - 1)
                for u in range(UNROLL - LAG, UNROLL):
                    y_half(NTILES - UNROLL + u, u)
                act.wait_ge(route_step, EXPERTS_OF)
                for n in range(STEPS):
                    act.wait_ge(back_loaded[n % 4], (n // 4 + 1) * 16 * TOPK)
                    i = n * UNROLL + UNROLL - 1
                    for s in range(TOPK):
                        returned = back[:, n % 4, s, UNROLL - 1, :]
                        act.activation(returned, returned, ACT.Copy, scale=weight[:, s, i:i + 1]).then_inc(weighted, 1)

            @block.tensor
            def _(pe):
                pe.wait_ge(ident_loaded, 16)

                def transpose_norm(n):
                    pe.wait_ge(xn_ready, n + 1)
                    if n >= 2:
                        pe.wait_ge(xnt_ready, n - 1)
                    for j in range(UNROLL):
                        for k in range(KT):
                            mm = pe.transpose(ps_xt[n % 2][:, k, j * P:(j + 1) * P],
                                              xn[:, n % 4, j, k * P:(k + 1) * P], ident[:])
                    mm.then_inc(xt_in_psum, 1)

                def gate_logits(n):
                    pe.wait_ge(xnt_ready, 4 * n + 4)
                    if n == 0:
                        pe.wait_ge(consts_loaded, 16 * len(consts))
                    if n >= 1:
                        pe.wait_ge(logits_t_ready, n)
                    for k in range(KT):
                        for h in range(4):
                            mm = pe.matmul(ps_l[32 * h:32 * h + 32, :], w_gate[:, k, :], xnt[:, h, k, :],
                                           start=(k == 0), stop=(k == KT - 1))
                    mm.then_inc(logits_t_in_psum, 1)

                def transpose_logits(n):
                    pe.wait_ge(logits_t_ready, n + 1)
                    for j in range(UNROLL):
                        mm = pe.transpose(ps_o[:, n, j * P:(j + 1) * P], logits_t[:, j * P:(j + 1) * P], ident[:])
                    mm.then_inc(logits_in_psum, 1)

                for n in range(STEPS):
                    transpose_norm(n)
                    if n % 4 == 0 and n > 0:
                        gate_logits(n // 4 - 1)
                    if n % 4 == 2 and n > 2:
                        transpose_logits(n // 4 - 1)
                gate_logits(ROUNDS - 1)
                transpose_logits(ROUNDS - 1)
                pe.wait_ge(casts_ready, 2)
                pe.wait_ge(route_step, CHOSEN)
                for n, mask in enumerate((tri, ones)):
                    mm = pe.matmul(ps_a[:, n * TILES * NE:(n + 1) * TILES * NE], mask[:], chosen[:], start=True, stop=True)
                mm.then_inc(counts_in_psum, 1)
                for g in range(GROUPS):
                    pe.wait_ge(rows_marked, g + 1)
                    pe.wait_ge(choice_numbers, g + 1)
                    for i in range(g * GROUP, (g + 1) * GROUP):
                        mm = pe.matmul(ps_o[:, 0, 0:2 * NTILES], at_row[:, i, :], number[:, i, :, :],
                                       start=(i == 0), stop=(i == CHOICES - 1))
                mm.then_inc(choices_in_psum, 1)

                def transpose_x(n, u):
                    pe.wait_ge(xs_loaded[u], (n - u) * (16 // UNROLL) + 16)
                    for k in range(KT):
                        mm = pe.transpose(ps_t[:, u % 2, k * P:(k + 1) * P], xs[:, u, k * P:(k + 1) * P], ident[:])
                    mm.then_inc(xst_in_psum, 1)

                def hidden(n, u, e):
                    pe.wait_ge(xst_ready, 1 + n + 1)
                    for part, w_part in ((0, 0), (1, 0), (0, 1)):
                        for k in range(KT):
                            mm = pe.matmul(ps_h[:, u % 2, :], one_pass(xst[:, u % 2, part, k, :]),
                                           one_pass(w1[w_part][k][:, bass.ds(e, E_COLUMNS)]),
                                           start=(part + w_part + k == 0), stop=(w_part == 1 and k == KT - 1))
                    mm.then_inc(h_in_psum, 1)

                def transpose_act(n, u):
                    pe.wait_ge(act_ready, 1 + n + 1)
                    pe.wait_ge(act_t_ready, 1 + n)
                    for k in range(KT):
                        mm = pe.transpose(ps_a[:, k * P:(k + 1) * P], act_in[:, u % 2, k * P:(k + 1) * P], ident[:])
                    mm.then_inc(act_t_in_psum, 1)

                def output(n, u, e):
                    if not (isinstance(n, int) and n < 2):
                        pe.wait_ge(ys_ready, 1 + n - 1)
                    for k in range(KT):
                        w = w2[k][:, bass.ds(e, E_COLUMNS)]
                        pe.matmul(ps_o[:, u % 2, :], one_pass(act_t[:, u % 2, 0, k, :]), one_pass(w),
                                  start=(k == 0), stop=False)
                        mm = pe.matmul(ps_o[:, u % 2, 0:C], one_pass(act_t[:, u % 2, 1, k, :]), one_pass(w[:, 0:C]),
                                       start=False, stop=(k == KT - 1))
                    mm.then_inc(y_in_psum, 1)

                def experts_at(turn):
                    return pe.value_load(experts_of[0:1, bass.ds(turn, 1)])

                def expert(packed, k):
                    shift = E_COLUMNS.bit_length() - 1 - DIGIT * k
                    moved = packed << shift if shift >= 0 else packed >> -shift
                    return pe.snap(moved & (NE - 1) * E_COLUMNS, min_val=0, max_val=(NE - 1) * E_COLUMNS)

                def turn_of_loop(turn):
                    first, last = (isinstance(turn, int) and turn == t for t in (0, TURNS - 1))
                    packed = experts_at(turn)
                    for u in range(UNROLL):
                        n = turn * UNROLL + u
                        if not first or u >= 1:
                            transpose_act(n - 1, (u - 1) % UNROLL)
                        if not last or u + 2 < UNROLL:
                            transpose_x(n + 2, (u + 2) % UNROLL)
                        if not first or u >= LAG:
                            output(n - LAG, (u - LAG) % UNROLL, expert(packed, u))
                        if not last or u + 1 < UNROLL:
                            hidden(n + 1, (u + 1) % UNROLL, expert(packed, LAG + u + 1))
                    if last:
                        transpose_act(NTILES - 1, UNROLL - 1)
                        for u in range(UNROLL - LAG, UNROLL):
                            pe.wait_ge(act_t_ready, 1 + turn * UNROLL + u + 1)
                            output(turn * UNROLL + u, u, expert(packed, LAG + u))

                pe.wait_ge(first_split, NE * KT)
                pe.wait_ge(second_split, KT)
                pe.wait_ge(route_step, EXPERTS_OF)
                transpose_x(0, 0)
                transpose_x(1, 1)
                hidden(0, 0, expert(experts_at(0), LAG))
                turn_of_loop(0)
                with pe.Fori(1, TURNS - 1) as turn:
                    turn_of_loop(turn)
                turn_of_loop(TURNS - 1)

            @block.vector
            def _(dve):
                def done(op):
                    op.then_inc(route_step, 1)

                def after(step):
                    dve.wait_ge(route_step, step)

                def each(ap):
                    return ap.unsqueeze(2).to_broadcast([P, TILES, NE])

                moments(dve, ln_stats, scratch, mean[:], vare[:], ln_moments, 0, C)
                for n in range(STEPS):
                    dve.wait_ge(ln_rstd, n * GROUPS // STEPS + 1)
                    if n >= 4:
                        dve.wait_ge(xn_stored[n % 4], (n // 4) * 16)
                        dve.wait_ge(xt_in_psum, n - 3)
                    for j in range(UNROLL):
                        i = n * UNROLL + j
                        op = dve.tensor_scalar(xn[:, n % 4, j, :], x[:, i, :], mean[:, i:i + 1], rstd[:, i:i + 1],
                                               ALU.subtract, ALU.mult)
                    op.then_inc(xn_ready, 1)
                dve.wait_ge(consts_loaded, 16 * len(consts))
                dve.tensor_copy(tri[:], tri_f[:]).then_inc(casts_ready, 1)
                dve.tensor_copy(count[:], count_f[:]).then_inc(casts_ready, 1)
                high, low, _ = weights[0]
                dve.wait_ge(weights_loaded[0], 16)
                dve.tensor_copy(one_pass(high[:]), low[:]).then_inc(first_high, 1)

                ranks = rank_of[:].unsqueeze(1).to_broadcast([P, TILES, NE])
                for n in range(ROUNDS):
                    dve.wait_ge(logits_in_psum, n + 1)
                    for h in range(4):
                        i = (4 * n + h) * UNROLL
                        op = dve.tensor_tensor(logits[:, i:i + UNROLL, :],
                                               ps_o[:, n, :].rearrange("p (j r) -> p j r", j=UNROLL)[:, :, 32 * h:32 * h + NE],
                                               b_gate[:].unsqueeze(1).to_broadcast([P, UNROLL, NE]), ALU.add)
                op.then_inc(logits_ready, 1)
                dve.wait_ge(logits_ready, 1)
                done(dve.tensor_reduce(top[:, 0, :], logits[:], AX, ALU.max))
                after(TOP1)
                done(dve.tensor_tensor(hits[:], logits[:], each(top[:, 0, :]), ALU.is_equal))
                after(EQ1)
                done(dve.tensor_tensor(hits[:], hits[:], ranks, ALU.mult))
                after(RANK1)
                done(dve.tensor_reduce(best[:, 0, :], hits[:], AX, ALU.max))
                after(BEST1)
                done(dve.tensor_tensor(first[:], ranks, each(best[:, 0, :]), ALU.is_equal))
                after(FIRST)
                done(dve.scalar_tensor_tensor(rest[:], first[:], -3.0e38, logits[:], ALU.mult, ALU.add))
                after(REST)
                done(dve.tensor_reduce(top[:, 1, :], rest[:], AX, ALU.max))
                after(TOP2)
                done(dve.tensor_tensor(hits[:], rest[:], each(top[:, 1, :]), ALU.is_equal))
                after(EQ2)
                done(dve.tensor_tensor(hits[:], hits[:], ranks, ALU.mult))
                after(RANK2)
                done(dve.tensor_reduce(best[:, 1, :], hits[:], AX, ALU.max))
                after(BEST2)
                done(dve.tensor_tensor(second[:], ranks, each(best[:, 1, :]), ALU.is_equal))
                done(dve.tensor_tensor(gap[:], top[:, 1, :], top[:, 0, :], ALU.subtract))
                after(SECOND)
                done(dve.tensor_tensor(chosen[:], first[:], second[:], ALU.add))
                dve.wait_ge(counts_in_psum, 1)
                before, counts = (ps_a[:, n * TILES * NE:(n + 1) * TILES * NE].rearrange("p (i e) -> p i e", e=NE)
                                  for n in range(2))
                for e in range(NE):
                    op = dve.tensor_tensor_scan(running[:, :, e], ones_row[:], counts[:, :, e], 0.0, ALU.mult, ALU.add)
                done(op)
                after(RUN)
                done(dve.tensor_tensor(slot[:], running[:], counts, ALU.subtract))
                after(EXCL)
                done(dve.tensor_tensor(slot[:], slot[:], before, ALU.add))
                done(dve.tensor_tensor(over[:], running[:, TILES - 1, :].unsqueeze(2).to_broadcast([P, NE, TILES]),
                                       fills[:].unsqueeze(1).to_broadcast([P, NE, TILES]), ALU.is_gt))
                after(OVER)
                done(dve.tensor_reduce(tiles_of[:], over[:], AX, ALU.add))
                after(TILES_OF)
                done(dve.tensor_tensor_scan(tiles_end[:], ones_row[:, 0:NE], tiles_of[:], 0.0, ALU.mult, ALU.add))
                after(TILES_END)
                done(dve.tensor_tensor(row_of[:], tiles_end[:], tiles_of[:], ALU.subtract))
                after(ROW)
                done(dve.tensor_scalar(row_of[:], row_of[:], float(P), None, ALU.mult))
                after(SHIFT)
                done(dve.tensor_tensor(slot[:], slot[:], row_of[:].unsqueeze(1).to_broadcast([P, TILES, NE]), ALU.add))
                after(PLACED)
                done(dve.tensor_tensor(hits[:], slot[:], first[:], ALU.mult))
                after(HIT1)
                done(dve.tensor_reduce(place[:, 0:TILES], hits[:], AX, ALU.add))
                done(dve.tensor_tensor(rest[:], slot[:], second[:], ALU.mult))
                after(HIT2)
                done(dve.tensor_reduce(place[:, TILES:CHOICES], rest[:], AX, ALU.add))
                after(POS2)
                done(dve.tensor_copy(place_i[:], place[:]))
                after(INTEGER)
                done(dve.tensor_scalar(in_tile_i[:], place_i[:], P - 1, None, ALU.bitwise_and))
                after(MASKED)
                done(dve.tensor_copy(in_tile[:], in_tile_i[:]))
                after(IN_TILE)
                done(dve.tensor_tensor(tile_row[:], place[:], in_tile[:], ALU.subtract))
                after(TILE_ROW)
                done(dve.tensor_scalar(tile_of[:], tile_row[:], 1.0 / P, None, ALU.mult))
                after(TILE_OF)
                for h in range(4):
                    dve.wait_ge(xn_stored[h], 16 * ROUNDS)
                for g in range(GROUPS):
                    group = slice(g * GROUP, (g + 1) * GROUP)

                    def over_group(ap, n, dim):
                        return ap.unsqueeze(dim).to_broadcast([P, GROUP, n])

                    dve.tensor_tensor(number[:, group, 1, :], over_group(count[:, 0:NTILES], NTILES, 1),
                                      over_group(tile_of[:, group], NTILES, 2), ALU.is_equal).then_inc(tiles_marked, 1)
                    dve.tensor_tensor(at_row[:, group, :], over_group(count[:], P, 1),
                                      over_group(in_tile[:, group], P, 2), ALU.is_equal).then_inc(rows_marked, 1)
                for n, (high, low, _) in enumerate(weights[KT:]):
                    dve.wait_ge(other_high, KT + n)
                    dve.tensor_tensor(one_pass(low[:]), low[:], high[:], ALU.subtract).then_inc(second_split, 1)
                dve.wait_ge(choices_in_psum, 1)
                done(dve.tensor_scalar(choice_at[:], ps_o[:, 0, NTILES:2 * NTILES], float(P), None, ALU.mult))
                after(HUNDREDS)
                done(dve.tensor_tensor(choice[:], choice_at[:], ps_o[:, 0, 0:NTILES], ALU.add))
                after(CHOICE)
                done(dve.tensor_scalar(second_at[:], choice[:], float(TOKENS), float(TOKENS), ALU.is_gt, ALU.mult))
                done(dve.scalar_tensor_tensor(spill_at[:], choice[:], 0.0, spill[:], ALU.is_equal, ALU.mult))
                done(dve.tensor_scalar(choice_at[:], choice[:], 1.0, 0.0, ALU.subtract, ALU.max))
                after(CHOICE_AT)
                done(dve.tensor_tensor(from_row[:], choice_at[:], second_at[:], ALU.subtract))
                done(dve.tensor_tensor(to_row[:], choice_at[:], spill_at[:], ALU.add))
                dve.wait_ge(odds_ready, 1)
                done(dve.tensor_scalar(total[:], odds[:], 1.0, None, ALU.add))
                after(SUM)
                done(dve.reciprocal(weight[:, 0, :], total[:]))
                after(SHARE)
                done(dve.tensor_tensor(weight[:, 1, :], weight[:, 0, :], odds[:], ALU.mult))
                done(dve.tensor_tensor(passed[:], tiles_end[:].unsqueeze(1).to_broadcast([P, NTILES, NE]),
                                       count_f[:, 0:NTILES].unsqueeze(2).to_broadcast([P, NTILES, NE]), ALU.is_le))
                after(PASSED)
                numbers = expert_f[:, LAG:LAG + NTILES]
                dve.wait_ge(constants_ready, 4)
                done(dve.tensor_reduce(numbers, passed[:], AX, ALU.add))
                after(EXPERT)
                done(dve.tensor_scalar(numbers, numbers, float(NE - 1), None, ALU.min))
                after(CLAMP)
                for n, k in enumerate(reversed(range(PACKS))):
                    digits = expert_f[:, k:k + NTILES - UNROLL + 1:UNROLL]
                    if n == 0:
                        dve.tensor_copy(experts_f[:], digits).then_inc(packing, 1)
                    else:
                        dve.wait_ge(packing, n)
                        dve.scalar_tensor_tensor(experts_f[:], experts_f[:], float(NE), digits, ALU.mult, ALU.add) \
                            .then_inc(packing, 1)
                dve.wait_ge(packing, PACKS)
                done(dve.tensor_copy(experts_of[:], experts_f[:]))

                def gate(n, u):
                    dve.wait_ge(silu_ready, n + 1)
                    dve.tensor_tensor(act_in[:, u % 2, :], silu_g[:, u % 2, :], ps_h[:, u % 2, FF:2 * FF], ALU.mult) \
                        .then_inc(act_ready, 1)

                def act_low(n, u):
                    dve.wait_ge(act_t_high, n + 1)
                    dve.tensor_tensor(one_pass(act_t[:, u % 2, 1]), act_t_in_bank, act_t[:, u % 2, 0], ALU.subtract) \
                        .then_inc(act_t_ready, 1)

                def x_low(n, u):
                    dve.wait_ge(xst_high, n + 1)
                    dve.tensor_tensor(one_pass(xst[:, u % 2, 1]), xt_in_bank(u), xst[:, u % 2, 0], ALU.subtract) \
                        .then_inc(xst_ready, 1)

                def y_out(n, u):
                    dve.wait_ge(y_half_out, n + 1)
                    dve.tensor_tensor(ys[:, u, :], ys[:, u, :], ps_o[:, u % 2, C:2 * C], ALU.add).then_inc(ys_ready, 1)

                def turn_of_loop(turn):
                    first, last = (isinstance(turn, int) and turn == t for t in (0, TURNS - 1))
                    for u in range(UNROLL):
                        n = turn * UNROLL + u
                        gate(n, u)
                        if not first or u >= 1:
                            act_low(n - 1, (u - 1) % UNROLL)
                        if not last or u + 2 < UNROLL:
                            x_low(n + 2, (u + 2) % UNROLL)
                        if not first or u >= LAG:
                            y_out(n - LAG, (u - LAG) % UNROLL)

                for n in range(2):
                    x_low(n, n)
                for turn in range(2):
                    turn_of_loop(turn)
                with dve.Fori(2, TURNS - 1) as turn:
                    turn_of_loop(turn)
                turn_of_loop(TURNS - 1)
                act_low(NTILES - 1, UNROLL - 1)
                for u in range(UNROLL - LAG, UNROLL):
                    y_out(NTILES - UNROLL + u, u)

                def stats_of_out(i):
                    dve.bn_stats(new_stats[:, i, :], x[:, i, :]).then_inc(new_stats_ready, 1)

                for n in range(STEPS):
                    dve.wait_ge(back_loaded[n % 4], (n // 4 + 1) * 16 * TOPK)
                    for s in range(TOPK):
                        for j in range(UNROLL - 1):
                            i = n * UNROLL + j
                            if s > 0:
                                dve.wait_ge(x_added, n * TOPK * (UNROLL - 1) + j + 1)
                            dve.scalar_tensor_tensor(x[:, i, :], back[:, n % 4, s, j, :], weight[:, s, i:i + 1], x[:, i, :],
                                                     ALU.mult, ALU.add).then_inc(x_added, 1)
                    if new_stats is not None:
                        for j in range(UNROLL - 1):
                            dve.wait_ge(x_added, (n * TOPK + TOPK - 1) * (UNROLL - 1) + j + 1)
                            stats_of_out(n * UNROLL + j)
                        if n > 0:
                            dve.wait_ge(pool_x_added, n * TOPK)
                            stats_of_out(n * UNROLL - 1)
                dve.wait_ge(x_added, STEPS * TOPK * (UNROLL - 1))
                if new_stats is not None:
                    dve.wait_ge(pool_x_added, STEPS * TOPK)
                    stats_of_out(TILES - 1)
                    dve.wait_ge(new_stats_ready, TILES)


NMIX = 5
LORA = 32
LORA_D = 64
TC = 512
CT = TC // P
CPB = T // TC
CHUNKS = B * CPB
SCANS = KT * HD
FOURS = SCANS // 4
READS = 8


def recurrence(nc, d, x, x_stats, name="rec"):
    with ExitStack() as ctx:
        def sb(n, shape, dt=F32):
            return ctx.enter_context(nc.sbuf_tensor(f"{name}_{n}", shape, dt))

        def ps(n, shape):
            return ctx.enter_context(nc.psum_tensor(f"{name}_{n}", shape, F32))

        def sem(n):
            return ctx.enter_context(nc.semaphore(f"{name}_{n}"))

        ident = sb("ident", [P, P])
        v_centre = sb("v_centre", [P, P])
        v_mean = sb("v_mean", [P, P])
        k_to_v = sb("k_to_v", [P, P])
        collect = sb("collect", [P, 4, 32])
        spread_f = sb("spread_f", [P, 4, P])
        spread = sb("spread", [P, 4, P], BF16)
        maa_x = sb("maa_x", [P, KT])
        maa = sb("maa", [P, NMIX, KT])
        tm_w1 = sb("tm_w1", [P, KT, NMIX * LORA])
        tm_w2 = sb("tm_w2", [P, NMIX, C])
        decay = sb("decay", [P, KT])
        td_w1 = sb("td_w1", [P, KT, LORA_D])
        td_w2 = sb("td_w2", [P, C])
        bonus = sb("bonus", [P, KT])
        w_of = {f: sb("w_" + f, [P, KT, C]) for f in "kvrgo"}
        ln_w = sb("ln_w", [P, KT])
        ln_b = sb("ln_b", [P, KT])
        eps = sb("eps", [P, 1])
        no_token = sb("no_token", [P, KT, 1])

        scratch = sb("scratch", [P, 3, TILES])
        mean = sb("mean", [P, TILES])
        vare = sb("vare", [P, TILES])
        expo = sb("expo", [P, TILES])
        rstd = sb("rstd", [P, TILES])
        offset = sb("offset", [P, TILES])
        xn = sb("xn", [P, CT, C])
        xnt = sb("xnt", [P, KT, TC + 1])
        sx = sb("sx", [P, KT, TC])
        mixed = sb("mixed", [P, 2, KT, TC])
        hidden = sb("hidden", [P, TC])
        hidden_g = sb("hidden_g", [P, TC])
        hidden_d = sb("hidden_d", [P, TC])
        wt = [sb(f"wt{h}", [P, KT, TC + 1]) for h in range(CPB)]
        kt = [sb(f"kt{h}", [P, KT, TC]) for h in range(CPB)]
        rt = [sb(f"rt{h}", [P, KT, TC]) for h in range(CPB)]
        silu_g = [sb(f"silu_g{h}", [P, KT, TC]) for h in range(CPB)]
        v_rows = [sb(f"v_rows{h}", [P, KT, 4, TC], BF16) for h in range(CPB)]
        vt = sb("vt", [P, KT, TC])
        v_part = [sb(f"v_part{i}", [P, KT, TC], BF16) for i in range(3)]
        v_rest = sb("v_rest", [P, KT, TC])
        rku = sb("rku", [P, KT, TC])
        y_bonus = sb("y_bonus", [P, KT, TC])
        add = [sb(f"add{n}", [P, TC + 1]) for n in range(4)]
        state = [sb(f"state{n}", [P, TC + 1]) for n in range(4)]
        carry = sb("carry", [P, SCANS])
        read = [sb(f"read{n}", [P, TC]) for n in range(READS)]
        y_raw = sb("y_raw", [P, TC])
        square = sb("square", [P, TC])
        log_var = sb("log_var", [P, TC])
        y_rstd = sb("y_rstd", [P, TC])
        gated = sb("gated", [P, KT, TC])

        ps_v = ps("ps_v", [P, 2, BANK])
        ps_y = ps("ps_y", [P, KT, BANK])
        ps_m = ps("ps_m", [P, 4, BANK])

        ident_loaded = sem("ident_loaded")
        loaded = sem("loaded")
        zeroed = sem("zeroed")
        constants_ready = sem("constants_ready")
        first_constants = sem("first_constants")
        ln_moments = sem("ln_moments")
        ln_rstd = sem("ln_rstd")
        xn_ready = sem("xn_ready")
        xt_in_psum = sem("xt_in_psum")
        first_column = sem("first_column")
        xnt_ready = sem("xnt_ready")
        sx_ready = sem("sx_ready")
        mixed_x_ready = sem("mixed_x_ready")
        hidden_in_psum = sem("hidden_in_psum")
        hidden_ready = sem("hidden_ready")
        delta_in_psum = sem("delta_in_psum")
        mix_scaled = sem("mix_scaled")
        mix_ready = sem("mix_ready")
        linear_in_psum = sem("linear_in_psum")
        linear_out = sem("linear_out")
        decay_ready = sem("decay_ready")
        v_split = sem("v_split")
        v_rows_loaded = sem("v_rows_loaded")
        rku_ready = sem("rku_ready")
        bonus_in_psum = sem("bonus_in_psum")
        y_bonus_ready = sem("y_bonus_ready")
        v_in_psum = sem("v_in_psum")
        add_ready = sem("add_ready")
        state_ready = sem("state_ready")
        carried = sem("carried")
        read_ready = sem("read_ready")
        y_in_psum = sem("y_in_psum")
        y_raw_ready = sem("y_raw_ready")
        y_centred = sem("y_centred")
        square_ready = sem("square_ready")
        var_in_psum = sem("var_in_psum")
        log_ready = sem("log_ready")
        y_rstd_ready = sem("y_rstd_ready")
        normed = sem("normed")
        gated_ready = sem("gated_ready")
        out_in_psum = sem("out_in_psum")
        x_added = sem("x_added")
        x_stats_ready = sem("x_stats_ready")

        consts = [(v_centre[:], "v_centre"), (v_mean[:], "v_mean"), (k_to_v[:], "k_to_v"),
                  (collect[:], "collect"), (spread_f[:], "spread"), (maa_x[:], "b_maa_x"), (maa[:], "b_maa"),
                  (tm_w1[:], "b_tm_w1"), (decay[:], "b_decay"), (td_w1[:], "b_td_w1"), (bonus[:], "b_bonus"),
                  (ln_w[:], "b_ln_w"), (ln_b[:], "b_ln_b")] + [(w_of[f][:], "b_w_" + f) for f in "kvrgo"]
        N_CONSTS = len(consts) + NMIX + 1
        N_ZEROED = 12
        W, V, K, R, G = range(NMIX)
        D_HID, D_0, D_1, V_0, V_1, K_0, K_1, R_0, R_1, G_0, G_1 = range(1, 12)
        LINEARS = 11
        PARTS = ["x0", "x1", "var_last", "hid0", "hid1", "out0", "w0", "w1", "out1", "v0", "v1", "d", "k0", "k1",
                 "d0", "d1", "lv0", "lv1", "r0", "r1", "var", "lk0", "lk1", "g0", "g1", "lr0", "lr1", "b0", "b1",
                 "lg0", "lg1"]

        def bank(part):
            return ps_m[:, PARTS.index(part) % 4, :]

        def halves(turns):
            run, loop = turns
            run(-1, 1, False, True, False)
            run(0, 0, True, True, True)
            with loop(0, B - 1) as b:
                run(b, 1, True, True, False)
                run(b + 1, 0, True, True, False)
            run(B - 1, 1, True, False, False)

        with nc.Block() as block:

            @block.sync
            def _(sp):
                sp.dma_start(ident[:], d["ident"]).then_inc(ident_loaded, 16)
                for tile, n in consts:
                    sp.dma_start(tile, d[n]).then_inc(loaded, 16)
                sp.wait_ge(zeroed, 2)
                for f in range(NMIX):
                    row = LORA * f % P
                    sp.dma_start(tm_w2[row:row + LORA, f, :], d["b_tm_w2"][LORA * f:LORA * (f + 1), :]) \
                        .then_inc(loaded, 16)
                sp.dma_start(td_w2[0:LORA_D, :], d["b_td_w2"]).then_inc(loaded, 16)
                sp.wait_ge(zeroed, 4)
                with sp.Fori(0, B) as b:
                    for h in range(CPB):
                        sp.wait_ge(v_split, (b * CPB + h + 1) * 5)
                        for part in range(3):
                            for g in range(4):
                                sp.dma_start(v_rows[h][32 * part:32 * part + 32, :, g, :],
                                             v_part[part][32 * g:32 * g + 32, :, :]).then_inc(v_rows_loaded, 16)
                sp.wait_ge(v_rows_loaded, 16 * 12 * CHUNKS)

            @block.gpsimd
            def _(pool):
                pool.memset(expo[:], -0.5).then_inc(first_constants, 1)
                pool.memset(no_token[:], 0.0).then_inc(first_constants, 1)
                pool.memset(tm_w2[:], 0.0).then_inc(zeroed, 1)
                pool.memset(td_w2[:], 0.0).then_inc(zeroed, 1)

                def ln_roots(chunks):
                    tiles = slice(chunks.start * CT, chunks.stop * CT)
                    pool.tensor_tensor(rstd[:, tiles], vare[:, tiles], expo[:, tiles], ALU.pow).then_inc(ln_rstd, 1)
                    pool.wait_ge(ln_rstd, 1 if chunks.start == 0 else 3)
                    pool.tensor_tensor(offset[:, tiles], mean[:, tiles], rstd[:, tiles], ALU.mult).then_inc(ln_rstd, 1)

                pool.wait_ge(first_constants, 2)
                pool.wait_ge(ln_moments, MOMENT_STEPS + 1)
                ln_roots(range(1))
                for h in range(CPB):
                    pool.memset(v_rows[h][:], 0.0).then_inc(zeroed, 1)
                pool.memset(hidden_g[:], 0.0).then_inc(zeroed, 1)
                pool.memset(hidden_d[:], 0.0).then_inc(zeroed, 1)
                pool.memset(eps[:], EPS).then_inc(zeroed, 1)
                for n in range(4):
                    pool.memset(add[n][:, 0:1], 0.0).then_inc(zeroed, 1)
                for h in range(CPB):
                    op = pool.memset(wt[h][:, :, 0:1], 1.0)
                op.then_inc(zeroed, 1)
                ln_roots(range(1, CHUNKS))

                def mix(nxt, f):
                    for k in range(KT):
                        pool.wait_ge(mix_scaled, nxt * NMIX * KT + f * KT + k + 1)
                        pool.tensor_tensor(mixed[:, f % 2, k, :], mixed[:, f % 2, k, :], xnt[:, k, 1:TC + 1], ALU.add) \
                            .then_inc(mix_ready, 1)

                def run(batch, h, scan, maps, first):
                    c = batch * CPB + h
                    for m in range(SCANS):
                        if scan:
                            pool.wait_ge(state_ready, c * SCANS + m + 1)
                            if m == 0:
                                pool.wait_ge(linear_out, c * LINEARS + R_1)
                            if m >= READS or not first:
                                pool.wait_ge(y_in_psum, c * FOURS + (m - READS) // 4 + 1)
                            pool.tensor_tensor(read[m % READS][:], rt[h][:, m // HD, :], state[m % 4][:, 0:TC], ALU.mult) \
                                .then_inc(read_ready, 1)
                        if maps:
                            if m == 10:
                                mix(c + 1, W)
                            if m == 12:
                                mix(c + 1, V)
                            if m == 14:
                                mix(c + 1, K)
                            if m == 19:
                                mix(c + 1, R)
                            if m == 25:
                                mix(c + 1, G)

                halves((run, pool.Fori))

            @block.scalar
            def _(act):
                def raw(c, k):
                    act.wait_ge(y_in_psum, c * FOURS + (k + 1) * FOURS // KT)
                    if not (isinstance(c, int) and c == 0 and k == 0):
                        act.wait_ge(y_centred, c * KT + k)
                    act.activation(y_raw[:], ps_y[:, k, :], ACT.Copy).then_inc(y_raw_ready, 1)

                def squares(c, k):
                    act.wait_ge(y_centred, c * KT + k + 1)
                    act.activation(square[:], ps_y[:, k, :], ACT.Square).then_inc(square_ready, 1)

                def root(c, k):
                    act.wait_ge(var_in_psum, c * KT + k + 1)
                    act.activation(log_var[:], bank("var" if k == 0 else "var_last"), ACT.Ln, bias=eps[:]) \
                        .then_inc(log_ready, 1)
                    act.wait_ge(log_ready, c * KT + k + 1)
                    if not (isinstance(c, int) and c == 0 and k == 0):
                        act.wait_ge(normed, c * KT + k)
                    act.activation(y_rstd[:], log_var[:], ACT.Exp, scale=-0.5).then_inc(y_rstd_ready, 1)

                def out(nxt, which, tile, part, fn=ACT.Copy, bias=0.0):
                    act.wait_ge(linear_in_psum, nxt * LINEARS + which)
                    act.activation(tile, bank(part), fn, bias=bias).then_inc(linear_out, 1)

                def run(batch, h, scan, maps, first):
                    c = batch * CPB + h
                    q = 1 - h
                    nxt = c + 1
                    for m in range(SCANS):
                        if scan and m == 1 and not first:
                            raw(c - 1, 1)
                        if scan and m == 2 and not first:
                            squares(c - 1, 1)
                        if scan and m == 4 and not first:
                            root(c - 1, 1)
                        if scan and m == 17:
                            raw(c, 0)
                        if scan and m == 18:
                            squares(c, 0)
                        if scan and m == 20:
                            root(c, 0)
                        if not maps:
                            continue
                        if m == 0:
                            act.wait_ge(ln_rstd, 4 if scan else 2)
                            for i in range(CT):
                                def own(ap):
                                    return ap[:, i:][:, bass.ds(nxt * CT, 1)]

                                act.activation(xn[:, i, :], x[:, i:, :][:, bass.ds(nxt * CT, 1), :], ACT.Identity,
                                               bias=own(offset), scale=own(rstd)).then_inc(xn_ready, 1)
                        if m == 2:
                            last = xnt[:, :, TC:TC + 1] if q == 1 else no_token[:]
                            if not scan:
                                act.wait_ge(first_constants, 2)
                            act.wait_ge(xt_in_psum, nxt * 2 + 1)
                            act.activation(xnt[:, :, 0:1], last, ACT.Copy).then_inc(first_column, 1)
                            act.wait_ge(first_column, nxt + 1)
                            for i in range(2):
                                act.wait_ge(xt_in_psum, nxt * 2 + i + 1)
                                act.activation(xnt[:, :, 1 + i * C:1 + (i + 1) * C],
                                               bank(f"x{i}").rearrange("p (k t) -> p k t", k=KT), ACT.Copy) \
                                    .then_inc(xnt_ready, 1)
                        if m == 6:
                            act.wait_ge(hidden_in_psum, nxt * 2 + 1)
                            act.activation(hidden[:], bank("hid0"), ACT.Tanh).then_inc(hidden_ready, 1)
                        if m == 7:
                            if not scan:
                                act.wait_ge(zeroed, N_ZEROED)
                            act.wait_ge(hidden_in_psum, nxt * 2 + 2)
                            act.activation(hidden_g[0:LORA, :], bank("hid1")[0:LORA, :], ACT.Tanh).then_inc(hidden_ready, 1)
                        if m == 12:
                            act.wait_ge(linear_in_psum, nxt * LINEARS + D_HID)
                            act.activation(hidden_d[0:LORA_D, :], bank("d")[0:LORA_D, :], ACT.Tanh).then_inc(linear_out, 1)
                        if m == 14:
                            for k in range(KT):
                                out(nxt, D_0 + k, wt[q][:, k, 1:TC + 1], f"d{k}", ACT.Exp, decay[:, k:k + 1])
                        if m == 15:
                            act.wait_ge(linear_out, nxt * LINEARS + D_1)
                            act.activation(wt[q][:, :, 1:TC + 1], wt[q][:, :, 1:TC + 1], ACT.Exp, scale=-1.0) \
                                .then_inc(decay_ready, 1)
                        if m == 8 and not scan:
                            act.wait_ge(loaded, 16 * N_CONSTS)
                            act.activation(spread[:], spread_f[:], ACT.Copy).then_inc(constants_ready, 1)
                        if m in (15, 16):
                            out(nxt, V_0 + m - 15, vt[:, m - 15, :], f"lv{m - 15}")
                        if m == 17:
                            if not (isinstance(nxt, int) and nxt == 0):
                                act.wait_ge(v_rows_loaded, nxt * 16 * 12)
                            act.wait_ge(linear_out, nxt * LINEARS + V_1)
                            act.activation(v_part[0][:], vt[:], ACT.Copy).then_inc(v_split, 1)
                        if m == 21:
                            act.wait_ge(v_split, nxt * 5 + 2)
                            act.activation(v_part[1][:], v_rest[:], ACT.Copy).then_inc(v_split, 1)
                        if m == 23:
                            act.wait_ge(v_split, nxt * 5 + 4)
                            act.activation(v_part[2][:], v_rest[:], ACT.Copy).then_inc(v_split, 1)
                        if m in (21, 22):
                            out(nxt, K_0 + m - 21, kt[q][:, m - 21, :], f"lk{m - 21}")
                        if m in (24, 26):
                            k = (m - 24) // 2
                            out(nxt, R_0 + k, rt[q][:, k, :], f"lr{k}")
                        if m in (30, 31):
                            out(nxt, G_0 + m - 30, silu_g[q][:, m - 30, :], f"lg{m - 30}", ACT.Silu)
                        if scan and h == 0:
                            act.wait_ge(state_ready, c * SCANS + m + 1)
                            act.activation(carry[:, m:m + 1], state[m % 4][:, TC:TC + 1], ACT.Copy).then_inc(carried, 1)

                halves((run, act.Fori))
                raw(CHUNKS - 1, 1)
                squares(CHUNKS - 1, 1)
                root(CHUNKS - 1, 1)

            @block.tensor
            def _(pe):
                pe.wait_ge(ident_loaded, 16)

                def spread_v(c, h, m, first):
                    if m == 0:
                        pe.wait_ge(v_rows_loaded, (c + 1) * 16 * 12)
                    if m >= 2 or not first:
                        pe.wait_ge(add_ready, c * SCANS + m - 1)
                    pe.matmul(ps_v[:, m % 2, :], spread[:, m % HD // 4, :], v_rows[h][:, m // HD, m % 4, :],
                              start=True, stop=True).then_inc(v_in_psum, 1)

                def sum_keys(c, four):
                    pe.wait_ge(read_ready, c * SCANS + 4 * four + 4)
                    for quarter in range(4):
                        mm = pe.matmul(ps_y[32 * quarter:32 * quarter + 32, 4 * four // HD, :], collect[:, four % 4, :],
                                       read[(4 * four + quarter) % READS][:], start=False, stop=(four % 4 == 3))
                    mm.then_inc(y_in_psum, 1)

                def begin_y(c, k, first):
                    pe.wait_ge(y_bonus_ready, c * KT + k + 1)
                    if not first:
                        pe.wait_ge(normed, (c - 1) * KT + k + 1)
                    pe.matmul(ps_y[:, k, :], ident[:], y_bonus[:, k, :], start=True, stop=False)

                def centre(c, k):
                    pe.wait_ge(y_raw_ready, c * KT + k + 1)
                    pe.matmul(ps_y[:, k, :], v_centre[:], y_raw[:], start=True, stop=True).then_inc(y_centred, 1)

                def variance(c, k):
                    pe.wait_ge(square_ready, c * KT + k + 1)
                    pe.matmul(bank("var" if k == 0 else "var_last"), v_mean[:], square[:], start=True, stop=True) \
                        .then_inc(var_in_psum, 1)

                def output(c, i):
                    pe.wait_ge(gated_ready, (c + 1) * KT)
                    for t in range(2):
                        for k in range(KT):
                            mm = pe.matmul(bank(f"out{i}")[:, t * C:(t + 1) * C],
                                           gated[:, k, (2 * i + t) * P:(2 * i + t + 1) * P], w_of["o"][:, k, :],
                                           start=(k == 0), stop=(k == KT - 1))
                    mm.then_inc(out_in_psum, 1)

                def delta(nxt, f, part, left, count):
                    for k in range(KT):
                        pe.wait_ge(left[k], count[k])
                        pe.matmul(bank(f"{part}{k}"), tm_w2[:, f, k * P:(k + 1) * P], (hidden if f < G else hidden_g)[:],
                                  start=True, stop=True).then_inc(delta_in_psum, 1)

                def linear(nxt, w, src, part, m0, m1, signal):
                    for k in range(KT):
                        mm = pe.matmul(bank(part)[0:m1 - m0, :], w[:, k, m0:m1], src[:, k, :], start=(k == 0),
                                       stop=(k == KT - 1))
                    mm.then_inc(signal, 1)

                def run(batch, h, scan, maps, first):
                    c = batch * CPB + h
                    q = 1 - h
                    nxt = c + 1
                    start = isinstance(nxt, int) and nxt == 0

                    def scaled(n):
                        return nxt * NMIX * KT + n

                    def left(which):
                        return nxt * LINEARS + which

                    for m in range(SCANS):
                        if scan:
                            if m + 2 < SCANS:
                                spread_v(c, h, m + 2, first)
                            if m in (1, HD + 1):
                                begin_y(c, m // HD, first)
                        if maps and m + 2 >= SCANS:
                            if not scan:
                                pe.wait_ge(constants_ready, 1)
                            spread_v(nxt, q, m + 2 - SCANS, start)
                        if scan and not first:
                            if m == 3:
                                pe.wait_ge(linear_out, left(0))
                                variance(c - 1, 1)
                            if m == 8:
                                if maps:
                                    pe.wait_ge(xnt_ready, nxt * 2 + 2)
                                else:
                                    pe.wait_ge(linear_out, left(0) - 1)
                                output(c - 1, 0)
                            if m == 10:
                                if maps:
                                    pe.wait_ge(hidden_ready, nxt * 2 + 2)
                                else:
                                    pe.wait_ge(y_bonus_ready, nxt * KT)
                                output(c - 1, 1)
                        if scan and m == 20:
                            if maps:
                                pe.wait_ge(linear_out, left(V_0))
                            else:
                                pe.wait_ge(x_added, c * 2)
                            variance(c, 0)
                        if maps:
                            if m == 2:
                                for i in range(2):
                                    pe.wait_ge(xn_ready, nxt * CT + 2 * (i + 1))
                                    if not start:
                                        if i == 0:
                                            pe.wait_ge(y_bonus_ready, nxt * KT)
                                        else:
                                            pe.wait_ge(linear_out, left(0) - 1)
                                    for t in range(2):
                                        for k in range(KT):
                                            mm = pe.transpose(bank(f"x{i}")[:, k * C + t * P:k * C + (t + 1) * P],
                                                              xn[:, 2 * i + t, k * P:(k + 1) * P], ident[:])
                                    mm.then_inc(xt_in_psum, 1)
                            if m == 3 and not scan:
                                pe.wait_ge(loaded, 16 * N_CONSTS)
                            if m == 6:
                                pe.wait_ge(mixed_x_ready, nxt * KT + KT)
                                if not start:
                                    pe.wait_ge(y_bonus_ready, nxt * KT - 1)
                                linear(nxt, tm_w1, mixed[:, 0], "hid0", 0, P, hidden_in_psum)
                            if m == 7:
                                pe.wait_ge(xnt_ready, nxt * 2 + 1)
                                linear(nxt, tm_w1, mixed[:, 0], "hid1", P, P + LORA, hidden_in_psum)
                            if m == 9:
                                pe.wait_ge(hidden_ready, nxt * 2 + 1)
                                if scan and not first:
                                    pe.wait_ge(y_rstd_ready, c * KT)
                                elif scan:
                                    pe.wait_ge(linear_out, left(0))
                                delta(nxt, W, "w", (hidden_ready, hidden_ready), (nxt * 2 + 1, nxt * 2 + 1))
                            if m == 11:
                                if scan and not first:
                                    pe.wait_ge(x_added, c * 2 - 1)
                                delta(nxt, V, "v", (xnt_ready, mix_scaled), (nxt * 2 + 2, scaled(1)))
                            if m == 12:
                                pe.wait_ge(mix_ready, scaled((W + 1) * KT))
                                linear(nxt, td_w1, mixed[:, W % 2], "d", 0, LORA_D, linear_in_psum)
                            if m == 13:
                                if scan and not first:
                                    pe.wait_ge(x_added, c * 2)
                                delta(nxt, K, "k", (hidden_ready, mix_scaled), (nxt * 2 + 2, scaled(3)))
                            if m == 14:
                                pe.wait_ge(mix_scaled, scaled(4))
                                pe.wait_ge(linear_out, left(D_HID))
                                for k in range(KT):
                                    pe.matmul(bank(f"d{k}"), td_w2[:, k * P:(k + 1) * P], hidden_d[:], start=True,
                                              stop=True).then_inc(linear_in_psum, 1)
                            if m in (15, 16):
                                k = m - 15
                                pe.wait_ge(mix_ready, scaled((V + 1) * KT))
                                pe.wait_ge(mix_scaled, scaled(5 + k))
                                linear(nxt, w_of["v"], mixed[:, V % 2], f"lv{k}", k * P, (k + 1) * P, linear_in_psum)
                            if m == 18:
                                delta(nxt, R, "r", (linear_out, linear_out), (left(D_0), left(D_1)))
                            if m in (21, 22):
                                k = m - 21
                                pe.wait_ge(mix_ready, scaled((K + 1) * KT))
                                if k == 0:
                                    pe.wait_ge(linear_out, left(V_1))
                                else:
                                    pe.wait_ge(mix_scaled, scaled(7))
                                linear(nxt, w_of["k"], mixed[:, K % 2], f"lk{k}", k * P, (k + 1) * P, linear_in_psum)
                            if m == 23:
                                if scan:
                                    pe.wait_ge(y_rstd_ready, c * KT + 1)
                                delta(nxt, G, "g", (mix_scaled, linear_out), (scaled(8), left(V_0)))
                            if m in (24, 26):
                                k = (m - 24) // 2
                                pe.wait_ge(mix_ready, scaled((R + 1) * KT))
                                pe.wait_ge(linear_out, left(K_0 + k))
                                linear(nxt, w_of["r"], mixed[:, R % 2], f"lr{k}", k * P, (k + 1) * P, linear_in_psum)
                            if m == 28:
                                for k in range(KT):
                                    pe.wait_ge(rku_ready, nxt * KT + k + 1)
                                    pe.wait_ge(mix_scaled, scaled(9 + k))
                                    pe.matmul(bank(f"b{k}"), k_to_v[:], rku[:, k, :], start=True, stop=True) \
                                        .then_inc(bonus_in_psum, 1)
                            if m in (30, 31):
                                k = m - 30
                                pe.wait_ge(mix_ready, scaled((G + 1) * KT))
                                pe.wait_ge(linear_out, left(R_0 + k))
                                linear(nxt, w_of["g"], mixed[:, G % 2], f"lg{k}", k * P, (k + 1) * P, linear_in_psum)
                        if scan and m >= 4 and m % 4 == 1:
                            sum_keys(c, m // 4 - 1)
                        if scan and m == 1 and not first:
                            sum_keys(c - 1, FOURS - 1)
                        if scan and m == 2 and not first:
                            centre(c - 1, 1)
                        if scan and m == 18:
                            centre(c, 0)

                halves((run, pe.Fori))
                sum_keys(CHUNKS - 1, FOURS - 1)
                centre(CHUNKS - 1, 1)
                pe.wait_ge(y_rstd_ready, CHUNKS * KT - 1)
                variance(CHUNKS - 1, 1)
                for i in range(2):
                    pe.wait_ge(x_added, (CHUNKS - 1) * 2)
                    output(CHUNKS - 1, i)

            @block.vector
            def _(dve):
                moments(dve, x_stats, scratch, mean[:], vare[:], ln_moments, 0, C)
                dve.wait_ge(ln_moments, MOMENT_STEPS)
                dve.tensor_scalar(mean[:], mean[:], -1.0, None, ALU.mult).then_inc(ln_moments, 1)

                def add_v(c, h, m, first):
                    if m == 0:
                        dve.wait_ge(linear_out, c * LINEARS + K_1)
                    dve.wait_ge(v_in_psum, c * SCANS + m + 1)
                    if m >= 4 or not first:
                        dve.wait_ge(state_ready, c * SCANS + m - 3)
                    dve.tensor_tensor(add[m % 4][:, 1:TC + 1], ps_v[:, m % 2, :], kt[h][:, m // HD, :], ALU.mult) \
                        .then_inc(add_ready, 1)

                def norm_y(c, h, k):
                    dve.wait_ge(y_rstd_ready, c * KT + k + 1)
                    dve.scalar_tensor_tensor(gated[:, k, :], ps_y[:, k, :], ln_w[:, k:k + 1], y_rstd[:], ALU.mult, ALU.mult) \
                        .then_inc(normed, 1)
                    dve.wait_ge(normed, c * KT + k + 1)
                    dve.scalar_tensor_tensor(gated[:, k, :], gated[:, k, :], ln_b[:, k:k + 1], silu_g[h][:, k, :],
                                             ALU.add, ALU.mult).then_inc(gated_ready, 1)

                def add_out(c, i):
                    dve.wait_ge(out_in_psum, c * 2 + i + 1)
                    two = x[:, 2 * i:, :][:, bass.ds(c * CT, 2), :]
                    dve.tensor_tensor(two, two, bank(f"out{i}").rearrange("p (t c) -> p t c", t=2), ALU.add) \
                        .then_inc(x_added, 1)

                def stats_of_out(c, i):
                    dve.wait_ge(x_added, c * 2 + i + 1)
                    for t in range(2):
                        def tile(ap):
                            return ap[:, 2 * i + t:, :][:, bass.ds(c * CT, 1), :]

                        dve.bn_stats(tile(x_stats), tile(x)).then_inc(x_stats_ready, 1)

                def mix(nxt, f, part):
                    if f >= 2:
                        dve.wait_ge(linear_in_psum, nxt * LINEARS + (D_HID, V_1, K_1)[f - 2])
                    for k in range(KT):
                        dve.wait_ge(delta_in_psum, nxt * NMIX * KT + f * KT + k + 1)
                        dve.scalar_tensor_tensor(mixed[:, f % 2, k, :], bank(f"{part}{k}"), maa[:, f, k:k + 1], sx[:, k, :],
                                                 ALU.add, ALU.mult).then_inc(mix_scaled, 1)

                def run(batch, h, scan, maps, first):
                    c = batch * CPB + h
                    q = 1 - h
                    nxt = c + 1
                    for m in range(SCANS):
                        if scan:
                            if m + 1 < SCANS:
                                add_v(c, h, m + 1, first)
                            if m == 0:
                                dve.wait_ge(decay_ready, c + 1)
                            dve.wait_ge(add_ready, c * SCANS + m + 1)
                            if m >= 4 or not first:
                                dve.wait_ge(read_ready, c * SCANS + m - 3)
                            if h == 0 and m >= 4:
                                dve.wait_ge(carried, batch * SCANS + m - 3)
                            if h == 1 and m < 4:
                                dve.wait_ge(carried, (batch + 1) * SCANS)
                            dve.tensor_tensor_scan(state[m % 4][:], wt[h][:, m // HD, :], add[m % 4][:],
                                                   carry[:, m:m + 1] if h == 1 else 0.0, ALU.mult, ALU.add) \
                                .then_inc(state_ready, 1)
                            if m == 6 and not first:
                                norm_y(c - 1, q, 1)
                            if m == 10 and not first:
                                add_out(c - 1, 0)
                            if m == 12 and not first:
                                add_out(c - 1, 1)
                            if m in (13, 15) and not first:
                                stats_of_out(c - 1, (m - 13) // 2)
                            if m == 22:
                                if not first:
                                    dve.wait_ge(out_in_psum, c * 2)
                                norm_y(c, h, 0)
                        if not maps:
                            continue
                        if m == 4:
                            dve.wait_ge(xnt_ready, (nxt + 1) * 2)
                            dve.tensor_tensor(sx[:], xnt[:, :, 0:TC], xnt[:, :, 1:TC + 1], ALU.subtract).then_inc(sx_ready, 1)
                        if m == 5:
                            dve.wait_ge(sx_ready, nxt + 1)
                            if not scan:
                                dve.wait_ge(loaded, 16 * N_CONSTS)
                            if scan:
                                dve.wait_ge(linear_in_psum, nxt * LINEARS)
                            for k in range(KT):
                                dve.scalar_tensor_tensor(mixed[:, 0, k, :], sx[:, k, :], maa_x[:, k:k + 1],
                                                         xnt[:, k, 1:TC + 1], ALU.mult, ALU.add).then_inc(mixed_x_ready, 1)
                        if m == 10:
                            mix(nxt, W, "w")
                        if m == 12:
                            mix(nxt, V, "v")
                        if m == 14:
                            mix(nxt, K, "k")
                        if m == 19:
                            mix(nxt, R, "r")
                        if m in (20, 22):
                            n = (m - 20) // 2
                            dve.wait_ge(v_split, nxt * 5 + 1 + 2 * n)
                            dve.tensor_tensor(v_rest[:], (vt, v_rest)[n][:], v_part[n][:], ALU.subtract).then_inc(v_split, 1)
                        if m == 25:
                            mix(nxt, G, "g")
                        if m == 27:
                            dve.wait_ge(linear_out, nxt * LINEARS + R_1)
                            for k in range(KT):
                                dve.scalar_tensor_tensor(rku[:, k, :], rt[q][:, k, :], bonus[:, k:k + 1], kt[q][:, k, :],
                                                         ALU.mult, ALU.mult).then_inc(rku_ready, 1)
                        if m == 29:
                            for k in range(KT):
                                dve.wait_ge(bonus_in_psum, nxt * KT + k + 1)
                                dve.tensor_tensor(y_bonus[:, k, :], bank(f"b{k}"), vt[:, k, :], ALU.mult) \
                                    .then_inc(y_bonus_ready, 1)
                        if m == SCANS - 1:
                            if not scan:
                                dve.wait_ge(zeroed, N_ZEROED)
                            add_v(nxt, q, 0, not scan)

                halves((run, dve.Fori))
                dve.wait_ge(out_in_psum, (CHUNKS - 1) * 2)
                norm_y(CHUNKS - 1, 1, 1)
                for i in range(2):
                    add_out(CHUNKS - 1, i)
                for i in range(2):
                    stats_of_out(CHUNKS - 1, i)
                dve.wait_ge(x_stats_ready, TILES)


def _shape_constants():
    import numpy as np
    f = np.float32
    half = np.arange(0, HD, 2, dtype=f)
    inv_freq = (f(1.0) / f(10000.0) ** (half / f(HD))).astype(f)
    t = np.arange(T, dtype=f)
    freqs = np.repeat((t[:, None] * inv_freq[None, :]).astype(f), 2, axis=1)
    scale_vec = (half + f(0.4 * HD)) / f(1.4 * HD)
    power = (t - T // 2) / f(512.0)
    scale = np.repeat(scale_vec[None, :].astype(np.float64) ** power[:, None], 2, axis=1)
    cos, sin = np.cos(freqs).astype(np.float64), np.sin(freqs).astype(np.float64)
    sin[:, 0::2] *= -1.0
    gamma = (f(1.0) - f(2.0) ** (f(-5.0) - np.arange(NH, dtype=f))).astype(np.float64)
    decay = gamma[None, :, None] ** np.arange(T, dtype=np.float64)[:, None, None]
    both = []
    for wave in (cos, sin):
        q = decay * (wave * scale)[:, None, :] * HD ** -0.5
        k = (wave / scale)[:, None, :] / decay
        table = np.concatenate([q.reshape(T, C), k.reshape(T, C)], axis=1)
        both.append(np.ascontiguousarray(table.reshape(TPB, P, 2 * C).transpose(1, 0, 2)).astype(f))
    i = np.arange(P)
    head = i // HD
    same = (head[:, None] == head[None, :]).astype(f)
    vrow_v, vrow_h = i // HPT, i % HPT
    vsame = (vrow_h[:, None] == vrow_h[None, :]).astype(f)
    k_to_v = (head[:, None] == vrow_h[None, :]).astype(f)
    collect = np.stack([k_to_v[:, :32] * (vrow_v[:32] == value) for value in range(4)], axis=1).astype(f)
    spread = np.zeros((P, 4, P), f)
    for part in range(3):
        for jj in range(4):
            for h in range(HPT):
                spread[part * 32 + jj * HPT + h, jj, h * HD:(h + 1) * HD] = 1.0
    tri = (i[:, None] < i[None, :]).astype(f)
    return {
        "rope_cos": both[0], "rope_sin": both[1], "ident": np.eye(P, dtype=f),
        "causal": (i[None, :] >= i[:, None]).astype(f),
        "head_of": (head[:, None] == np.arange(HPT)[None, :]).astype(f),
        "same_head": same, "head_mean": (same / f(HD)).astype(f),
        "v_centre": (vsame * (np.eye(P, dtype=f) * 0 + (vrow_v[:, None] == vrow_v[None, :]) - f(1.0 / HD))).astype(f),
        "v_mean": (vsame / f(HD)).astype(f), "k_to_v": k_to_v, "collect": collect, "spread": spread,
        "tri": tri, "ones": np.ones((P, P), f),
    }


def _laid_out(i):
    import numpy as np
    i = {k: np.asarray(v) for k, v in i.items()}

    def rows(w):
        return w.reshape(-1, P, w.shape[1]).transpose(1, 0, 2)

    def column(w):
        return w.reshape(-1, P).T

    def by_value(w, axis):
        s = w.shape
        w = w.reshape(*s[:axis], KT, HPT, HD, *s[axis + 1:])
        return np.swapaxes(w, axis + 1, axis + 2).reshape(s)

    w_qkv = i["L0_attn_a_w_qkv"]
    b = {k.removeprefix("L0_attn_b_"): v for k, v in i.items() if k.startswith("L0_attn_b_")}
    maps = [0, 2, 1, 3, 4]
    w1, w2 = i["L0_ffn_w1"], i["L0_ffn_w2"]
    out = {
        "x": i["L0_attn_a_x"].reshape(TILES, P, C).transpose(1, 0, 2),
        "a_w_qk": rows(w_qkv[:2 * C].T), "a_w_v": rows(w_qkv[2 * C:].T),
        "a_w_gate": rows(i["L0_attn_a_w_gated"].T), "a_w_proj": rows(i["L0_attn_a_w_proj"].T),
        "a_gn_w": column(i["L0_attn_a_gn_weight"]), "a_gn_b": column(i["L0_attn_a_gn_bias"]),
        "f_w_gate": np.tile(rows(i["L0_ffn_Wg"].T), 32 // NE), "f_b_gate": np.broadcast_to(i["L0_ffn_bg"], (P, NE)),
        "f_w1": w1.transpose(2, 0, 1).reshape(KT, P, NE, 2 * FF).transpose(1, 2, 0, 3),
        "f_w2": w2.transpose(2, 0, 1).reshape(FF // P, P, NE, C).transpose(1, 2, 0, 3),
        "b_maa_x": column(b["time_maa_x"]),
        "b_maa": b["time_maa_wkvrg"][maps].reshape(5, KT, P).transpose(2, 0, 1),
        "b_tm_w1": rows(b["tm_w1"].reshape(C, 5, -1)[:, maps].reshape(C, -1)),
        "b_tm_w2": b["tm_w2"][maps].reshape(-1, C),
        "b_decay": column(b["time_decay"]), "b_td_w1": rows(b["td_w1"]), "b_td_w2": b["td_w2"],
        "b_bonus": column(b["time_faaaa"].reshape(-1)),
        "b_w_r": rows(b["Wr"]), "b_w_k": rows(b["Wk"]),
        "b_w_v": rows(by_value(b["Wv"], 1)), "b_w_g": rows(by_value(b["Wg"], 1)),
        "b_w_o": rows(by_value(b["Wo"], 0)),
        "b_ln_w": column(by_value(b["ln_w"], 0)), "b_ln_b": column(by_value(b["ln_b"], 0)),
    }
    return {k: np.ascontiguousarray(v) for k, v in out.items()}


def _route_constants():
    import numpy as np
    f = np.float32
    return {
        "rank_of": np.broadcast_to(NE - np.arange(NE, dtype=f), (P, NE)).copy(),
        "fills": np.broadcast_to(P * np.arange(TILES, dtype=f), (P, TILES)).copy(),
        "count": np.broadcast_to(np.arange(P, dtype=f), (P, P)).copy(),
        "part_no": 1 + np.arange(P, dtype=f)[:, None],
        "spill": (SPILL + np.arange(NTILES, dtype=f)[None, :] * P + np.arange(P, dtype=f)[:, None]).copy(),
    }


_NAMES = ["L0_attn_a_x", "L0_attn_a_w_qkv", "L0_attn_a_w_gated", "L0_attn_a_w_proj", "L0_attn_a_gn_weight",
          "L0_attn_a_gn_bias", "L0_attn_b_time_maa_x", "L0_attn_b_time_maa_wkvrg", "L0_attn_b_tm_w1",
          "L0_attn_b_tm_w2", "L0_attn_b_time_decay", "L0_attn_b_td_w1", "L0_attn_b_td_w2", "L0_attn_b_time_faaaa",
          "L0_attn_b_Wr", "L0_attn_b_Wk", "L0_attn_b_Wv", "L0_attn_b_Wg", "L0_attn_b_Wo", "L0_attn_b_ln_w",
          "L0_attn_b_ln_b", "L0_ffn_Wg", "L0_ffn_bg", "L0_ffn_w1", "L0_ffn_w2"]


def program(nc, d, out):
    xn_rows = nc.dram_tensor("xn_rows", (TOKENS, C), F32, kind="Internal").ap()
    y_rows = nc.dram_tensor("y_rows", (Y_ROWS, C), F32, kind="Internal").ap()
    with ExitStack() as ctx:
        x = ctx.enter_context(nc.sbuf_tensor("x", [P, TILES, C], F32))
        x_loaded = ctx.enter_context(nc.semaphore("x_loaded"))
        moves = {layer: [[ctx.enter_context(nc.semaphore(f"{layer}_{n}{u}")) for u in range(UNROLL)]
                         for n in ("xs_loaded", "ys_stored")] for layer in ("ffn1", "ffn2")}
        x_stats = ctx.enter_context(nc.sbuf_tensor("x_stats", [P, TILES, 6], F32))
        retention(nc, d, x, x_loaded, x_stats)
        experts(nc, d, x, x_stats, "ffn1", xn_rows, y_rows, *moves["ffn1"], new_stats=x_stats)
        recurrence(nc, d, x, x_stats)
        experts(nc, d, x, x_stats, "ffn2", xn_rows, y_rows, *moves["ffn2"], out=out)


def kernel(**inputs):
    import numpy as np
    import concourse.bacc as bacc
    from concourse.bass_utils import run_bass_kernel_spmd

    arrays = {**_laid_out({n: inputs[n] for n in _NAMES}), **_shape_constants(), **_route_constants()}
    nc = bacc.Bacc("TRN2", target_bir_lowering=False, num_devices=1)
    d = {n: nc.dram_tensor("in_" + n, a.shape, F32, kind="ExternalInput").ap() for n, a in arrays.items()}
    out = nc.dram_tensor("out", (P, TILES, C), F32, kind="ExternalOutput").ap()
    program(nc, d, out)
    got = run_bass_kernel_spmd(nc, [{"in_" + n: a for n, a in arrays.items()}], core_ids=[0])
    return np.ascontiguousarray(got.results[0]["out"].transpose(1, 0, 2)).reshape(B, T, C)
```
